# Optimizing a Trainium2 kernel written in Bass

```python
import numpy as np
import jax
import jax.numpy as jnp

def _softmax(x, axis=-1):
    return jax.nn.softmax(x, axis=axis)

def _gelu(x):
    return jax.nn.gelu(x, approximate=True)

def _silu(x):
    return jax.nn.silu(x)

def _sigmoid(x):
    return jax.nn.sigmoid(x)

def _layernorm(x, axis=-1, eps=1e-05):
    m = jnp.mean(x, axis=axis, keepdims=True)
    v = jnp.var(x, axis=axis, keepdims=True)
    return (x - m) / jnp.sqrt(v + eps)

def _scatter_add(tgt, idx, src, axis=0):
    return tgt.at[idx].add(src)

def _segment_sum(src, seg, n):
    return jax.ops.segment_sum(src, seg, n)
kernel_name = 'mk_perceiver_d1_seqx_r2_b34f76'

def setup_inputs(seed: int=0):
    np.random.seed(seed)
    _w = jnp.asarray

    def _rec_inputs():
        import jax
        import jax.numpy as jnp
        _rk = jax.random.key(seed)
        x = -0.0002928 + 1 * jax.random.normal(jax.random.fold_in(_rk, 1), (1, 512, 512), jnp.float32)
        _lenS = 512 - jax.random.randint(jax.random.fold_in(_rk, 7), (1,), 0, max(1, 512 // 4) + 1, jnp.int32)
        _lenS2 = 8192 - jax.random.randint(jax.random.fold_in(_rk, 8), (1,), 0, max(1, 8192 // 4) + 1, jnp.int32)
        _ctx_1024P = jax.random.normal(jax.random.fold_in(_rk, 11), (1, 16, 512), jnp.float32)
        _ctx_1024c = jax.random.dirichlet(jax.random.fold_in(_rk, 511), 0.3 * jnp.ones((16,), jnp.float32), (1, 8192))
        _ctx_1024t = jnp.einsum('bsk,bkd->bsd', _ctx_1024c, _ctx_1024P)
        _ctx_1024t = _ctx_1024t * jax.lax.rsqrt(jnp.mean(jnp.square(_ctx_1024t)) + 1e-12) * 0.953939
        ctx_1024 = -1.52775e-05 + 0.999936 * (_ctx_1024t + 0.3 * jax.random.normal(jax.random.fold_in(_rk, 611), (1, 8192, 512), jnp.float32))
        _validS = jnp.arange(512)[None, :] < _lenS[:, None]
        _validS2 = jnp.arange(8192)[None, :] < _lenS2[:, None]
        _causal = jnp.tril(jnp.ones((512, 512), dtype=bool))
        mask_Bx1xSxS_ik0 = jnp.where(jnp.broadcast_to(_validS[:, None, None, :], (1, 1, 512, 512)), 0, 1).astype(jnp.int32)
        mask_Bx1x1xS2_if1 = jnp.where(jnp.ones((1, 1, 1, 8192), dtype=bool), 1, 0).astype(jnp.int32)
        return (x, ctx_1024, mask_Bx1xSxS_ik0, mask_Bx1x1xS2_if1)
    x, ctx_1024, mask_Bx1xSxS_ik0, mask_Bx1x1xS2_if1 = _rec_inputs()

    def _L0_xattn_setup():
        import jax, jax.numpy as jnp
        import numpy as np
        B, TQ, TK, DM, H, FF, STRIDE = (4, 512, 4096, 512, 16, 2048, 16)
        DH = DM // H
        J = TK // STRIDE
        NEG = -1000000000.0

        def _layer_norm(x, g, b, eps=1e-06):
            m = x.mean(-1, keepdims=True)
            v = ((x - m) ** 2).mean(-1, keepdims=True)
            return g * (x - m) / jnp.sqrt(v + eps) + b

        def _full_attn(q, k, v, mask, wq, bq, wk, bk, wv, bv, wo, bo):
            b_, tq, _ = q.shape
            tk = k.shape[1]
            Q = (q @ wq + bq).reshape(b_, tq, H, DH)
            K = (k @ wk + bk).reshape(b_, tk, H, DH)
            V = (v @ wv + bv).reshape(b_, tk, H, DH)
            scores = jnp.einsum('bqhd,bkhd->bhqk', Q, K) / np.sqrt(DH).astype(np.float32)
            scores = jnp.where(mask == 0, NEG, scores)
            attn = jax.nn.softmax(scores, axis=-1)
            out = jnp.einsum('bhqk,bkhd->bqhd', attn, V).reshape(b_, tq, DM)
            return out @ wo + bo

        def _hepos_attn(q, k, v, src_mask, wq, bq, wk, bk, wv, bv, wo, bo):
            b_, tq, _ = q.shape
            tk = k.shape[1]
            Q = (q @ wq + bq).reshape(b_, tq, H, DH)
            K = (k @ wk + bk).reshape(b_, tk, H, DH)
            V = (v @ wv + bv).reshape(b_, tk, H, DH)
            idx = jnp.arange(H)[:, None] + STRIDE * jnp.arange(J)[None, :]
            hsel = jnp.arange(H)[:, None]
            Kh = K[:, idx, hsel, :]
            Vh = V[:, idx, hsel, :]
            scores = jnp.einsum('bqhd,bhjd->bhqj', Q, Kh) / np.sqrt(DH).astype(np.float32)
            mask_h = src_mask[:, 0, 0, :][:, idx][:, :, None, :]
            scores = jnp.where(mask_h == 0, NEG, scores)
            attn = jax.nn.softmax(scores, axis=-1)
            out = jnp.einsum('bhqj,bhjd->bqhd', attn, Vh).reshape(b_, tq, DM)
            return out @ wo + bo
        key = jax.random.key(seed)
        ks = jax.random.split(key, 16)
        lin = lambda k, din, dout: jax.random.normal(k, (din, dout), jnp.float32) / np.sqrt(din).astype(np.float32)
        inp = {'x': jax.random.normal(ks[0], (B, TQ, DM), jnp.float32), 'enc': jax.random.normal(ks[1], (B, TK, DM), jnp.float32), 'trg_mask': jnp.broadcast_to(jnp.tril(jnp.ones((TQ, TQ), jnp.int32))[None, None], (B, 1, TQ, TQ)), 'src_mask': jnp.ones((B, 1, 1, TK), jnp.int32), 'sa_wq': lin(ks[2], DM, DM), 'sa_bq': jnp.zeros((DM,), jnp.float32), 'sa_wk': lin(ks[3], DM, DM), 'sa_bk': jnp.zeros((DM,), jnp.float32), 'sa_wv': lin(ks[4], DM, DM), 'sa_bv': jnp.zeros((DM,), jnp.float32), 'sa_wo': lin(ks[5], DM, DM), 'sa_bo': jnp.zeros((DM,), jnp.float32), 'ca_wq': lin(ks[6], DM, DM), 'ca_bq': jnp.zeros((DM,), jnp.float32), 'ca_wk': lin(ks[7], DM, DM), 'ca_bk': jnp.zeros((DM,), jnp.float32), 'ca_wv': lin(ks[8], DM, DM), 'ca_bv': jnp.zeros((DM,), jnp.float32), 'ca_wo': lin(ks[9], DM, DM), 'ca_bo': jnp.zeros((DM,), jnp.float32), 'ffn_w1': lin(ks[10], DM, FF), 'ffn_b1': jnp.zeros((FF,), jnp.float32), 'ffn_w2': lin(ks[11], FF, DM), 'ffn_b2': jnp.zeros((DM,), jnp.float32), 'ln1_g': jnp.ones((DM,), jnp.float32), 'ln1_b': jnp.zeros((DM,), jnp.float32), 'ln2_g': jnp.ones((DM,), jnp.float32), 'ln2_b': jnp.zeros((DM,), jnp.float32), 'ln3_g': jnp.ones((DM,), jnp.float32), 'ln3_b': jnp.zeros((DM,), jnp.float32)}
        return inp
    _L0_xattn_all = _L0_xattn_setup()
    _L0_xattn_in = {k: v for k, v in _L0_xattn_all.items() if k in ('sa_wq', 'sa_bq', 'sa_wk', 'sa_bk', 'sa_wv', 'sa_bv', 'sa_wo', 'sa_bo', 'ca_wq', 'ca_bq', 'ca_wk', 'ca_bk', 'ca_wv', 'ca_bv', 'ca_wo', 'ca_bo', 'ffn_w1', 'ffn_b1', 'ffn_w2', 'ffn_b2', 'ln1_g', 'ln1_b', 'ln2_g', 'ln2_b', 'ln3_g', 'ln3_b')}
    del _L0_xattn_all

    def _L0_attn_setup():
        import jax, jax.numpy as jnp
        import numpy as np
        HEADS = 16
        EPS = 1e-08

        def _attention(x, Wq, Wkv, Wo, heads=HEADS, causal=True, eps=EPS):
            B, N, D = x.shape
            dh = D // heads
            q = x @ Wq.T
            k, v = jnp.split(x @ Wkv.T, 2, axis=-1)

            def split_heads(t):
                return t.reshape(B, N, heads, dh).transpose(0, 2, 1, 3)
            q, k, v = map(split_heads, (q, k, v))
            q = q * dh ** (-0.5)
            sim = jnp.einsum('bhid,bhjd->bhij', q, k)
            mask_value = -jnp.finfo(sim.dtype).max
            if causal:
                causal_mask = jnp.triu(jnp.ones((N, N), dtype=bool), 1)
                sim = jnp.where(causal_mask, mask_value, sim)
            m = jax.lax.stop_gradient(jnp.max(sim, axis=-1, keepdims=True))
            e = jnp.exp(sim - m)
            num = jnp.einsum('bhij,bhjd->bhid', e, v)
            den = jnp.sum(e, axis=-1, keepdims=True) + eps
            out = num / den
            out = out.transpose(0, 2, 1, 3).reshape(B, N, D)
            return out @ Wo.T
        key = jax.random.key(seed)
        k0, k1, k2, k3 = jax.random.split(key, 4)
        B, N, D = (2, 1024, 512)
        x = jax.random.normal(k0, (B, N, D), jnp.float32)
        Wq = jax.random.normal(k1, (D, D), jnp.float32) * 0.02
        Wkv = jax.random.normal(k2, (2 * D, D), jnp.float32) * 0.02
        Wo = jax.random.normal(k3, (D, D), jnp.float32) * 0.02
        return {'x': x, 'Wq': Wq, 'Wkv': Wkv, 'Wo': Wo}
    _L0_attn_all = _L0_attn_setup()
    _L0_attn_in = {k: v for k, v in _L0_attn_all.items() if k in ('Wq', 'Wkv', 'Wo')}
    del _L0_attn_all

    def _L0_ffn_setup():
        import jax, jax.numpy as jnp
        import numpy as np
        H, KVH, HD, D = (8, 2, 128, 512)
        E, TOPK, FFN = (8, 2, 1792)
        THETA, EPS = (1000000.0, 1e-05)
        NBITS, GS = (4, 128)
        QMAX = float(2 ** NBITS - 1)
        NEG = -1e+30

        def qgroup(w):
            shp = w.shape
            w2 = w.reshape(-1, GS)
            wmax = jnp.max(w2, -1, keepdims=True)
            wmin = jnp.min(w2, -1, keepdims=True)
            scales = jnp.clip(wmax - wmin, 1e-05, None) / QMAX
            base = jnp.clip(jnp.round(-wmin / scales), 0.0, QMAX)
            wq = (jnp.clip(jnp.round(w2 / scales) + base, 0.0, QMAX) - base) * scales
            return wq.reshape(shp)

        def rms(x, g):
            return x * jax.lax.rsqrt(jnp.mean(x * x, -1, keepdims=True) + EPS) * g

        def rot_half(x):
            h = x.shape[-1] // 2
            return jnp.concatenate([-x[..., h:], x[..., :h]], axis=-1)
        key = jax.random.key(seed)
        ks = jax.random.split(key, 12)
        B, S = (2, 512)
        n = lambda k, s: 0.02 * jax.random.normal(k, s, dtype=jnp.float32)
        return {'hidden_states': jax.random.normal(ks[0], (B, S, D), dtype=jnp.float32), 'w_q': n(ks[1], (H * HD, D)), 'w_k': n(ks[2], (KVH * HD, D)), 'w_v': n(ks[3], (KVH * HD, D)), 'w_o': n(ks[4], (D, H * HD)), 'g1': jnp.ones((D,), jnp.float32), 'g2': jnp.ones((D,), jnp.float32), 'w_gate': n(ks[5], (E, D)), 'w1': n(ks[6], (E, FFN, D)), 'w3': n(ks[7], (E, FFN, D)), 'w2': n(ks[8], (E, D, FFN))}
    _L0_ffn_all = _L0_ffn_setup()
    _L0_ffn_in = {k: v for k, v in _L0_ffn_all.items() if k in ('w_q', 'w_k', 'w_v', 'w_o', 'g1', 'g2', 'w_gate', 'w1', 'w3', 'w2')}
    del _L0_ffn_all
    return {'x': x, 'ctx_1024': ctx_1024, 'mask_Bx1xSxS_ik0': mask_Bx1xSxS_ik0, 'mask_Bx1x1xS2_if1': mask_Bx1x1xS2_if1, 'L0_xattn_sa_wq': _L0_xattn_in['sa_wq'], 'L0_xattn_sa_bq': _L0_xattn_in['sa_bq'], 'L0_xattn_sa_wk': _L0_xattn_in['sa_wk'], 'L0_xattn_sa_bk': _L0_xattn_in['sa_bk'], 'L0_xattn_sa_wv': _L0_xattn_in['sa_wv'], 'L0_xattn_sa_bv': _L0_xattn_in['sa_bv'], 'L0_xattn_sa_wo': _L0_xattn_in['sa_wo'], 'L0_xattn_sa_bo': _L0_xattn_in['sa_bo'], 'L0_xattn_ca_wq': _L0_xattn_in['ca_wq'], 'L0_xattn_ca_bq': _L0_xattn_in['ca_bq'], 'L0_xattn_ca_wk': _L0_xattn_in['ca_wk'], 'L0_xattn_ca_bk': _L0_xattn_in['ca_bk'], 'L0_xattn_ca_wv': _L0_xattn_in['ca_wv'], 'L0_xattn_ca_bv': _L0_xattn_in['ca_bv'], 'L0_xattn_ca_wo': _L0_xattn_in['ca_wo'], 'L0_xattn_ca_bo': _L0_xattn_in['ca_bo'], 'L0_xattn_ffn_w1': _L0_xattn_in['ffn_w1'], 'L0_xattn_ffn_b1': _L0_xattn_in['ffn_b1'], 'L0_xattn_ffn_w2': _L0_xattn_in['ffn_w2'], 'L0_xattn_ffn_b2': _L0_xattn_in['ffn_b2'], 'L0_xattn_ln1_g': _L0_xattn_in['ln1_g'], 'L0_xattn_ln1_b': _L0_xattn_in['ln1_b'], 'L0_xattn_ln2_g': _L0_xattn_in['ln2_g'], 'L0_xattn_ln2_b': _L0_xattn_in['ln2_b'], 'L0_xattn_ln3_g': _L0_xattn_in['ln3_g'], 'L0_xattn_ln3_b': _L0_xattn_in['ln3_b'], 'L0_attn_Wq': _L0_attn_in['Wq'], 'L0_attn_Wkv': _L0_attn_in['Wkv'], 'L0_attn_Wo': _L0_attn_in['Wo'], 'L0_ffn_w_q': _L0_ffn_in['w_q'], 'L0_ffn_w_k': _L0_ffn_in['w_k'], 'L0_ffn_w_v': _L0_ffn_in['w_v'], 'L0_ffn_w_o': _L0_ffn_in['w_o'], 'L0_ffn_g1': _L0_ffn_in['g1'], 'L0_ffn_g2': _L0_ffn_in['g2'], 'L0_ffn_w_gate': _L0_ffn_in['w_gate'], 'L0_ffn_w1': _L0_ffn_in['w1'], 'L0_ffn_w3': _L0_ffn_in['w3'], 'L0_ffn_w2': _L0_ffn_in['w2']}

def reference(x, ctx_1024, mask_Bx1xSxS_ik0, mask_Bx1x1xS2_if1, L0_xattn_sa_wq, L0_xattn_sa_bq, L0_xattn_sa_wk, L0_xattn_sa_bk, L0_xattn_sa_wv, L0_xattn_sa_bv, L0_xattn_sa_wo, L0_xattn_sa_bo, L0_xattn_ca_wq, L0_xattn_ca_bq, L0_xattn_ca_wk, L0_xattn_ca_bk, L0_xattn_ca_wv, L0_xattn_ca_bv, L0_xattn_ca_wo, L0_xattn_ca_bo, L0_xattn_ffn_w1, L0_xattn_ffn_b1, L0_xattn_ffn_w2, L0_xattn_ffn_b2, L0_xattn_ln1_g, L0_xattn_ln1_b, L0_xattn_ln2_g, L0_xattn_ln2_b, L0_xattn_ln3_g, L0_xattn_ln3_b, L0_attn_Wq, L0_attn_Wkv, L0_attn_Wo, L0_ffn_w_q, L0_ffn_w_k, L0_ffn_w_v, L0_ffn_w_o, L0_ffn_g1, L0_ffn_g2, L0_ffn_w_gate, L0_ffn_w1, L0_ffn_w3, L0_ffn_w2):
    import jax
    import jax.numpy as jnp

    def _L0_xattn_ref(x, enc, trg_mask, src_mask, sa_wq, sa_bq, sa_wk, sa_bk, sa_wv, sa_bv, sa_wo, sa_bo, ca_wq, ca_bq, ca_wk, ca_bk, ca_wv, ca_bv, ca_wo, ca_bo, ffn_w1, ffn_b1, ffn_w2, ffn_b2, ln1_g, ln1_b, ln2_g, ln2_b, ln3_g, ln3_b):
        import jax, jax.numpy as jnp
        import numpy as np
        B, TQ, TK, DM, H, FF, STRIDE = (4, 512, 4096, 512, 16, 2048, 16)
        DH = DM // H
        J = TK // STRIDE
        NEG = -1000000000.0

        def _layer_norm(x, g, b, eps=1e-06):
            m = x.mean(-1, keepdims=True)
            v = ((x - m) ** 2).mean(-1, keepdims=True)
            return g * (x - m) / jnp.sqrt(v + eps) + b

        def _full_attn(q, k, v, mask, wq, bq, wk, bk, wv, bv, wo, bo):
            b_, tq, _ = q.shape
            tk = k.shape[1]
            Q = (q @ wq + bq).reshape(b_, tq, H, DH)
            K = (k @ wk + bk).reshape(b_, tk, H, DH)
            V = (v @ wv + bv).reshape(b_, tk, H, DH)
            scores = jnp.einsum('bqhd,bkhd->bhqk', Q, K) / np.sqrt(DH).astype(np.float32)
            scores = jnp.where(mask == 0, NEG, scores)
            attn = jax.nn.softmax(scores, axis=-1)
            out = jnp.einsum('bhqk,bkhd->bqhd', attn, V).reshape(b_, tq, DM)
            return out @ wo + bo

        def _hepos_attn(q, k, v, src_mask, wq, bq, wk, bk, wv, bv, wo, bo):
            b_, tq, _ = q.shape
            tk = k.shape[1]
            Q = (q @ wq + bq).reshape(b_, tq, H, DH)
            K = (k @ wk + bk).reshape(b_, tk, H, DH)
            V = (v @ wv + bv).reshape(b_, tk, H, DH)
            idx = jnp.arange(H)[:, None] + STRIDE * jnp.arange(J)[None, :]
            hsel = jnp.arange(H)[:, None]
            Kh = K[:, idx, hsel, :]
            Vh = V[:, idx, hsel, :]
            scores = jnp.einsum('bqhd,bhjd->bhqj', Q, Kh) / np.sqrt(DH).astype(np.float32)
            mask_h = src_mask[:, 0, 0, :][:, idx][:, :, None, :]
            scores = jnp.where(mask_h == 0, NEG, scores)
            attn = jax.nn.softmax(scores, axis=-1)
            out = jnp.einsum('bhqj,bhjd->bqhd', attn, Vh).reshape(b_, tq, DM)
            return out @ wo + bo
        x = _layer_norm(x + _full_attn(x, x, x, trg_mask, sa_wq, sa_bq, sa_wk, sa_bk, sa_wv, sa_bv, sa_wo, sa_bo), ln1_g, ln1_b)
        x = _layer_norm(x + _hepos_attn(x, enc, enc, src_mask, ca_wq, ca_bq, ca_wk, ca_bk, ca_wv, ca_bv, ca_wo, ca_bo), ln2_g, ln2_b)
        ff = jax.nn.relu(x @ ffn_w1 + ffn_b1) @ ffn_w2 + ffn_b2
        x = _layer_norm(x + ff, ln3_g, ln3_b)
        return x

    def _L0_attn_ref(x, Wq, Wkv, Wo):
        import jax, jax.numpy as jnp
        import numpy as np
        HEADS = 16
        EPS = 1e-08

        def _attention(x, Wq, Wkv, Wo, heads=HEADS, causal=True, eps=EPS):
            B, N, D = x.shape
            dh = D // heads
            q = x @ Wq.T
            k, v = jnp.split(x @ Wkv.T, 2, axis=-1)

            def split_heads(t):
                return t.reshape(B, N, heads, dh).transpose(0, 2, 1, 3)
            q, k, v = map(split_heads, (q, k, v))
            q = q * dh ** (-0.5)
            sim = jnp.einsum('bhid,bhjd->bhij', q, k)
            mask_value = -jnp.finfo(sim.dtype).max
            if causal:
                causal_mask = jnp.triu(jnp.ones((N, N), dtype=bool), 1)
                sim = jnp.where(causal_mask, mask_value, sim)
            m = jax.lax.stop_gradient(jnp.max(sim, axis=-1, keepdims=True))
            e = jnp.exp(sim - m)
            num = jnp.einsum('bhij,bhjd->bhid', e, v)
            den = jnp.sum(e, axis=-1, keepdims=True) + eps
            out = num / den
            out = out.transpose(0, 2, 1, 3).reshape(B, N, D)
            return out @ Wo.T
        return _attention(x, Wq, Wkv, Wo)

    def _L0_ffn_ref(hidden_states, w_q, w_k, w_v, w_o, g1, g2, w_gate, w1, w3, w2):
        import jax, jax.numpy as jnp
        import numpy as np
        H, KVH, HD, D = (8, 2, 128, 512)
        E, TOPK, FFN = (8, 2, 1792)
        THETA, EPS = (1000000.0, 1e-05)
        NBITS, GS = (4, 128)
        QMAX = float(2 ** NBITS - 1)
        NEG = -1e+30

        def qgroup(w):
            shp = w.shape
            w2 = w.reshape(-1, GS)
            wmax = jnp.max(w2, -1, keepdims=True)
            wmin = jnp.min(w2, -1, keepdims=True)
            scales = jnp.clip(wmax - wmin, 1e-05, None) / QMAX
            base = jnp.clip(jnp.round(-wmin / scales), 0.0, QMAX)
            wq = (jnp.clip(jnp.round(w2 / scales) + base, 0.0, QMAX) - base) * scales
            return wq.reshape(shp)

        def rms(x, g):
            return x * jax.lax.rsqrt(jnp.mean(x * x, -1, keepdims=True) + EPS) * g

        def rot_half(x):
            h = x.shape[-1] // 2
            return jnp.concatenate([-x[..., h:], x[..., :h]], axis=-1)
        B, S, _ = hidden_states.shape
        T = B * S
        xn = rms(hidden_states, g1)
        q = (xn @ qgroup(w_q).T).reshape(B, S, H, HD).transpose(0, 2, 1, 3)
        k = (xn @ qgroup(w_k).T).reshape(B, S, KVH, HD).transpose(0, 2, 1, 3)
        v = (xn @ qgroup(w_v).T).reshape(B, S, KVH, HD).transpose(0, 2, 1, 3)
        k = qgroup(k)
        pos = jnp.arange(S, dtype=jnp.float32)
        inv = 1.0 / THETA ** (jnp.arange(0, HD, 2, dtype=jnp.float32) / HD)
        freqs = pos[:, None] * inv[None, :]
        emb = jnp.concatenate([freqs, freqs], axis=-1)
        cos = jnp.cos(emb)[None, None]
        sin = jnp.sin(emb)[None, None]
        q = q * cos + rot_half(q) * sin
        k = k * cos + rot_half(k) * sin
        rep = H // KVH
        k = jnp.repeat(k, rep, axis=1)
        v = jnp.repeat(v, rep, axis=1)
        v = qgroup(v)
        scores = jnp.einsum('bhqd,bhkd->bhqk', q, k) / np.float32(np.sqrt(HD))
        causal = jnp.tril(jnp.ones((S, S), dtype=bool))
        scores = jnp.where(causal[None, None], scores, NEG)
        attn = jax.nn.softmax(scores, axis=-1)
        o = jnp.einsum('bhqk,bhkd->bhqd', attn, v).transpose(0, 2, 1, 3).reshape(B, S, H * HD)
        h = hidden_states + o @ qgroup(w_o).T
        hn = rms(h, g2).reshape(T, D)
        logits = hn @ w_gate.T
        probs = jax.nn.softmax(logits, axis=-1)
        tv, ti = jax.lax.top_k(probs, TOPK)
        tv = tv / jnp.sum(tv, axis=-1, keepdims=True)
        rw = jnp.zeros((T, E), hn.dtype).at[jnp.arange(T)[:, None], ti].set(tv)
        moe = jnp.zeros((T, D), hn.dtype)
        for e in range(E):
            up = jax.nn.silu(hn @ qgroup(w1[e]).T) * (hn @ qgroup(w3[e]).T)
            moe = moe + rw[:, e:e + 1] * (up @ qgroup(w2[e]).T)
        return h + moe.reshape(B, S, D)
    x = x + _L0_xattn_ref(_layernorm(x, axis=-1), ctx_1024, mask_Bx1xSxS_ik0, mask_Bx1x1xS2_if1, L0_xattn_sa_wq, L0_xattn_sa_bq, L0_xattn_sa_wk, L0_xattn_sa_bk, L0_xattn_sa_wv, L0_xattn_sa_bv, L0_xattn_sa_wo, L0_xattn_sa_bo, L0_xattn_ca_wq, L0_xattn_ca_bq, L0_xattn_ca_wk, L0_xattn_ca_bk, L0_xattn_ca_wv, L0_xattn_ca_bv, L0_xattn_ca_wo, L0_xattn_ca_bo, L0_xattn_ffn_w1, L0_xattn_ffn_b1, L0_xattn_ffn_w2, L0_xattn_ffn_b2, L0_xattn_ln1_g, L0_xattn_ln1_b, L0_xattn_ln2_g, L0_xattn_ln2_b, L0_xattn_ln3_g, L0_xattn_ln3_b)
    x = x + _L0_attn_ref(_layernorm(x, axis=-1), L0_attn_Wq, L0_attn_Wkv, L0_attn_Wo)
    x = x + _L0_ffn_ref(_layernorm(x, axis=-1), L0_ffn_w_q, L0_ffn_w_k, L0_ffn_w_v, L0_ffn_w_o, L0_ffn_g1, L0_ffn_g2, L0_ffn_w_gate, L0_ffn_w1, L0_ffn_w3, L0_ffn_w2)
    return x

_drawn_inputs = setup_inputs


def setup_inputs(seed=0):
    import zlib

    import numpy as np

    out = dict(_drawn_inputs(seed))
    spreads = {'L0_xattn_sa_bq': (0.0, 0.8),
     'L0_xattn_sa_bk': (0.0, 0.8),
     'L0_xattn_sa_bv': (0.0, 0.1),
     'L0_xattn_sa_bo': (0.0, 0.1),
     'L0_xattn_ca_bq': (0.0, 0.8),
     'L0_xattn_ca_bk': (0.0, 0.8),
     'L0_xattn_ca_bv': (0.0, 0.1),
     'L0_xattn_ca_bo': (0.0, 0.1),
     'L0_xattn_ffn_b1': (0.0, 0.1),
     'L0_xattn_ffn_b2': (0.0, 0.1),
     'L0_xattn_ln1_g': (1.0, 0.2),
     'L0_xattn_ln1_b': (0.0, 0.1),
     'L0_xattn_ln2_g': (1.0, 0.2),
     'L0_xattn_ln2_b': (0.0, 0.1),
     'L0_xattn_ln3_g': (1.0, 0.2),
     'L0_xattn_ln3_b': (0.0, 0.1),
     'L0_ffn_g1': (1.0, 0.6),
     'L0_ffn_g2': (1.0, 0.6)}
    factors = {'L0_attn_Wq': 8.0, 'L0_ffn_w_q': 8.0, 'L0_ffn_w_k': 8.0}
    for name, (base, spread) in spreads.items():
        noise = np.random.default_rng([zlib.crc32(name.encode()), seed]).standard_normal(out[name].shape)
        drawn = base * np.exp(spread * noise) if base else spread * noise
        out[name] = jnp.asarray(drawn.astype(out[name].dtype))
    for name, factor in factors.items():
        out[name] = (out[name] * factor).astype(out[name].dtype)
    return out
```

```python
from contextlib import ExitStack

import concourse.bass as bass
from concourse import mybir

F32 = mybir.dt.float32
F32R = mybir.dt.float32r
I32 = mybir.dt.int32
ALU = mybir.AluOpType
ACT = mybir.ActivationFunctionType
AXX = mybir.AxisListType.X
ds = bass.ds

P = 128
T = 512
TT = T // P
D = 512
KC = D // P
HEADS = 16
DH = D // HEADS
HPG = P // DH
GROUPS = HEADS // HPG
START = 1
KEYS = 256
FF = 2048
QH, KVH, HD = 8, 2, 128
E, FFN = 8, 1792
FT = FFN // P
GS = 128
BLK = 12
QKV_TILES = (QH + 2 * KVH) * HD // P
BIG = 1.0e30
HUGE = 3.0e38
ROUND = 1.5 * 2.0 ** 23
ROUND_UP = 2.0 ** 23


def wait(eng, sem, value):
    if isinstance(value, int) and value <= 0:
        return
    eng.wait_ge(sem, value)


class Steps:

    def __init__(self, eng, sem, start=0):
        self.eng, self.sem, self.n, self.k = eng, sem, start, 0

    def __call__(self, ins):
        self.n, self.k = self.n + 1, self.k + 1
        ins.then_inc(self.sem, 1)
        self.eng.wait_ge(self.sem, self.n)


class Memory:

    def __init__(self, nc, ctx, prefix=""):
        self.nc, self.ctx, self.prefix = nc, ctx, prefix

    def sb(self, name, shape, dtype=F32):
        return self.ctx.enter_context(self.nc.sbuf_tensor(self.prefix + name, shape, dtype))

    def ps(self, name, shape, dtype=F32):
        return self.ctx.enter_context(self.nc.psum_tensor(self.prefix + name, shape, dtype))

    def sem(self, name):
        sem = self.nc.alloc_semaphore(self.prefix + name)
        self.ctx.callback(self.clear, sem)
        return sem

    def clear(self, sem):
        self.nc.gpsimd.sem_clear(sem)
        self.nc.release_semaphore(sem)


def row(ap):
    return ap.rearrange("(a n) -> a n", a=1).broadcast_to([P, ap.shape[0]])


def middle(ap, n):
    return ap.unsqueeze(1).broadcast_to([ap.shape[0], n, ap.shape[1]])


def last(ap, n):
    return ap.unsqueeze(len(ap.shape)).broadcast_to([*ap.shape, n])



def norm_stats(step, stats, x, eps, rms=False):
    dve = step.eng
    for t in range(TT):
        ins = dve.bn_stats(stats["raw"][:, t, :], x[:, t, :])
    step(ins)
    for t in range(TT):
        ins = dve.bn_aggr(stats["mv"][:, t, :], stats["raw"][:, t, :])
    step(ins)
    mean, var = stats["mv"][:, :, 0], stats["mv"][:, :, 1]
    if rms:
        step(dve.tensor_tensor(stats["tmp"], mean, mean, ALU.mult))
        step(dve.scalar_tensor_tensor(stats["v"], var, eps, stats["tmp"], ALU.add, ALU.add))
    else:
        step(dve.tensor_scalar(stats["v"], var, eps, None, ALU.add))


def norm_scale(step, stats):
    dve, r, t, v = step.eng, stats["r"], stats["tmp"], stats["v"]
    step(dve.reciprocal(r, stats["root"]))
    step(dve.tensor_tensor(t, r, r, ALU.mult))
    step(dve.tensor_tensor(t, t, v, ALU.mult))
    step(dve.tensor_scalar(t, t, -0.5, 1.5, ALU.mult, ALU.add))
    step(dve.tensor_tensor(r, r, t, ALU.mult))


def norm_apply(step, stats, y, x, gain=None, shift=None, rms=False):
    dve = step.eng
    for t in range(TT):
        if rms:
            ins = dve.tensor_scalar(y[:, t, :], x[:, t, :], stats["r"][:, t:t + 1], None, ALU.mult)
        else:
            ins = dve.tensor_scalar(y[:, t, :], x[:, t, :], stats["mv"][:, t, 0:1],
                                    stats["r"][:, t:t + 1], ALU.subtract, ALU.mult)
    step(ins)
    if gain is not None:
        step(dve.tensor_tensor(y[:, :, :], y[:, :, :], middle(gain[:, :], TT), ALU.mult))
    if shift is not None:
        step(dve.tensor_tensor(y[:, :, :], y[:, :, :], middle(shift[:, :], TT), ALU.add))


def norm(step, stats, y, x, eps, count, gain=None, shift=None, rms=False):
    norm_stats(step, stats, x, eps, rms)
    step.eng.sem_inc(stats["var_ready"], 1)
    step.eng.wait_ge(stats["root_ready"], count)
    norm_scale(step, stats)
    norm_apply(step, stats, y, x, gain, shift, rms)


def norm_root(act, stats, count):
    act.wait_ge(stats["var_ready"], count)
    act.activation(stats["root"], stats["v"], ACT.Sqrt).then_inc(stats["root_ready"], 1)


def stats_tiles(mem):
    small = mem.sb("norm_small", [P, 4, TT])
    return {"var_ready": mem.sem("var_ready"), "root_ready": mem.sem("root_ready"),
            "raw": mem.sb("norm_raw", [P, TT, 6]), "mv": mem.sb("norm_mv", [P, TT, 2]),
            "v": small[:, 0, :], "root": small[:, 1, :], "r": small[:, 2, :], "tmp": small[:, 3, :]}



def phase_start(nc, g, dram):
    with ExitStack() as ctx:
        m = Memory(nc, ctx, "start_")
        stats = stats_tiles(m)
        mask_raw = m.sb("mask_raw", [P, TT, T], I32)
        key_raw = m.sb("key_raw", [P, HEADS * KEYS], I32)
        x_loaded, consts_loaded = m.sem("x_loaded"), m.sem("consts_loaded")
        dve_step, zeroed, ident_made = m.sem("dve_step"), m.sem("zeroed"), m.sem("ident_made")
        normed, turned, copied = m.sem("normed"), m.sem("turned"), m.sem("copied")
        turn = [m.ps(f"turn{i}", [P, T]) for i in range(2)]
        block = ctx.enter_context(nc.Block())

        @block.sync
        def _(sp):
            sp.dma_start(g["x"][:, :, :], dram["x"].rearrange("(t p) d -> p t d", p=P)).then_inc(x_loaded, 16)
            sp.dma_start(mask_raw[:, :, :], dram["mask"].rearrange("(t p) k -> p t k", p=P)).then_inc(consts_loaded, 16)
            sp.dma_start(key_raw[:, :], row(dram["key_mask"])).then_inc(consts_loaded, 16)

        @block.gpsimd
        def _(pool):
            pool.memset(g["ident"][:, :], 0.0).then_inc(zeroed, 1)
            pool.memset(g["causal"][:, :, :], 0.0).then_inc(zeroed, 1)
            pool.wait_ge(zeroed, 2)
            pool.affine_select(out=g["ident"][:, :], in_=g["ident"][:, :], compare_op=ALU.not_equal, fill=1.0,
                               base=0, pattern=[[-1, P]], channel_multiplier=1).then_inc(ident_made, 1)
            pool.affine_select(out=g["causal"][:, :, :], in_=g["causal"][:, :, :], compare_op=ALU.is_ge, fill=BIG,
                               base=0, pattern=[[P, TT], [-1, T]], channel_multiplier=1)

        @block.vector
        def _(dve):
            step = Steps(dve, dve_step)
            dve.wait_ge(x_loaded, 16)
            norm(step, stats, g["a"], g["x"], 1e-5, 1)
            dve.sem_inc(normed, 1)
            dve.wait_ge(consts_loaded, 32)
            dve.tensor_scalar(g["mask"][:, :, :], mask_raw[:, :, :], 0.0, BIG, ALU.is_equal, ALU.mult)
            dve.tensor_scalar(g["key_mask"][:, :], key_raw[:, :], 0.0, BIG, ALU.is_equal, ALU.mult)

        @block.tensor
        def _(pe):
            pe.wait_ge(ident_made, 1)
            pe.wait_ge(normed, 1)
            turn_tokens(pe, g["a"], turn, g["ident"], turned, copied)

        @block.scalar
        def _(act):
            norm_root(act, stats, 1)
            copy_turned(act, g["aT"], turn, turned, copied)


def turn_tokens(pe, src, turn, ident, turned, copied, chunks=KC):
    for c in range(chunks):
        wait(pe, copied, c - 1)
        for t in range(TT):
            ins = pe.transpose(turn[c % 2][:, t * P:(t + 1) * P], src[:, t, c * P:(c + 1) * P], ident[:, :])
        ins.then_inc(turned, 1)


def copy_turned(act, dst, turn, turned, copied, chunks=KC):
    for c in range(chunks):
        act.wait_ge(turned, c + 1)
        act.activation(dst[:, c, :], turn[c % 2][:, :], ACT.Copy).then_inc(copied, 1)



class Core:

    def __init__(self, m, units, q, k, v, bias, keys, width, eps):
        self.units, self.q, self.k, self.v, self.bias, self.keys = units, q, k, v, bias, keys
        self.width, self.eps = width, eps
        self.heads = len({h for h, _ in units})
        self.n = len(units)
        self.shifted = m.sb("shifted", [P, 4, T])
        self.least = m.sb("least", [P, self.n])
        self.row_sum = m.sb("row_sum", [P, TT, self.heads])
        self.row_inv = m.sb("row_inv", [P, TT, self.heads])
        self.probsT = m.sb("probsT", [P, 2, T])
        self.psS = [m.ps(f"psS{i}", [P, T]) for i in range(2)]
        self.psT = [m.ps(f"psT{i}", [P, T]) for i in range(2)]
        self.psO = m.ps("psO", [P, T])
        self.scores_ready = m.sem("scores_ready")
        self.shifted_ready = m.sem("shifted_ready")
        self.probs_ready = m.sem("probs_ready")
        self.probsT_ready = m.sem("probsT_ready")
        self.probsT_copied = m.sem("probsT_copied")
        self.values_done = m.sem("values_done")
        self.normalised = m.sem("normalised")
        self.begun = m.sem("begun")

    SHIFTED0, COPIED0, TURNED0, VALUES0, NORMALISED0 = 2, 2, 4, 2, 1

    def prime_vector(self, dve):
        dve.sem_inc(self.shifted_ready, self.SHIFTED0)
        dve.sem_inc(self.probsT_copied, self.COPIED0)
        dve.sem_inc(self.normalised, self.NORMALISED0)

    def prime_tensor(self, pe):
        pe.sem_inc(self.probsT_ready, self.TURNED0)
        pe.sem_inc(self.values_done, self.VALUES0)

    def tensor(self, pe, g, ident):
        base = g * self.n
        for s in range(self.n + 3):
            if s < self.n:
                h, t = self.units[s]
                n = self.keys(t)
                pe.wait_ge(self.shifted_ready, base + s - 1 + self.SHIFTED0)
                pe.matmul(self.psS[s % 2][:, 0:n], self.q(g, h, t), self.k(g, h, n), start=True, stop=True)\
                  .then_inc(self.scores_ready, 1)
            u = s - 2
            if 0 <= u < self.n:
                h, t = self.units[u]
                pe.wait_ge(self.probs_ready, base + u + 1)
                pe.wait_ge(self.probsT_copied, base + u - 1 + self.COPIED0)
                for c in range(self.keys(t) // P):
                    ins = pe.transpose(self.psT[u % 2][:, c * P:(c + 1) * P],
                                       self.shifted[:, u % 4, c * P:(c + 1) * P], ident[:, :])
                ins.then_inc(self.probsT_ready, 1)
            u = s - 3
            if u >= 0:
                h, t = self.units[u]
                if u == 0:
                    pe.wait_ge(self.normalised, g + self.NORMALISED0)
                pe.wait_ge(self.probsT_copied, base + u + 1 + self.COPIED0)
                col = (t * self.heads + h) * self.width
                chunks = self.keys(t) // P
                for c in range(chunks):
                    ins = pe.matmul(self.psO[:, col:col + self.width], self.probsT[:, u % 2, c * P:(c + 1) * P],
                                    self.v(g, h, c), start=(c == 0), stop=(c == chunks - 1))
                ins.then_inc(self.values_done, 1)

    def vector(self, dve, g, step, out):
        base = g * self.n
        for s in range(self.n + 2):
            if s < self.n:
                h, t = self.units[s]
                n = self.keys(t)
                dve.wait_ge(self.scores_ready, base + s + 1)
                dve.wait_ge(self.probsT_ready, base + s - 3 + self.TURNED0)
                dve.sem_inc(self.begun, 1)
                dve.tensor_tensor_reduce(self.shifted[:, s % 4, 0:n], self.psS[s % 2][:, 0:n],
                                         self.bias(g, h, t, n), 1.0, HUGE, ALU.add, ALU.min,
                                         self.least[:, s:s + 1]).then_inc(self.shifted_ready, 1)
            u = s - 2
            if u >= 0:
                n = self.keys(self.units[u][1])
                dve.wait_ge(self.probsT_ready, base + u + 1 + self.TURNED0)
                dve.wait_ge(self.values_done, base + u - 1 + self.VALUES0)
                dve.tensor_copy(self.probsT[:, u % 2, 0:n], self.psT[u % 2][:, 0:n]).then_inc(self.probsT_copied, 1)
        dve.wait_ge(self.values_done, base + self.n + self.VALUES0)
        if self.eps:
            step(dve.tensor_scalar(self.row_sum[:, :, :], self.row_sum[:, :, :], self.eps, None, ALU.add))
        step(dve.reciprocal(self.row_inv[:, :, :], self.row_sum[:, :, :]))
        width = self.heads * self.width
        dve.tensor_tensor(out.rearrange("p t (h d) -> p t h d", h=self.heads),
                          self.psO[:, 0:TT * width].rearrange("p (t h d) -> p t h d", t=TT, h=self.heads),
                          last(self.row_inv[:, :, :], self.width), ALU.mult).then_inc(self.normalised, 1)

    @property
    def vector_steps(self):
        return 2 if self.eps else 1

    def scalar(self, act, g):
        base = g * self.n
        act.wait_ge(self.normalised, g + self.NORMALISED0)
        for s in range(self.n):
            h, t = self.units[s]
            n = self.keys(t)
            act.wait_ge(self.shifted_ready, base + s + 1 + self.SHIFTED0)
            act.activation(self.shifted[:, s % 4, 0:n], self.shifted[:, s % 4, 0:n], ACT.Exp,
                           bias=self.least[:, s:s + 1], scale=-1.0,
                           accum_out=self.row_sum[:, t, h:h + 1]).then_inc(self.probs_ready, 1)



def phase_self_attention(nc, g, dram, name, causal, eps):
    with ExitStack() as ctx:
        m = Memory(nc, ctx, name + "_")
        has_bias = dram.get(name + "_bq") is not None
        w = {c: m.sb(f"w{c}", [P, KC, P]) for c in "qkv"}
        q, k = m.sb("q", [P, T]), m.sb("k", [P, T])
        v = m.sb("v", [P, TT, P])
        if has_bias:
            bq, bk, bq_scaled = (m.sb(n, [P, GROUPS]) for n in ("bq", "bk", "bq_scaled"))
            bv = m.sb("bv", [P, D])
        core = Core(
            m, [(h, t) for h in range(HPG) for t in range(TT)],
            q=lambda j, h, t: q[h * DH:(h + 1) * DH, t * P:(t + 1) * P],
            k=lambda j, h, n: k[h * DH:(h + 1) * DH, 0:n],
            v=lambda j, h, c: v[:, c, h * DH:(h + 1) * DH],
            bias=lambda j, h, t, n: g["causal" if causal else "mask"][:, t, 0:n],
            keys=(lambda t: (t + 1) * P) if causal else (lambda t: T), width=DH, eps=eps)
        psQ, psK = m.ps("psQ", [P, T]), m.ps("psK", [P, T])
        psV = psQ
        bias_loaded, bias_scaled, w_loaded = m.sem("bias_loaded"), m.sem("bias_scaled"), m.sem("w_loaded")
        qk_ready, v_ready = m.sem("qk_ready"), m.sem("v_ready")
        q_copied, kv_copied = m.sem("q_copied"), m.sem("kv_copied")
        dve_step = m.sem("dve_step")
        block = ctx.enter_context(nc.Block())

        @block.sync
        def _(sp):
            if has_bias:
                sp.dma_start(bq[:, :], dram[name + "_bq"]).then_inc(bias_loaded, 16)
                sp.dma_start(bk[:, :], dram[name + "_bk"]).then_inc(bias_loaded, 16)
                sp.dma_start(bv[:, :], row(dram[name + "_bv"])).then_inc(bias_loaded, 16)
            with sp.Fori(0, GROUPS) as j:
                sp.wait_ge(v_ready, j + START)
                for c in "qkv":
                    src = dram[f"{name}_w{c}"].rearrange("(c p) n -> p c n", p=P)
                    sp.dma_start(w[c][:, :, :], src[:, :, ds(j * P, P)]).then_inc(w_loaded, 16)

        @block.tensor
        def _(pe):
            core.prime_tensor(pe)
            pe.sem_inc(v_ready, START)
            with pe.Fori(0, GROUPS) as j:
                pe.wait_ge(w_loaded, 48 * j + 48)
                for c, ps in (("q", psQ), ("k", psK)):
                    for i in range(KC):
                        ins = pe.matmul(ps[:, :], w[c][:, i, :], g["aT"][:, i, :], start=(i == 0), stop=(i == KC - 1))
                    ins.then_inc(qk_ready, 1)
                pe.wait_ge(q_copied, j + 1)
                for t in range(TT):
                    for i in range(KC):
                        ins = pe.matmul(psV[:, t * P:(t + 1) * P], g["aT"][:, i, t * P:(t + 1) * P], w["v"][:, i, :],
                                        start=(i == 0), stop=(i == KC - 1))
                ins.then_inc(v_ready, 1)
                pe.wait_ge(kv_copied, 2 * j + 2)
                core.tensor(pe, j, g["ident"])

        @block.scalar
        def _(act):
            if has_bias:
                act.wait_ge(bias_loaded, 48)
                act.activation(bq_scaled[:, :], bq[:, :], ACT.Copy, scale=-DH ** -0.5).then_inc(bias_scaled, 1)
                act.wait_ge(bias_scaled, 1)
            with act.Fori(0, GROUPS) as j:
                act.wait_ge(qk_ready, 2 * j + 1)
                if has_bias:
                    act.activation(q[:, :], psQ[:, :], ACT.Identity, bias=bq_scaled[:, ds(j, 1)],
                                   scale=-DH ** -0.5).then_inc(q_copied, 1)
                else:
                    act.activation(q[:, :], psQ[:, :], ACT.Copy, scale=-DH ** -0.5).then_inc(q_copied, 1)
                act.wait_ge(qk_ready, 2 * j + 2)
                if has_bias:
                    act.activation(k[:, :], psK[:, :], ACT.Identity, bias=bk[:, ds(j, 1)]).then_inc(kv_copied, 1)
                else:
                    act.activation(k[:, :], psK[:, :], ACT.Copy).then_inc(kv_copied, 1)
                core.scalar(act, j)

        @block.vector
        def _(dve):
            core.prime_vector(dve)
            step = Steps(dve, dve_step)
            if has_bias:
                dve.wait_ge(bias_loaded, 48)
            with dve.Fori(0, GROUPS) as j:
                step.n, step.k = j * core.vector_steps, 0
                dve.wait_ge(v_ready, j + 1 + START)
                pv = psV[:, :].rearrange("p (t n) -> p t n", t=TT)
                if has_bias:
                    dve.tensor_tensor(v[:, :, :], pv, middle(bv[:, ds(j * P, P)], TT), ALU.add).then_inc(kv_copied, 1)
                else:
                    dve.tensor_copy(v[:, :, :], pv).then_inc(kv_copied, 1)
                core.vector(dve, j, step, g["o"][:, :, ds(j * P, P)])
                assert step.k == core.vector_steps



def phase_cross_attention(nc, g, dram, name):
    with ExitStack() as ctx:
        m = Memory(nc, ctx, name + "_")
        w = {c: m.sb(f"w{c}", [P, KC, P]) for c in "qkv"}
        enc = m.sb("enc", [P, HPG, KC, KEYS])
        bias = m.sb("bias", [P, HPG * KEYS])
        q, k = m.sb("q", [P, T]), m.sb("k", [P, KEYS])
        v = m.sb("v", [P, HPG, KEYS // P, DH])
        bq, bk, bq_scaled = (m.sb(n, [P, GROUPS]) for n in ("bq", "bk", "bq_scaled"))
        bv = m.sb("bv", [P, D])
        core = Core(
            m, [(h, t) for h in range(HPG) for t in range(TT)],
            q=lambda j, h, t: q[h * DH:(h + 1) * DH, t * P:(t + 1) * P],
            k=lambda j, h, n: k[h * DH:(h + 1) * DH, 0:n],
            v=lambda j, h, c: v[:, h, c, :],
            bias=lambda j, h, t, n: bias[:, h * KEYS:(h + 1) * KEYS],
            keys=lambda t: KEYS, width=DH, eps=0.0)
        psQ, psK, psV = m.ps("psQ", [P, T]), m.ps("psK", [P, T]), m.ps("psV", [P, T])
        bias_loaded, bias_scaled, w_loaded = m.sem("bias_loaded"), m.sem("bias_scaled"), m.sem("w_loaded")
        qk_ready, v_ready, copied = m.sem("qk_ready"), m.sem("v_ready"), m.sem("copied")
        bias_copied = m.sem("bias_copied")
        dve_step = m.sem("dve_step")
        block = ctx.enter_context(nc.Block())

        @block.sync
        def _(sp):
            sp.dma_start(bq[:, :], dram[name + "_bq"]).then_inc(bias_loaded, 16)
            sp.dma_start(bk[:, :], dram[name + "_bk"]).then_inc(bias_loaded, 16)
            sp.dma_start(bv[:, :], row(dram[name + "_bv"])).then_inc(bias_loaded, 16)
            enc_src = dram["enc"].rearrange("(j h) (c p) n -> p j h c n", h=HPG, p=P)
            with sp.Fori(0, GROUPS) as j:
                sp.wait_ge(v_ready, j + START)
                for c in "qkv":
                    src = dram[f"{name}_w{c}"].rearrange("(c p) n -> p c n", p=P)
                    sp.dma_start(w[c][:, :, :], src[:, :, ds(j * P, P)]).then_inc(w_loaded, 16)
                for h in range(HPG):
                    sp.dma_start(enc[:, h, :, :], enc_src[:, ds(j, 1), h, :, :].squeeze(1)).then_inc(w_loaded, 16)

        @block.tensor
        def _(pe):
            core.prime_tensor(pe)
            pe.sem_inc(v_ready, START)
            with pe.Fori(0, GROUPS) as j:
                pe.wait_ge(w_loaded, 16 * (3 + HPG) * (j + 1))
                for i in range(KC):
                    ins = pe.matmul(psQ[:, :], w["q"][:, i, :], g["aT"][:, i, :], start=(i == 0), stop=(i == KC - 1))
                ins.then_inc(qk_ready, 1)
                for h in range(HPG):
                    for i in range(KC):
                        ins = pe.matmul(psK[h * DH:(h + 1) * DH, 0:KEYS], w["k"][:, i, h * DH:(h + 1) * DH],
                                        enc[:, h, i, :], start=(i == 0), stop=(i == KC - 1))
                ins.then_inc(qk_ready, 1)
                for h in range(HPG):
                    for c in range(KEYS // P):
                        for i in range(KC):
                            col = (h * (KEYS // P) + c) * DH
                            ins = pe.matmul(psV[:, col:col + DH], enc[:, h, i, c * P:(c + 1) * P],
                                            w["v"][:, i, h * DH:(h + 1) * DH], start=(i == 0), stop=(i == KC - 1))
                ins.then_inc(v_ready, 1)
                pe.wait_ge(copied, 3 * j + 3)
                core.tensor(pe, j, g["ident"])

        @block.scalar
        def _(act):
            act.wait_ge(bias_loaded, 48)
            act.activation(bq_scaled[:, :], bq[:, :], ACT.Copy, scale=-DH ** -0.5).then_inc(bias_scaled, 1)
            act.wait_ge(bias_scaled, 1)
            with act.Fori(0, GROUPS) as j:
                act.activation(bias[:, :], g["key_mask"][:, ds(j * (HPG * KEYS), HPG * KEYS)], ACT.Copy)\
                   .then_inc(bias_copied, 1)
                act.wait_ge(qk_ready, 2 * j + 1)
                act.activation(q[:, :], psQ[:, :], ACT.Identity, bias=bq_scaled[:, ds(j, 1)],
                               scale=-DH ** -0.5).then_inc(copied, 1)
                act.wait_ge(qk_ready, 2 * j + 2)
                act.activation(k[:, :], psK[:, 0:KEYS], ACT.Identity, bias=bk[:, ds(j, 1)]).then_inc(copied, 1)
                core.scalar(act, j)

        @block.vector
        def _(dve):
            core.prime_vector(dve)
            step = Steps(dve, dve_step)
            dve.wait_ge(bias_loaded, 48)
            with dve.Fori(0, GROUPS) as j:
                step.n, step.k = j * core.vector_steps, 0
                dve.wait_ge(v_ready, j + 1 + START)
                for c in range(KEYS // P):
                    ins = dve.tensor_tensor(
                        v[:, :, c, :], psV[:, 0:HPG * KEYS // P * DH].rearrange("p (h c d) -> p h c d", h=HPG, d=DH)[:, :, c, :],
                        bv[:, ds(j * P, P)].rearrange("p (h d) -> p h d", h=HPG), ALU.add)
                ins.then_inc(copied, 1)
                dve.wait_ge(bias_copied, j + 1)
                core.vector(dve, j, step, g["o"][:, :, ds(j * P, P)])
                assert step.k == core.vector_steps



def project(pe, acc, oT, w, copied, done, chunks):
    pe.wait_ge(copied, chunks)
    for t in range(TT):
        for c in range(chunks):
            ins = pe.matmul(acc[t][:, :], oT[:, c, t * P:(t + 1) * P], w[:, c, :], start=(c == 0), stop=(c == chunks - 1))
        ins.then_inc(done, 1)


def phase_project(nc, g, dram, name, src, w_src, last_of):
    with ExitStack() as ctx:
        m = Memory(nc, ctx, name + "_out_")
        stats = stats_tiles(m)
        w = m.sb("w", [P, KC, D])
        oT = m.sb("oT", [P, KC, T])
        turn = [m.ps(f"turn{i}", [P, T]) for i in range(2)]
        acc = [m.ps(f"acc{i}", [P, D]) for i in range(TT)]
        loaded, turned, copied = m.sem("loaded"), m.sem("turned"), m.sem("copied")
        done, dve_step, normed = m.sem("done"), m.sem("dve_step"), m.sem("normed")
        rows = {}
        if last_of in ("sa", "ca"):
            rows = {k: m.sb(k, [P, D]) for k in ("bo", "gain", "shift")}
            ln = {"sa": "ln1", "ca": "ln2"}[last_of]
            row_src = {"bo": f"{name}_bo", "gain": f"{ln}_g", "shift": f"{ln}_b"}
        else:
            rows, row_src = {"gain": m.sb("gain", [P, D])}, {"gain": "g1"}
            xn = m.sb("xn", [P, TT, D])
        block = ctx.enter_context(nc.Block())

        @block.sync
        def _(sp):
            sp.dma_start(w[:, :, :], w_src.rearrange("(c p) n -> p c n", p=P)).then_inc(loaded, 16)
            for k, tile in rows.items():
                sp.dma_start(tile[:, :], row(dram[row_src[k]])).then_inc(loaded, 16)

        @block.tensor
        def _(pe):
            turn_tokens(pe, src, turn, g["ident"], turned, copied)
            pe.wait_ge(loaded, 16 * (1 + len(rows)))
            project(pe, acc, oT, w, copied, done, KC)
            pe.wait_ge(normed, 1)
            for c in range(KC):
                pe.wait_ge(copied, KC + c - 1)
                for t in range(TT):
                    final = xn if last_of == "attn" else g["a"]
                    ins = pe.transpose(turn[c % 2][:, t * P:(t + 1) * P], final[:, t, c * P:(c + 1) * P], g["ident"][:, :])
                ins.then_inc(turned, 1)

        @block.scalar
        def _(act):
            copy_turned(act, oT, turn, turned, copied)
            norm_root(act, stats, 1)
            if last_of == "attn":
                norm_root(act, stats, 2)
            for c in range(KC):
                act.wait_ge(turned, KC + c + 1)
                act.activation(g["aT"][:, c, :], turn[c % 2][:, :], ACT.Copy).then_inc(copied, 1)

        @block.vector
        def _(dve):
            step = Steps(dve, dve_step)
            dve.wait_ge(loaded, 16 * (1 + len(rows)))
            if last_of in ("sa", "ca"):
                step(dve.tensor_tensor(g["a"][:, :, :], g["a"][:, :, :], middle(rows["bo"][:, :], TT), ALU.add))
            into = g["x"] if last_of == "attn" else g["a"]
            for t in range(TT):
                dve.wait_ge(done, t + 1)
                ins = dve.tensor_tensor(into[:, t, :], into[:, t, :], acc[t][:, :], ALU.add)
            step(ins)
            if last_of in ("sa", "ca"):
                norm(step, stats, g["a"], g["a"], 1e-6, 1, gain=rows["gain"], shift=rows["shift"])
            else:
                norm(step, stats, g["a"], g["x"], 1e-5, 1)
                norm(step, stats, xn, g["a"], 1e-5, 2, gain=rows["gain"], rms=True)
            dve.sem_inc(normed, 1)



def phase_mlp(nc, g, dram):
    with ExitStack() as ctx:
        m = Memory(nc, ctx, "mlp_")
        stats = stats_tiles(m)
        PAIRS = FF // (2 * P)
        w1, w2 = m.sb("w1", [P, KC, 2 * P]), m.sb("w2", [P, 2, D])
        b1 = m.sb("b1", [P, FF // P])
        rows = {k: m.sb(k, [P, D]) for k in ("b2", "gain", "shift")}
        hT = m.sb("hT", [P, 2, T])
        zero = m.sb("zero", [P, D])
        psH = [m.ps(f"psH{i}", [P, T]) for i in range(2)]
        acc = [m.ps(f"acc{i}", [P, D]) for i in range(TT)]
        turn = [m.ps(f"turn{i}", [P, T]) for i in range(2)]
        rows_loaded, w1_loaded, w2_loaded = m.sem("rows_loaded"), m.sem("w1_loaded"), m.sem("w2_loaded")
        zeroed, h_ready, relu_done, out_done = m.sem("zeroed"), m.sem("h_ready"), m.sem("relu_done"), m.sem("out_done")
        dve_step, normed, turned, copied = m.sem("dve_step"), m.sem("normed"), m.sem("turned"), m.sem("copied")
        block = ctx.enter_context(nc.Block())

        @block.sync
        def _(sp):
            sp.dma_start(b1[:, :], dram["ffn_b1"]).then_inc(rows_loaded, 16)
            for k, name in (("b2", "ffn_b2"), ("gain", "ln3_g"), ("shift", "ln3_b")):
                sp.dma_start(rows[k][:, :], row(dram[name])).then_inc(rows_loaded, 16)
            w1_src = dram["ffn_w1"].rearrange("(c p) n -> p c n", p=P)
            w2_src = dram["ffn_w2"].rearrange("(i c p) n -> p i c n", c=2, p=P)
            with sp.Fori(0, PAIRS) as i:
                sp.wait_ge(h_ready, 2 * i + START)
                sp.dma_start(w1[:, :, :], w1_src[:, :, ds(i * (2 * P), 2 * P)]).then_inc(w1_loaded, 16)
                sp.wait_ge(out_done, 2 * i + START + 1)
                sp.dma_start(w2[:, :, :], w2_src[:, ds(i, 1), :, :].squeeze(1)).then_inc(w2_loaded, 16)

        @block.gpsimd
        def _(pool):
            pool.memset(zero[:, :], 0.0).then_inc(zeroed, 1)

        @block.tensor
        def _(pe):
            pe.wait_ge(zeroed, 1)
            for t in range(TT):
                pe.matmul(acc[t][:, :], zero[:, 0:P], zero[:, :], start=True, stop=False, skip_group_check=True)
            pe.sem_inc(h_ready, START)
            pe.sem_inc(out_done, START + 1)
            with pe.Fori(0, PAIRS) as i:
                pe.wait_ge(w1_loaded, 16 * i + 16)
                pe.wait_ge(relu_done, 2 * i + START)
                for f in range(2):
                    for c in range(KC):
                        ins = pe.matmul(psH[f][:, :], w1[:, c, f * P:(f + 1) * P], g["aT"][:, c, :],
                                        start=(c == 0), stop=(c == KC - 1))
                    ins.then_inc(h_ready, 1)
                pe.wait_ge(w2_loaded, 16 * i + 16)
                for f in range(2):
                    pe.wait_ge(relu_done, 2 * i + f + 1 + START)
                    for t in range(TT):
                        ins = pe.matmul(acc[t][:, :], hT[:, f, t * P:(t + 1) * P], w2[:, f, :],
                                        start=False, stop=False, skip_group_check=True)
                    ins.then_inc(out_done, 1)
            for t in range(TT):
                ins = pe.matmul(acc[t][:, :], zero[:, 0:P], zero[:, :], start=False, stop=True, skip_group_check=True)
            ins.then_inc(out_done, 1)
            pe.wait_ge(normed, 1)
            turn_tokens(pe, g["a"], turn, g["ident"], turned, copied)

        @block.scalar
        def _(act):
            act.wait_ge(rows_loaded, 64)
            act.sem_inc(relu_done, START)
            with act.Fori(0, PAIRS) as i:
                for f in range(2):
                    act.wait_ge(h_ready, 2 * i + f + 1 + START)
                    act.wait_ge(out_done, 2 * i + f + START)
                    act.activation(hT[:, f, :], psH[f][:, :], ACT.Relu, bias=b1[:, ds(2 * i + f, 1)]).then_inc(relu_done, 1)
            norm_root(act, stats, 1)
            norm_root(act, stats, 2)
            copy_turned(act, g["aT"], turn, turned, copied)

        @block.vector
        def _(dve):
            step = Steps(dve, dve_step)
            dve.wait_ge(rows_loaded, 64)
            step(dve.tensor_tensor(g["a"][:, :, :], g["a"][:, :, :], middle(rows["b2"][:, :], TT), ALU.add))
            dve.wait_ge(out_done, 2 * PAIRS + 1 + START + 1)
            for t in range(TT):
                ins = dve.tensor_tensor(g["a"][:, t, :], g["a"][:, t, :], acc[t][:, :], ALU.add)
            step(ins)
            norm(step, stats, g["a"], g["a"], 1e-6, 1, gain=rows["gain"], shift=rows["shift"])
            step(dve.tensor_tensor(g["x"][:, :, :], g["x"][:, :, :], g["a"][:, :, :], ALU.add))
            norm(step, stats, g["a"], g["x"], 1e-5, 2)
            dve.sem_inc(normed, 1)



def quantise(step, w, small):
    dve = step.eng
    hi, lo, scale, inv, base = (small[:, i, :] for i in range(5))
    dve.tensor_reduce(hi, w, AXX, ALU.max)
    step(dve.tensor_reduce(lo, w, AXX, ALU.min))
    step(dve.tensor_tensor(scale, hi, lo, ALU.subtract))
    step(dve.tensor_scalar(scale, scale, 1e-5, 1.0 / 15.0, ALU.max, ALU.mult))
    step(dve.reciprocal(inv, scale))
    step(dve.tensor_tensor(base, lo, inv, ALU.mult))
    step(dve.tensor_scalar(base, base, -1.0, ROUND, ALU.mult, ALU.add))
    step(dve.tensor_scalar(base, base, ROUND, 0.0, ALU.subtract, ALU.max))
    step(dve.tensor_scalar(base, base, 15.0, None, ALU.min))
    step(dve.tensor_tensor(w, w, last(inv, GS), ALU.mult))
    step(dve.tensor_scalar(w, w, ROUND, None, ALU.add))
    step(dve.scalar_tensor_tensor(w, w, ROUND, last(base, GS), ALU.subtract, ALU.add))
    step(dve.tensor_scalar(w, w, 0.0, 15.0, ALU.max, ALU.min))
    step(dve.tensor_tensor(w, w, last(base, GS), ALU.subtract))
    step(dve.tensor_tensor(w, w, last(scale, GS), ALU.mult))


QUANT_STEPS = 14


def phase_quantise_weights(nc, g, dram):
    N = 16
    BANKS = N * P // T
    with ExitStack() as ctx:
        m = Memory(nc, ctx, "quant_")
        raw, small = m.sb("raw", [P, N, GS]), m.sb("small", [P, 5, N])
        psT = [m.ps(f"psT{i}", [P, T]) for i in range(BANKS)]
        loaded, dve_step, quantised = m.sem("loaded"), m.sem("dve_step"), m.sem("quantised")
        turned, copied = m.sem("turned"), m.sem("copied")
        batches = (QKV_TILES * KC + KC * QH) // N
        block = ctx.enter_context(nc.Block())

        @block.sync
        def _(sp):
            with sp.Fori(0, batches) as i:
                sp.wait_ge(turned, BANKS * i + START)
                sp.dma_start(raw[:, :, :], dram["w_attn"][ds(i, 1), :, :].squeeze(0).rearrange("p (n k) -> p n k", n=N))\
                  .then_inc(loaded, 16)

        @block.vector
        def _(dve):
            step = Steps(dve, dve_step)
            with dve.Fori(0, batches) as i:
                step.n, step.k = i * QUANT_STEPS, 0
                dve.wait_ge(loaded, 16 * i + 16)
                quantise(step, raw[:, :, :], small)
                assert step.k == QUANT_STEPS
                dve.sem_inc(quantised, 1)

        @block.tensor
        def _(pe):
            pe.sem_inc(turned, START)
            with pe.Fori(0, batches) as i:
                pe.wait_ge(quantised, i + 1)
                pe.wait_ge(copied, BANKS * i + START)
                for b in range(BANKS):
                    for c in range(T // P):
                        ins = pe.transpose(psT[b][:, c * P:(c + 1) * P], raw[:, b * (T // P) + c, :], g["ident"][:, :])
                    ins.then_inc(turned, 1)

        @block.scalar
        def _(act):
            act.sem_inc(copied, START)
            with act.Fori(0, batches) as i:
                for b in range(BANKS):
                    act.wait_ge(turned, BANKS * i + b + 1 + START)
                    act.activation(g["wT"][:, ds(i * (N * P) + b * T, T)], psT[b][:, :], ACT.Copy).then_inc(copied, 1)



def phase_qkv(nc, g, dram):
    rows = QKV_TILES * P
    with ExitStack() as ctx:
        m = Memory(nc, ctx, "qkv_")
        q = m.sb("q", [P, TT, QH * HD])
        small = m.sb("small", [P, 5, TT * 2 * KVH])
        part = m.sb("part", [P, 2, QH * HD])
        rope = {k: m.sb(k, [P, TT, HD // 2]) for k in ("cos_q", "sin_q", "cos_k", "sin_k")}
        ps = [m.ps(f"ps{i}", [P, T]) for i in range(8)]
        loaded, ready, q_copied, kv_copied = (m.sem(n) for n in ("loaded", "ready", "q_copied", "kv_copied"))
        dve_step, rotated, turned, copied = m.sem("dve_step"), m.sem("rotated"), m.sem("turned"), m.sem("copied")
        kv_flat = g["kv"][:, :, :, :].rearrange("p t h d -> p (t h) d")
        block = ctx.enter_context(nc.Block())

        @block.sync
        def _(sp):
            for k, tile in rope.items():
                sp.dma_start(tile[:, :, :], dram[k].rearrange("(t p) d -> p t d", p=P)).then_inc(loaded, 16)

        @block.tensor
        def _(pe):
            for n, col in enumerate((2 * T, 0, T)):
                for t in range(TT):
                    b = (n * TT + t) % 8
                    if n == 2:
                        pe.wait_ge(kv_copied, t + 1)
                    for c in range(KC):
                        ins = pe.matmul(ps[b][:, :], g["aT"][:, c, t * P:(t + 1) * P],
                                        g["wT"][:, c * rows + col:c * rows + col + T], start=(c == 0), stop=(c == KC - 1))
                    ins.then_inc(ready, 1)
            for h in range(QH + KVH):
                if h == 0:
                    pe.wait_ge(rotated, 1)
                if h == QH:
                    pe.wait_ge(rotated, 2)
                pe.wait_ge(q_copied, 8)
                wait(pe, copied, h - 1)
                for t in range(TT):
                    src = q[:, t, h * HD:(h + 1) * HD] if h < QH else g["kv"][:, t, h - QH, :]
                    ins = pe.transpose(ps[h % 2][:, t * P:(t + 1) * P], src, g["ident"][:, :])
                ins.then_inc(turned, 1)

        @block.scalar
        def _(act):
            for t in range(TT):
                act.wait_ge(ready, t + 1)
                act.activation(g["kv"][:, t, :, :].rearrange("p h d -> p (h d)"), ps[t][:, :], ACT.Copy).then_inc(kv_copied, 1)
            for n in range(2):
                for t in range(TT):
                    act.wait_ge(ready, (n + 1) * TT + t + 1)
                    act.activation(q[:, t, n * T:(n + 1) * T], ps[((n + 1) * TT + t) % 8][:, :], ACT.Copy).then_inc(q_copied, 1)
            for h in range(QH + KVH):
                act.wait_ge(turned, h + 1)
                dst = g["qT"][:, h, :] if h < QH else g["kT"][:, h - QH, :]
                act.activation(dst, ps[h % 2][:, :], ACT.Copy).then_inc(copied, 1)

        def rotate(step, x, cos, sin, heads):
            dve = step.eng
            halves = x.rearrange("p (n d) -> p n d", d=HD // 2)
            pc, psn = (part[:, i, 0:heads * HD].rearrange("p (n d) -> p n d", d=HD // 2) for i in range(2))
            dve.tensor_tensor(pc, halves, middle(cos, 2 * heads), ALU.mult)
            step(dve.tensor_tensor(psn, halves, middle(sin, 2 * heads), ALU.mult))
            xs, cs, ss = (y.rearrange("p (h two) d -> p h two d", two=2) for y in (halves, pc, psn))
            dve.tensor_tensor(xs[:, :, 0, :], cs[:, :, 0, :], ss[:, :, 1, :], ALU.subtract)
            step(dve.tensor_tensor(xs[:, :, 1, :], cs[:, :, 1, :], ss[:, :, 0, :], ALU.add))

        @block.vector
        def _(dve):
            step = Steps(dve, dve_step)
            dve.wait_ge(loaded, 64)
            dve.wait_ge(q_copied, 8)
            for t in range(TT):
                rotate(step, q[:, t, :], rope["cos_q"][:, t, :], rope["sin_q"][:, t, :], QH)
            dve.sem_inc(rotated, 1)
            dve.wait_ge(kv_copied, 4)
            quantise(step, kv_flat, small)
            for t in range(TT):
                k = g["kv"][:, t, 0:KVH, :].rearrange("p h d -> p (h d)")
                rotate(step, k, rope["cos_k"][:, t, :], rope["sin_k"][:, t, :], KVH)
            dve.sem_inc(rotated, 1)


def phase_gqa_attention(nc, g):
    with ExitStack() as ctx:
        m = Memory(nc, ctx, "gqa_")
        rep = QH // KVH
        core = Core(
            m, [(0, t) for t in range(TT)],
            q=lambda j, h, t: g["qT"][:, j, t * P:(t + 1) * P],
            k=lambda j, h, n: g["kT"][:, j // rep, 0:n],
            v=lambda j, h, c: g["kv"][:, c, KVH + j // rep, :],
            bias=lambda j, h, t, n: g["causal"][:, t, 0:n],
            keys=lambda t: (t + 1) * P, width=HD, eps=0.0)
        dve_step = m.sem("dve_step")
        block = ctx.enter_context(nc.Block())

        @block.tensor
        def _(pe):
            core.prime_tensor(pe)
            for j in range(QH):
                core.tensor(pe, j, g["ident"])

        @block.scalar
        def _(act):
            for j in range(QH):
                core.scalar(act, j)

        @block.vector
        def _(dve):
            core.prime_vector(dve)
            step = Steps(dve, dve_step)
            for j in range(QH):
                core.vector(dve, j, step, g["o"][:, :, j * HD:(j + 1) * HD])



def phase_router(nc, g, dram):
    chunks = QH * HD // P
    with ExitStack() as ctx:
        m = Memory(nc, ctx, "router_")
        stats = stats_tiles(m)
        oT = m.sb("oT", [P, chunks, T])
        hn = m.sb("hn", [P, TT, D])
        gain, wg = m.sb("gain", [P, D]), m.sb("wg", [P, KC, E])
        earlier = m.sb("earlier", [P, E, E])
        logits, e, picked, rw = (m.sb(n, [P, TT, E]) for n in ("logits", "exps", "picked", "rw"))
        above, level = (m.sb(n, [P, TT, E, E]) for n in ("above", "level"))
        col = m.sb("col", [P, 3, TT])
        rwT, pick = m.sb("rwT", [E, T]), m.sb("pick", [E, E, P])
        turn = [m.ps(f"turn{i}", [P, T]) for i in range(2)]
        acc = [m.ps(f"acc{i}", [P, D]) for i in range(TT)]
        psL, psR = m.ps("psL", [P, TT, E]), m.ps("psR", [P, T])
        names = ("loaded turned copied done dve_step normed ones tri logits_ready shifted exps_ready "
                 "rw_ready rwT_ready rwT_copied spread spread_copied").split()
        (loaded, turned, copied, done, dve_step, normed, ones, tri, logits_ready, shifted, exps_ready,
         rw_ready, rwT_ready, rwT_copied, spread, spread_copied) = (m.sem(n) for n in names)
        block = ctx.enter_context(nc.Block())

        @block.sync
        def _(sp):
            sp.dma_start(gain[:, :], row(dram["g2"])).then_inc(loaded, 16)
            sp.dma_start(wg[:, :, :], dram["w_gate"]).then_inc(loaded, 16)

        @block.gpsimd
        def _(pool):
            pool.memset(earlier[:, :, :], 1.0).then_inc(ones, 1)
            pool.wait_ge(ones, 1)
            pool.affine_select(out=earlier[:, :, :], in_=earlier[:, :, :], compare_op=ALU.is_gt, fill=0.0,
                               base=0, pattern=[[1, E], [-1, E]], channel_multiplier=0).then_inc(tri, 1)

        @block.tensor
        def _(pe):
            turn_tokens(pe, g["o"], turn, g["ident"], turned, copied, chunks)
            wo = g["wT"][:, QKV_TILES * KC * P:].rearrange("p (c n) -> p c n", n=D)
            project(pe, acc, oT, wo, copied, done, chunks)
            pe.wait_ge(normed, 1)
            for c in range(KC):
                pe.wait_ge(copied, chunks + c - 1)
                for t in range(TT):
                    ins = pe.transpose(turn[c % 2][:, t * P:(t + 1) * P], hn[:, t, c * P:(c + 1) * P], g["ident"][:, :])
                ins.then_inc(turned, 1)
            pe.wait_ge(loaded, 32)
            pe.wait_ge(copied, chunks + KC)
            for t in range(TT):
                for c in range(KC):
                    ins = pe.matmul(psL[:, t, :], g["aT"][:, c, t * P:(t + 1) * P], wg[:, c, :],
                                    start=(c == 0), stop=(c == KC - 1))
            ins.then_inc(logits_ready, 1)
            pe.wait_ge(rw_ready, 1)
            for t in range(TT):
                ins = pe.transpose(psR[0:E, t * P:(t + 1) * P], rw[:, t, :], g["ident"][:, :])
            ins.then_inc(rwT_ready, 1)
            pe.wait_ge(rwT_copied, 1)
            for x in range(E):
                wait(pe, spread_copied, x - 1)
                pe.matmul(turn[x % 2][:, :], pick[:, x, :], rwT[:, :], start=True, stop=True).then_inc(spread, 1)

        @block.scalar
        def _(act):
            copy_turned(act, oT, turn, turned, copied, chunks)
            norm_root(act, stats, 1)
            for c in range(KC):
                act.wait_ge(turned, chunks + c + 1)
                act.activation(g["aT"][:, c, :], turn[c % 2][:, :], ACT.Copy).then_inc(copied, 1)
            act.wait_ge(shifted, 1)
            act.activation(e[:, :, :], e[:, :, :], ACT.Exp).then_inc(exps_ready, 1)
            for x in range(E):
                act.wait_ge(spread, x + 1)
                act.activation(g["rw"][:, x, :], turn[x % 2][:, :], ACT.Copy).then_inc(spread_copied, 1)

        @block.vector
        def _(dve):
            step = Steps(dve, dve_step)
            for x in range(E):
                dve.tensor_copy(pick[:, x, :], g["ident"][0:E, x:x + 1].broadcast_to([E, P]))
            for t in range(TT):
                dve.wait_ge(done, t + 1)
                ins = dve.tensor_tensor(g["a"][:, t, :], g["a"][:, t, :], acc[t][:, :], ALU.add)
            step(ins)
            dve.wait_ge(loaded, 32)
            norm(step, stats, hn, g["a"], 1e-5, 1, gain=gain, rms=True)
            dve.sem_inc(normed, 1)
            step(dve.tensor_tensor(g["x"][:, :, :], g["x"][:, :, :], g["a"][:, :, :], ALU.add))
            dve.wait_ge(copied, chunks + KC)
            step(dve.tensor_copy(g["hn_hi"][:, :, :], g["aT"][:, :, :]))
            dve.tensor_tensor(g["hn_lo"][:, :, :], g["aT"][:, :, :], g["hn_hi"][:, :, :].bitcast(F32), ALU.subtract)
            dve.wait_ge(logits_ready, 1)
            step(dve.tensor_copy(logits[:, :, :], psL[:, :, :]))
            step(dve.tensor_reduce(col[:, 0, :], logits[:, :, :], AXX, ALU.max))
            step(dve.tensor_tensor(e[:, :, :], logits[:, :, :], last(col[:, 0, :], E), ALU.subtract))
            dve.sem_inc(shifted, 1)
            mine = last(logits[:, :, :], E)
            other = logits[:, :, :].unsqueeze(2).broadcast_to([P, TT, E, E])
            dve.tensor_tensor(above[:, :, :, :], other, mine, ALU.is_gt)
            step(dve.tensor_tensor(level[:, :, :, :], other, mine, ALU.is_equal))
            dve.wait_ge(tri, 1)
            step(dve.tensor_tensor(level[:, :, :, :], level[:, :, :, :],
                                   earlier[:, :, :].unsqueeze(1).broadcast_to([P, TT, E, E]), ALU.mult))
            step(dve.tensor_tensor(above[:, :, :, :], above[:, :, :, :], level[:, :, :, :], ALU.add))
            step(dve.tensor_reduce(picked[:, :, :], above[:, :, :, :], AXX, ALU.add))
            step(dve.tensor_scalar(picked[:, :, :], picked[:, :, :], 1.5, None, ALU.is_lt))
            dve.wait_ge(exps_ready, 1)
            step(dve.tensor_tensor(picked[:, :, :], picked[:, :, :], e[:, :, :], ALU.mult))
            step(dve.tensor_reduce(col[:, 1, :], picked[:, :, :], AXX, ALU.add))
            step(dve.reciprocal(col[:, 2, :], col[:, 1, :]))
            dve.tensor_tensor(rw[:, :, :], picked[:, :, :], last(col[:, 2, :], E), ALU.mult).then_inc(rw_ready, 1)
            dve.wait_ge(rwT_ready, 1)
            dve.tensor_copy(rwT[:, :], psR[0:E, :]).then_inc(rwT_copied, 1)



def phase_experts(nc, g, dram):
    N = E * FT
    UNIT = T
    with ExitStack() as ctx:
        m = Memory(nc, ctx, "moe_")
        raw = [m.sb(f"raw{i}", [P, BLK, GS]) for i in range(4)]
        deq = [m.sb(f"deq{i}", [P, BLK, GS]) for i in range(2)]
        scales = [m.sb(f"scales{i}", [P, 6, BLK]) for i in range(4)]
        wT_hi = [m.sb(f"wT_hi{i}", [P, 3, UNIT], F32R) for i in range(2)]
        wT_lo = [m.sb(f"wT_lo{i}", [P, 3, UNIT], F32R) for i in range(2)]
        silu, gate, up = (m.sb(n, [P, 2, T]) for n in ("silu", "gate", "up"))
        up_hi, up_lo = (m.sb(n, [P, 2, T], F32R) for n in ("up_hi", "up_lo"))
        zero = m.sb("zero", [P, D])
        psH1, psH3 = m.ps("psH1", [P, T]), m.ps("psH3", [P, T])
        psT = [m.ps(f"psT{i}", [P, T]) for i in range(2)]
        acc = [m.ps(f"acc{i}", [P, D]) for i in range(TT)]
        loaded = [m.sem(f"loaded{i}") for i in range(4)]
        names = ("scales_ready scaled rounded dequantised turned hi_copied lo_copied h_ready silu_done "
                 "gate_done up_done up_hi_done up_lo_done out_done closed dve_step zeroed begun").split()
        (scales_ready, scaled, rounded, dequantised, turned, hi_copied, lo_copied, h_ready, silu_done,
         gate_done, up_done, up_hi_done, up_lo_done, out_done, closed, dve_step, zeroed, begun) = (m.sem(n) for n in names)
        HI, LO, SCALE, INV, BASE, SHIFT = range(6)
        SCALE_STEPS = 8
        block = ctx.enter_context(nc.Block())

        def live(n):
            return not isinstance(n, int) or 0 <= n < N

        def steps(eng, each):
            for n in range(-4, 4):
                each(n, n % 4)
            with eng.Fori(1, N // 4 - 1) as i:
                for j in range(4):
                    each(4 * i + j, j)
            for n in range(N - 4, N + 1):
                each(n, n % 4)

        @block.sync
        def _(sp):
            def each(n, j):
                if live(n + 4):
                    wait(sp, scaled, 3 * n + 3)
                    sp.dma_start(raw[j][:, :, :], dram["w_moe"][ds(n + 4, 1), :, :].squeeze(0)
                                 .rearrange("p (b k) -> p b k", b=BLK)).then_inc(loaded[j], 16)
            steps(sp, each)

        @block.vector
        def _(dve):
            step = Steps(dve, dve_step)

            def scales_of(n, j):
                s = scales[j]
                dve.wait_ge(loaded[j], 4 * (n - j) + 16)
                step.n, step.k = n * SCALE_STEPS, 0
                dve.tensor_reduce(s[:, HI, :], raw[j][:, :, :], AXX, ALU.max)
                step(dve.tensor_reduce(s[:, LO, :], raw[j][:, :, :], AXX, ALU.min))
                step(dve.tensor_tensor(s[:, SCALE, :], s[:, HI, :], s[:, LO, :], ALU.subtract))
                step(dve.tensor_scalar(s[:, SCALE, :], s[:, SCALE, :], 1e-5, 1.0 / 15.0, ALU.max, ALU.mult))
                step(dve.reciprocal(s[:, INV, :], s[:, SCALE, :]))
                step(dve.tensor_tensor(s[:, BASE, :], s[:, LO, :], s[:, INV, :], ALU.mult))
                step(dve.tensor_scalar(s[:, BASE, :], s[:, BASE, :], -1.0, ROUND, ALU.mult, ALU.add))
                step(dve.tensor_scalar(s[:, BASE, :], s[:, BASE, :], ROUND, 0.0, ALU.subtract, ALU.max))
                step(dve.tensor_scalar(s[:, BASE, :], s[:, BASE, :], 15.0, None, ALU.min))
                dve.tensor_scalar(s[:, SHIFT, :], s[:, BASE, :], ROUND_UP, -1.0, ALU.add, ALU.mult)\
                   .then_inc(scales_ready, 1)
                assert step.k == SCALE_STEPS

            def round_unit(n, j, r):
                dve.wait_ge(scaled, 3 * n + r + 1)
                d = deq[j % 2][:, 4 * r:4 * r + 4, :]
                dve.tensor_scalar(d, d, 15.0, ROUND_UP, ALU.min, ALU.add).then_inc(rounded, 1)

            def lo_unit(n, j, r):
                dve.wait_ge(hi_copied, 3 * n + r + 1)
                dve.tensor_tensor(wT_lo[j % 2][:, r, :], psT[(3 * j + r) % 2][:, :],
                                  wT_hi[j % 2][:, r, :].bitcast(F32), ALU.subtract).then_inc(lo_copied, 1)

            def each(n, j):
                j1, j2, j3 = (j + 1) % 4, (j + 2) % 4, (j + 3) % 4
                if live(n):
                    lo_unit(n, j, 2)
                if live(n + 3):
                    scales_of(n + 3, j3)
                if live(n + 2):
                    round_unit(n + 2, j2, 0)
                if live(n + 1):
                    lo_unit(n + 1, j1, 0)
                if live(n):
                    dve.wait_ge(h_ready, 2 * n + 2)
                    wait(dve, up_done, n - 1)
                    dve.tensor_tensor(gate[:, j % 2, :], psH3[:, :], rw_row(g, n), ALU.mult).then_inc(gate_done, 1)
                if live(n + 2):
                    round_unit(n + 2, j2, 1)
                    round_unit(n + 2, j2, 2)
                if live(n + 1):
                    lo_unit(n + 1, j1, 1)
                if live(n):
                    dve.wait_ge(up_done, n + 1)
                    wait(dve, out_done, n - 1)
                    dve.tensor_copy(up_hi[:, j % 2, :], up[:, j % 2, :]).then_inc(up_hi_done, 1)
            steps(dve, each)
            dve.wait_ge(out_done, N)
            dve.wait_ge(closed, 1)
            for t in range(TT):
                dve.tensor_tensor(g["x"][:, t, :], g["x"][:, t, :], acc[t][:, :], ALU.add)

        @block.scalar
        def _(act):
            def scale_blocks(n, j, r):
                if r == 0:
                    act.wait_ge(scales_ready, n + 1)
                wait(act, turned, 3 * (n - 2) + r + 1)
                for b in range(4 * r, 4 * r + 4):
                    ins = act.activation(deq[j % 2][:, b, :], raw[j][:, b, :], ACT.Relu,
                                         bias=scales[j][:, BASE, b:b + 1], scale=scales[j][:, INV, b:b + 1])
                ins.then_inc(scaled, 1)

            def hi_unit(n, j, r):
                act.wait_ge(turned, 3 * n + r + 1)
                act.activation(wT_hi[j % 2][:, r, :], psT[(3 * j + r) % 2][:, :], ACT.Copy).then_inc(hi_copied, 1)

            def each(n, j):
                j1, j2 = (j + 1) % 4, (j + 2) % 4
                if live(n):
                    hi_unit(n, j, 2)
                if live(n + 2):
                    scale_blocks(n + 2, j2, 0)
                if live(n):
                    act.wait_ge(h_ready, 2 * n + 1)
                    wait(act, up_done, n - 1)
                    act.activation(silu[:, j % 2, :], psH1[:, :], ACT.Silu).then_inc(silu_done, 1)
                if live(n + 1):
                    hi_unit(n + 1, j1, 0)
                if live(n + 2):
                    scale_blocks(n + 2, j2, 1)
                    scale_blocks(n + 2, j2, 2)
                if live(n + 1):
                    hi_unit(n + 1, j1, 1)
            steps(act, each)

        @block.gpsimd
        def _(pool):
            pool.memset(zero[:, :], 0.0).then_inc(zeroed, 1)

            def dequantise(n, j, r):
                pool.wait_ge(rounded, 3 * n + r + 1)
                pool.sem_inc(begun, 1)
                s = scales[j]
                for b in range(4 * r, 4 * r + 4):
                    ins = pool.tensor_scalar(deq[j % 2][:, b, :], deq[j % 2][:, b, :], s[:, SHIFT, b:b + 1],
                                             s[:, SCALE, b:b + 1], ALU.add, ALU.mult)
                ins.then_inc(dequantised, 1)

            def each(n, j):
                if live(n):
                    pool.wait_ge(silu_done, n + 1)
                    pool.wait_ge(gate_done, n + 1)
                    wait(pool, up_lo_done, n - 1)
                    pool.tensor_tensor(up[:, j % 2, :], silu[:, j % 2, :], gate[:, j % 2, :], ALU.mult)\
                        .then_inc(up_done, 1)
                if live(n + 2):
                    dequantise(n + 2, (j + 2) % 4, 0)
                if live(n):
                    pool.wait_ge(up_hi_done, n + 1)
                    pool.tensor_tensor(up_lo[:, j % 2, :], up[:, j % 2, :], up_hi[:, j % 2, :].bitcast(F32),
                                       ALU.subtract).then_inc(up_lo_done, 1)
                if live(n + 2):
                    dequantise(n + 2, (j + 2) % 4, 1)
                    dequantise(n + 2, (j + 2) % 4, 2)
            steps(pool, each)

        @block.tensor
        def _(pe):
            pe.wait_ge(zeroed, 1)
            for t in range(TT):
                pe.matmul(acc[t][:, :], zero[:, 0:P], zero[:, :], start=True, stop=False, skip_group_check=True)

            def hidden(n, j, r, ps):
                pe.wait_ge(lo_copied, 3 * n + r + 1)
                wait(pe, silu_done if r == 0 else gate_done, n)
                hi, lo = wT_hi[j % 2], wT_lo[j % 2]
                for c in range(KC):
                    col = slice(c * P, (c + 1) * P)
                    pe.matmul(ps[:, :], hi[:, r, col], g["hn_hi"][:, c, :], start=(c == 0), stop=False)
                    pe.matmul(ps[:, :], hi[:, r, col], g["hn_lo"][:, c, :], start=False, stop=False)
                    ins = pe.matmul(ps[:, :], lo[:, r, col], g["hn_hi"][:, c, :], start=False, stop=(c == KC - 1))
                ins.then_inc(h_ready, 1)

            def turn_unit(n, j, r):
                pe.wait_ge(dequantised, 3 * n + r + 1)
                wait(pe, lo_copied, 3 * n + r - 1)
                for c in range(4):
                    ins = pe.transpose(psT[(3 * j + r) % 2][:, c * P:(c + 1) * P], deq[j % 2][:, 4 * r + c, :],
                                       g["ident"][:, :])
                ins.then_inc(turned, 1)

            def output(n, j):
                pe.wait_ge(lo_copied, 3 * n + 3)
                pe.wait_ge(up_lo_done, n + 1)
                w_hi, w_lo = wT_hi[j % 2][:, 2, :], wT_lo[j % 2][:, 2, :]
                for t in range(TT):
                    hi, lo = (u[:, j % 2, t * P:(t + 1) * P] for u in (up_hi, up_lo))
                    for a, b in ((hi, w_hi), (hi, w_lo), (lo, w_hi)):
                        ins = pe.matmul(acc[t][:, :], a, b, start=False, stop=False, skip_group_check=True)
                ins.then_inc(out_done, 1)

            def each(n, j):
                j1 = (j + 1) % 4
                if live(n):
                    hidden(n, j, 0, psH1)
                if live(n + 1):
                    turn_unit(n + 1, j1, 0)
                if live(n):
                    hidden(n, j, 1, psH3)
                if live(n + 1):
                    turn_unit(n + 1, j1, 1)
                if live(n - 1):
                    output(n - 1, (j - 1) % 4)
                if live(n + 1):
                    turn_unit(n + 1, j1, 2)
            steps(pe, each)
            for t in range(TT):
                ins = pe.matmul(acc[t][:, :], zero[:, 0:P], zero[:, :], start=False, stop=True, skip_group_check=True)
            ins.then_inc(closed, 1)


def rw_row(g, n):
    e = n // FT
    return g["rw"][:, e, :] if isinstance(e, int) else g["rw"][:, ds(e, 1), :].squeeze(1)


def phase_store(nc, src, out):
    with ExitStack() as ctx:
        stored = Memory(nc, ctx).sem("stored")
        block = ctx.enter_context(nc.Block())

        @block.sync
        def _(sp):
            sp.dma_start(out.rearrange("(t p) d -> p t d", p=P), src).then_inc(stored, 16)
            sp.wait_ge(stored, 16)


def program(nc, dram, out):
    with ExitStack() as ctx:
        m = Memory(nc, ctx)
        g = {"x": m.sb("x", [P, TT, D]), "a": m.sb("a", [P, TT, D]), "aT": m.sb("aT", [P, KC, T]),
             "ident": m.sb("ident", [P, P]), "causal": m.sb("causal", [P, TT, T])}
        with ExitStack() as early:
            me = Memory(nc, early)
            g["mask"] = me.sb("mask", [P, TT, T])
            g["key_mask"] = me.sb("key_mask", [P, HEADS * KEYS])
            g["o"] = me.sb("o", [P, TT, D])
            phase_start(nc, g, dram)
            phase_self_attention(nc, g, dram, "sa", causal=False, eps=0.0)
            phase_project(nc, g, dram, "sa", g["o"], dram["sa_wo"], "sa")
            phase_cross_attention(nc, g, dram, "ca")
            phase_project(nc, g, dram, "ca", g["o"], dram["ca_wo"], "ca")
            phase_mlp(nc, g, dram)
            phase_self_attention(nc, g, dram, "attn", causal=True, eps=1e-8)
            phase_project(nc, g, dram, "attn", g["o"], dram["attn_wo"], "attn")
        with ExitStack() as router:
            mr = Memory(nc, router)
            g["hn_hi"], g["hn_lo"] = mr.sb("hn_hi", [P, KC, T], F32R), mr.sb("hn_lo", [P, KC, T], F32R)
            g["rw"] = mr.sb("rw", [P, E, T])
            with ExitStack() as late:
                ml = Memory(nc, late)
                g["wT"] = ml.sb("wT", [P, (QKV_TILES * KC + KC * QH) * P])
                g["kv"] = ml.sb("kv", [P, TT, 2 * KVH, HD])
                g["qT"], g["kT"] = ml.sb("qT", [P, QH, T]), ml.sb("kT", [P, KVH, T])
                g["o"] = ml.sb("gqa_o", [P, TT, QH * HD])
                phase_quantise_weights(nc, g, dram)
                phase_qkv(nc, g, dram)
                phase_gqa_attention(nc, g)
                phase_router(nc, g, dram)
            phase_experts(nc, g, dram)
            phase_store(nc, g["x"][:, :, :], out)


def lay_out(i):
    import numpy as np
    xa, at = "L0_xattn_", "L0_attn_"
    c = np.ascontiguousarray
    out = {"x": c(i["x"][0]), "mask": c(i["mask_Bx1xSxS_ik0"][0, 0])}
    out["key_mask"] = c(i["mask_Bx1x1xS2_if1"][0, 0, 0, :HEADS * KEYS].reshape(KEYS, HEADS).T).reshape(-1)
    out["enc"] = c(i["ctx_1024"][0, :HEADS * KEYS].reshape(KEYS, HEADS, D).transpose(1, 2, 0))
    for n in ("sa_wq", "sa_bq", "sa_wk", "sa_bk", "sa_wv", "sa_bv", "sa_wo", "sa_bo",
              "ca_wq", "ca_bq", "ca_wk", "ca_bk", "ca_wv", "ca_bv", "ca_wo", "ca_bo",
              "ffn_w1", "ffn_b1", "ffn_w2", "ffn_b2", "ln1_g", "ln1_b", "ln2_g", "ln2_b", "ln3_g", "ln3_b"):
        out[n] = c(i[xa + n])
    for n in ("sa_bq", "sa_bk", "ca_bq", "ca_bk", "ffn_b1"):
        out[n] = c(out[n].reshape(-1, P).T)
    out["attn_wq"], out["attn_wo"] = c(i[at + "Wq"].T), c(i[at + "Wo"].T)
    out["attn_wk"], out["attn_wv"] = c(i[at + "Wkv"][:D].T), c(i[at + "Wkv"][D:].T)
    f = "L0_ffn_"
    out["g1"], out["g2"] = c(i[f + "g1"]), c(i[f + "g2"])
    qkv = np.concatenate([i[f + "w_q"], i[f + "w_k"], i[f + "w_v"]]).reshape(QKV_TILES, P, KC, GS)
    wo = i[f + "w_o"].reshape(KC, P, QH, GS)
    blocks = np.concatenate([w.transpose(2, 0, 1, 3).reshape(-1, P, GS) for w in (qkv, wo)])
    out["w_attn"] = c(blocks.reshape(-1, 16, P, GS).transpose(0, 2, 1, 3)).reshape(-1, P, 16 * GS)
    out["w_gate"] = c(i[f + "w_gate"].T.reshape(KC, P, E).transpose(1, 0, 2))
    w1, w3 = (i[f + w].reshape(E * FT, P, KC * GS) for w in ("w1", "w3"))
    w2 = i[f + "w2"].reshape(E, KC, P, FT, GS).transpose(0, 3, 2, 1, 4).reshape(E * FT, P, KC * GS)
    out["w_moe"] = np.concatenate([w1, w3, w2], axis=2)
    inv = (1.0 / np.float32(1e6) ** (np.arange(0, HD, 2, dtype=np.float32) / np.float32(HD))).astype(np.float32)
    angle = np.arange(T, dtype=np.float32)[:, None] * inv[None, :]
    out["cos_k"], out["sin_k"] = np.cos(angle), np.sin(angle)
    scale = np.float32(-(HD ** -0.5))
    out["cos_q"], out["sin_q"] = out["cos_k"] * scale, out["sin_k"] * scale
    return out



def kernel(**inputs):
    import numpy as np
    import concourse.bacc as bacc
    from concourse.bass_utils import run_bass_kernel_spmd

    arrays = {f"{n}_dram": a for n, a in lay_out({k: np.asarray(v) for k, v in inputs.items()}).items()}
    nc = bacc.Bacc("TRN2", target_bir_lowering=False, num_devices=1)
    dram = {n[:-5]: nc.dram_tensor(n, a.shape, mybir.dt.from_np(a.dtype), kind="ExternalInput").ap()
            for n, a in arrays.items()}
    out = nc.dram_tensor("out_dram", (T, D), F32, kind="ExternalOutput").ap()
    program(nc, dram, out)
    result = run_bass_kernel_spmd(nc, [arrays], core_ids=[0])
    return result.results[0]["out_dram"].reshape(1, T, D)
```

```python
from contextlib import ExitStack

import concourse.bass as bass
from concourse import mybir

F32 = mybir.dt.float32
F32R = mybir.dt.float32r
I32 = mybir.dt.int32
ALU = mybir.AluOpType
ACT = mybir.ActivationFunctionType
AXX = mybir.AxisListType.X
ds = bass.ds

P = 128
T = 512
TT = T // P
D = 512
KC = D // P
HEADS = 16
DH = D // HEADS
HPG = P // DH
GROUPS = HEADS // HPG
START = 1
KEYS = 256
FF = 2048
QH, KVH, HD = 8, 2, 128
E, FFN = 8, 1792
FT = FFN // P
GS = 128
BLK = 12
QKV_TILES = (QH + 2 * KVH) * HD // P
BIG = 1.0e30
HUGE = 3.0e38
ROUND = 1.5 * 2.0 ** 23
ROUND_UP = 2.0 ** 23


def wait(eng, sem, value):
    if isinstance(value, int) and value <= 0:
        return
    eng.wait_ge(sem, value)


class Steps:

    def __init__(self, eng, sem, start=0):
        self.eng, self.sem, self.n, self.k = eng, sem, start, 0

    def __call__(self, ins):
        self.n, self.k = self.n + 1, self.k + 1
        ins.then_inc(self.sem, 1)
        self.eng.wait_ge(self.sem, self.n)


class Memory:

    def __init__(self, nc, ctx, prefix=""):
        self.nc, self.ctx, self.prefix = nc, ctx, prefix

    def sb(self, name, shape, dtype=F32):
        return self.ctx.enter_context(self.nc.sbuf_tensor(self.prefix + name, shape, dtype))

    def ps(self, name, shape, dtype=F32):
        return self.ctx.enter_context(self.nc.psum_tensor(self.prefix + name, shape, dtype))

    def sem(self, name):
        sem = self.nc.alloc_semaphore(self.prefix + name)
        self.ctx.callback(self.clear, sem)
        return sem

    def clear(self, sem):
        self.nc.gpsimd.sem_clear(sem)
        self.nc.release_semaphore(sem)


def row(ap):
    return ap.rearrange("(a n) -> a n", a=1).broadcast_to([P, ap.shape[0]])


def middle(ap, n):
    return ap.unsqueeze(1).broadcast_to([ap.shape[0], n, ap.shape[1]])


def last(ap, n):
    return ap.unsqueeze(len(ap.shape)).broadcast_to([*ap.shape, n])



def norm_stats(step, stats, x, eps, rms=False):
    dve = step.eng
    for t in range(TT):
        ins = dve.bn_stats(stats["raw"][:, t, :], x[:, t, :])
    step(ins)
    for t in range(TT):
        ins = dve.bn_aggr(stats["mv"][:, t, :], stats["raw"][:, t, :])
    step(ins)
    mean, var = stats["mv"][:, :, 0], stats["mv"][:, :, 1]
    if rms:
        step(dve.tensor_tensor(stats["tmp"], mean, mean, ALU.mult))
        step(dve.scalar_tensor_tensor(stats["v"], var, eps, stats["tmp"], ALU.add, ALU.add))
    else:
        step(dve.tensor_scalar(stats["v"], var, eps, None, ALU.add))


def norm_scale(step, stats):
    dve, r, t, v = step.eng, stats["r"], stats["tmp"], stats["v"]
    step(dve.reciprocal(r, stats["root"]))
    step(dve.tensor_tensor(t, r, r, ALU.mult))
    step(dve.tensor_tensor(t, t, v, ALU.mult))
    step(dve.tensor_scalar(t, t, -0.5, 1.5, ALU.mult, ALU.add))
    step(dve.tensor_tensor(r, r, t, ALU.mult))


def norm_apply(step, stats, y, x, gain=None, shift=None, rms=False):
    dve = step.eng
    for t in range(TT):
        if rms:
            ins = dve.tensor_scalar(y[:, t, :], x[:, t, :], stats["r"][:, t:t + 1], None, ALU.mult)
        else:
            ins = dve.tensor_scalar(y[:, t, :], x[:, t, :], stats["mv"][:, t, 0:1],
                                    stats["r"][:, t:t + 1], ALU.subtract, ALU.mult)
    step(ins)
    if gain is not None:
        step(dve.tensor_tensor(y[:, :, :], y[:, :, :], middle(gain[:, :], TT), ALU.mult))
    if shift is not None:
        step(dve.tensor_tensor(y[:, :, :], y[:, :, :], middle(shift[:, :], TT), ALU.add))


def norm(step, stats, y, x, eps, count, gain=None, shift=None, rms=False):
    norm_stats(step, stats, x, eps, rms)
    step.eng.sem_inc(stats["var_ready"], 1)
    step.eng.wait_ge(stats["root_ready"], count)
    norm_scale(step, stats)
    norm_apply(step, stats, y, x, gain, shift, rms)


def norm_root(act, stats, count):
    act.wait_ge(stats["var_ready"], count)
    act.activation(stats["root"], stats["v"], ACT.Sqrt).then_inc(stats["root_ready"], 1)


def stats_tiles(mem):
    small = mem.sb("norm_small", [P, 4, TT])
    return {"var_ready": mem.sem("var_ready"), "root_ready": mem.sem("root_ready"),
            "raw": mem.sb("norm_raw", [P, TT, 6]), "mv": mem.sb("norm_mv", [P, TT, 2]),
            "v": small[:, 0, :], "root": small[:, 1, :], "r": small[:, 2, :], "tmp": small[:, 3, :]}



def phase_start(nc, g, dram):
    with ExitStack() as ctx:
        m = Memory(nc, ctx, "start_")
        stats = stats_tiles(m)
        mask_raw = m.sb("mask_raw", [P, TT, T], I32)
        key_raw = m.sb("key_raw", [P, HEADS * KEYS], I32)
        x_loaded, consts_loaded = m.sem("x_loaded"), m.sem("consts_loaded")
        dve_step, zeroed, ident_made = m.sem("dve_step"), m.sem("zeroed"), m.sem("ident_made")
        normed, turned, copied = m.sem("normed"), m.sem("turned"), m.sem("copied")
        turn = [m.ps(f"turn{i}", [P, T]) for i in range(2)]
        block = ctx.enter_context(nc.Block())

        @block.sync
        def _(sp):
            sp.dma_start(g["x"][:, :, :], dram["x"].rearrange("(t p) d -> p t d", p=P)).then_inc(x_loaded, 16)
            sp.dma_start(mask_raw[:, :, :], dram["mask"].rearrange("(t p) k -> p t k", p=P)).then_inc(consts_loaded, 16)
            sp.dma_start(key_raw[:, :], row(dram["key_mask"])).then_inc(consts_loaded, 16)

        @block.gpsimd
        def _(pool):
            pool.memset(g["ident"][:, :], 0.0).then_inc(zeroed, 1)
            pool.memset(g["causal"][:, :, :], 0.0).then_inc(zeroed, 1)
            pool.wait_ge(zeroed, 2)
            pool.affine_select(out=g["ident"][:, :], in_=g["ident"][:, :], compare_op=ALU.not_equal, fill=1.0,
                               base=0, pattern=[[-1, P]], channel_multiplier=1).then_inc(ident_made, 1)
            pool.affine_select(out=g["causal"][:, :, :], in_=g["causal"][:, :, :], compare_op=ALU.is_ge, fill=BIG,
                               base=0, pattern=[[P, TT], [-1, T]], channel_multiplier=1)

        @block.vector
        def _(dve):
            step = Steps(dve, dve_step)
            dve.wait_ge(x_loaded, 16)
            norm(step, stats, g["a"], g["x"], 1e-5, 1)
            dve.sem_inc(normed, 1)
            dve.wait_ge(consts_loaded, 32)
            dve.tensor_scalar(g["mask"][:, :, :], mask_raw[:, :, :], 0.0, BIG, ALU.is_equal, ALU.mult)
            dve.tensor_scalar(g["key_mask"][:, :], key_raw[:, :], 0.0, BIG, ALU.is_equal, ALU.mult)

        @block.tensor
        def _(pe):
            pe.wait_ge(ident_made, 1)
            pe.wait_ge(normed, 1)
            turn_tokens(pe, g["a"], turn, g["ident"], turned, copied)

        @block.scalar
        def _(act):
            norm_root(act, stats, 1)
            copy_turned(act, g["aT"], turn, turned, copied)


def turn_tokens(pe, src, turn, ident, turned, copied, chunks=KC):
    for c in range(chunks):
        wait(pe, copied, c - 1)
        for t in range(TT):
            ins = pe.transpose(turn[c % 2][:, t * P:(t + 1) * P], src[:, t, c * P:(c + 1) * P], ident[:, :])
        ins.then_inc(turned, 1)


def copy_turned(act, dst, turn, turned, copied, chunks=KC):
    for c in range(chunks):
        act.wait_ge(turned, c + 1)
        act.activation(dst[:, c, :], turn[c % 2][:, :], ACT.Copy).then_inc(copied, 1)



class Core:
    LAG = 3
    BUFFERS = 4
    SHIFTED0, TURNED0, COPIED0, VALUES0, OUT0 = 2, 4, 2, 2, 2

    def __init__(self, m, heads, qk, v, bias, keys, width, per_out, out, eps):
        self.units = [(h, t) for h in range(heads) for t in range(TT)]
        self.n, self.heads, self.width, self.per_out, self.eps = len(self.units), heads, width, per_out, eps
        self.qk, self.v, self.bias, self.keys, self.out = qk, v, bias, keys, out
        self.banks = 1 if per_out > 1 else 2
        self.shifted = m.sb("shifted", [P, self.BUFFERS, T])
        self.least = m.sb("least", [P, self.n])
        self.row_sum = m.sb("row_sum", [P, self.n])
        self.row_inv = m.sb("row_inv", [P, self.n])
        self.probsT = m.sb("probsT", [P, 2, TT, T])
        self.psS = [m.ps(f"psS{i}", [P, T]) for i in range(2)]
        self.psT = [m.ps(f"psT{i}", [P, T]) for i in range(2)]
        self.psO = [m.ps(f"psO{i}", [P, T]) for i in range(self.banks)]
        (self.scores_ready, self.begun, self.shifted_ready, self.exps_done, self.probs_ready, self.turned,
         self.probsT_copied, self.values_done, self.out_copied) = (m.sem(n) for n in (
             "scores_ready", "begun", "shifted_ready", "exps_done", "probs_ready", "turned",
             "probsT_copied", "values_done", "out_copied"))

    def prime_vector(self, dve):
        dve.sem_inc(self.shifted_ready, self.SHIFTED0)

    def prime_scalar(self, act):
        act.sem_inc(self.probsT_copied, self.COPIED0)
        act.sem_inc(self.out_copied, self.OUT0)

    def prime_tensor(self, pe):
        pe.sem_inc(self.turned, self.TURNED0)
        pe.sem_inc(self.values_done, self.VALUES0)

    def value_step(self, h):
        return min(TT * h + TT - 1 + self.LAG + 2, self.n + self.LAG)

    @property
    def steps(self):
        return self.n + self.LAG + 1

    def ends_bank(self, h):
        return (h + 1) % self.per_out == 0

    def tensor(self, pe, g, s, ident, v_ready=None):
        base = g * self.n
        if s < self.n:
            h, t = self.units[s]
            n = self.keys(t)
            q_hi, q_lo, k_hi, k_lo = self.qk(h)
            q = slice(t * P, (t + 1) * P)
            pe.wait_ge(self.shifted_ready, base + s - 1 + self.SHIFTED0)
            ps = self.psS[s % 2][:, 0:n]
            pe.matmul(ps, q_hi[:, q], k_hi[:, 0:n], start=True, stop=False)
            pe.matmul(ps, q_hi[:, q], k_lo[:, 0:n], start=False, stop=False)
            pe.matmul(ps, q_lo[:, q], k_hi[:, 0:n], start=False, stop=True).then_inc(self.scores_ready, 1)
        u = s - self.LAG
        if 0 <= u < self.n:
            h, t = self.units[u]
            pe.wait_ge(self.probs_ready, base + u + 1)
            pe.wait_ge(self.probsT_copied, base + u - 1 + self.COPIED0)
            for c in range(self.keys(t) // P):
                ins = pe.transpose(self.psT[u % 2][:, c * P:(c + 1) * P],
                                   self.shifted[:, u % self.BUFFERS, c * P:(c + 1) * P], ident[:, :])
            ins.then_inc(self.turned, 1)
        for h in range(self.heads):
            if self.value_step(h) != s:
                continue
            o = h // self.per_out
            if h % self.per_out == 0:
                pe.wait_ge(self.out_copied, g * (self.heads // self.per_out) + o + 1 - self.banks + self.OUT0)
            if h == 0 and v_ready is not None:
                pe.wait_ge(*v_ready)
            pe.wait_ge(self.probsT_copied, base + TT * h + TT + self.COPIED0)
            row = (h % self.per_out) * self.width
            chunks = self.keys(TT - 1) // P
            for c in range(chunks):
                first = next(t for t in range(TT) if self.keys(t) > c * P) * P
                ins = pe.matmul(self.psO[o % self.banks][row:row + self.width, first:T], self.v(h, c),
                                self.probsT[:, h % 2, c, first:T], start=(c == 0), stop=(c == chunks - 1))
            ins.then_inc(self.values_done, 1)

    def vector(self, dve, g, s, step):
        base = g * self.n
        if s < self.n:
            h, t = self.units[s]
            n = self.keys(t)
            dve.wait_ge(self.scores_ready, base + s + 1)
            dve.wait_ge(self.turned, base + s - 3 + self.TURNED0)
            dve.sem_inc(self.begun, 1)
            dve.tensor_tensor_reduce(self.shifted[:, s % self.BUFFERS, 0:n], self.psS[s % 2][:, 0:n],
                                     self.bias(h, t, n), 1.0, HUGE, ALU.add, ALU.min,
                                     self.least[:, s:s + 1]).then_inc(self.shifted_ready, 1)
        u = s - 1
        if 0 <= u < self.n:
            n = self.keys(self.units[u][1])
            dve.wait_ge(self.exps_done, base + u + 1)
            total, inv = self.row_sum[:, u:u + 1], self.row_inv[:, u:u + 1]
            if self.eps:
                step(dve.tensor_scalar(total, total, self.eps, None, ALU.add))
            step(dve.reciprocal(inv, total))
            p = self.shifted[:, u % self.BUFFERS, 0:n]
            dve.tensor_scalar(p, p, inv, None, ALU.mult).then_inc(self.probs_ready, 1)

    @property
    def vector_steps(self):
        return self.n * (2 if self.eps else 1)

    def scalar(self, act, g, s):
        base = g * self.n
        if s < self.n:
            n = self.keys(self.units[s][1])
            act.wait_ge(self.shifted_ready, base + s + 1 + self.SHIFTED0)
            act.activation(self.shifted[:, s % self.BUFFERS, 0:n], self.shifted[:, s % self.BUFFERS, 0:n], ACT.Exp,
                           bias=self.least[:, s:s + 1], scale=-1.0,
                           accum_out=self.row_sum[:, s:s + 1]).then_inc(self.exps_done, 1)
        u = s - self.LAG
        if 0 <= u < self.n:
            h, t = self.units[u]
            chunks = self.keys(t) // P
            act.wait_ge(self.turned, base + u + 1 + self.TURNED0)
            act.wait_ge(self.values_done, g * self.heads + h - 1 + self.VALUES0)
            act.activation(self.probsT[:, h % 2, 0:chunks, t * P:(t + 1) * P],
                           self.psT[u % 2][:, 0:chunks * P].rearrange("p (c q) -> p c q", q=P), ACT.Copy)\
               .then_inc(self.probsT_copied, 1)
        for h in range(self.heads):
            if self.ends_bank(h) and min(self.value_step(h) + 1, self.n + self.LAG) == s:
                o = h // self.per_out
                act.wait_ge(self.values_done, g * self.heads + h + 1 + self.VALUES0)
                act.activation(self.out(g, o), self.psO[o % self.banks][:, :], ACT.Copy).then_inc(self.out_copied, 1)


class Split:

    def __init__(self, m, keys):
        self.q, self.k = m.sb("q", [P, T]), m.sb("k", [P, keys])
        self.q_hi, self.q_lo = m.sb("q_hi", [P, T], F32R), m.sb("q_lo", [P, T], F32R)
        self.k_hi, self.k_lo = m.sb("k_hi", [P, keys], F32R), m.sb("k_lo", [P, keys], F32R)
        self.ready = m.sem("qk_split")

    def head(self, h):
        rows = slice(h * DH, (h + 1) * DH)
        return self.q_hi[rows, :], self.q_lo[rows, :], self.k_hi[rows, :], self.k_lo[rows, :]

    def vector(self, step):
        dve = step.eng
        dve.tensor_copy(self.q_hi[:, :], self.q[:, :])
        step(dve.tensor_copy(self.k_hi[:, :], self.k[:, :]))
        dve.tensor_tensor(self.q_lo[:, :], self.q[:, :], self.q_hi[:, :].bitcast(F32), ALU.subtract)
        dve.tensor_tensor(self.k_lo[:, :], self.k[:, :], self.k_hi[:, :].bitcast(F32), ALU.subtract)\
           .then_inc(self.ready, 1)



def phase_attention(nc, g, dram, name, kind, eps=0.0):
    strided = kind == "strided"
    keys = KEYS if strided else T
    with ExitStack() as ctx:
        m = Memory(nc, ctx, name + "_")
        has_bias = name + "_bq" in dram
        w = {c: m.sb(f"w{c}", [P, KC, P]) for c in "qkv"}
        split = Split(m, keys)
        v = m.sb("v", [P, keys // P * P if not strided else HPG * (keys // P) * DH])
        if strided:
            enc = m.sb("enc", [P, HPG, KC, KEYS])
            v_view = v[:, :].rearrange("p (h c d) -> p h c d", h=HPG, d=DH)
            v_of = lambda h, c: v_view[:, h, c, :]
            group_bias = m.sb("group_bias", [P, HPG * KEYS])
            bias = lambda h, t, n: group_bias[:, h * KEYS:(h + 1) * KEYS]
        else:
            v_view = v[:, :].rearrange("p (c n) -> p c n", n=P)
            v_of = lambda h, c: v_view[:, c, h * DH:(h + 1) * DH]
            bias = lambda h, t, n: g["causal" if kind == "causal" else "mask"][:, t, 0:n]
        if has_bias:
            bq, bk, bq_scaled = (m.sb(n, [P, GROUPS]) for n in ("bq", "bk", "bq_scaled"))
            bv = m.sb("bv", [P, D])
        core = Core(m, HPG, qk=split.head, v=v_of, bias=bias,
                    keys=(lambda t: (t + 1) * P) if kind == "causal" else (lambda t: keys),
                    width=DH, per_out=HPG, out=lambda j, o: g["oT"][:, ds(j, 1), :].squeeze(1), eps=eps)
        psQ, psK, psV = m.ps("psQ", [P, T]), m.ps("psK", [P, T]), m.ps("psV", [P, T])
        (bias_loaded, bias_scaled, w_loaded, q_ready, k_ready, v_ready, qk_copied, v_copied, bias_copied,
         dve_step) = (m.sem(n) for n in ("bias_loaded", "bias_scaled", "w_loaded", "q_ready", "k_ready",
                                         "v_ready", "qk_copied", "v_copied", "bias_copied", "dve_step"))
        loads = 3 + (HPG if strided else 0)
        Q_AT, K_AT, V_AT, COPY_Q_AT, COPY_K_AT, COPY_V_AT = 5, 8, 11, 8, 12, 4
        block = ctx.enter_context(nc.Block())

        def groups(eng, body):
            with eng.Fori(0, GROUPS - 1) as j:
                body(j, True)
            body(GROUPS - 1, False)

        @block.sync
        def _(sp):
            def load(j):
                for c in "qkv":
                    src = dram[f"{name}_w{c}"].rearrange("(c p) n -> p c n", p=P)
                    sp.dma_start(w[c][:, :, :], src[:, :, ds(j * P, P)]).then_inc(w_loaded, 16)
                if strided:
                    enc_src = dram["enc"].rearrange("(j h) (c p) n -> p j h c n", h=HPG, p=P)
                    for h in range(HPG):
                        sp.dma_start(enc[:, h, :, :], enc_src[:, ds(j, 1), h, :, :].squeeze(1)).then_inc(w_loaded, 16)
            load(0)
            if has_bias:
                sp.dma_start(bq[:, :], dram[name + "_bq"]).then_inc(bias_loaded, 16)
                sp.dma_start(bk[:, :], dram[name + "_bk"]).then_inc(bias_loaded, 16)
                sp.dma_start(bv[:, :], row(dram[name + "_bv"])).then_inc(bias_loaded, 16)
            with sp.Fori(1, GROUPS) as j:
                sp.wait_ge(v_ready, j)
                load(j)

        @block.tensor
        def _(pe):
            def project_q(j):
                pe.wait_ge(w_loaded, 16 * loads * j + 16 * loads)
                for i in range(KC):
                    ins = pe.matmul(psQ[:, :], w["q"][:, i, :], g["aT"][:, i, :], start=(i == 0), stop=(i == KC - 1))
                ins.then_inc(q_ready, 1)

            def project_k():
                for h in range(HPG) if strided else [None]:
                    rows = slice(0, P) if h is None else slice(h * DH, (h + 1) * DH)
                    for i in range(KC):
                        src = g["aT"][:, i, :] if h is None else enc[:, h, i, :]
                        ins = pe.matmul(psK[rows, 0:keys], w["k"][:, i, rows], src, start=(i == 0), stop=(i == KC - 1))
                ins.then_inc(k_ready, 1)

            def project_v():
                if strided:
                    for h in range(HPG):
                        for c in range(KEYS // P):
                            col = (h * (KEYS // P) + c) * DH
                            for i in range(KC):
                                ins = pe.matmul(psV[:, col:col + DH], enc[:, h, i, c * P:(c + 1) * P],
                                                w["v"][:, i, h * DH:(h + 1) * DH], start=(i == 0), stop=(i == KC - 1))
                else:
                    for t in range(TT):
                        for i in range(KC):
                            ins = pe.matmul(psV[:, t * P:(t + 1) * P], g["aT"][:, i, t * P:(t + 1) * P],
                                            w["v"][:, i, :], start=(i == 0), stop=(i == KC - 1))
                ins.then_inc(v_ready, 1)

            def body(j, more):
                pe.wait_ge(split.ready, j + 1)
                for s in range(core.steps):
                    core.tensor(pe, j, s, g["ident"], v_ready=(v_copied, j + 1))
                    if more and s == Q_AT:
                        project_q(j + 1)
                    if more and s == K_AT:
                        project_k()
                    if more and s == V_AT:
                        project_v()
            core.prime_tensor(pe)
            project_q(0)
            project_k()
            project_v()
            groups(pe, body)

        @block.scalar
        def _(act):
            def copy_q(j):
                act.wait_ge(q_ready, j + 1)
                if has_bias:
                    act.activation(split.q[:, :], psQ[:, :], ACT.Identity, bias=bq_scaled[:, ds(j, 1)],
                                   scale=-DH ** -0.5).then_inc(qk_copied, 1)
                else:
                    act.activation(split.q[:, :], psQ[:, :], ACT.Copy, scale=-DH ** -0.5).then_inc(qk_copied, 1)

            def copy_k(j):
                act.wait_ge(k_ready, j + 1)
                if has_bias:
                    act.activation(split.k[:, :], psK[:, 0:keys], ACT.Identity, bias=bk[:, ds(j, 1)]).then_inc(qk_copied, 1)
                else:
                    act.activation(split.k[:, :], psK[:, 0:keys], ACT.Copy).then_inc(qk_copied, 1)

            def copy_bias(j):
                if strided:
                    act.activation(group_bias[:, :], g["key_mask"][:, ds(j * (HPG * KEYS), HPG * KEYS)], ACT.Copy)\
                       .then_inc(bias_copied, 1)

            def body(j, more):
                for s in range(core.steps):
                    core.scalar(act, j, s)
                    if more and s == COPY_Q_AT:
                        copy_q(j + 1)
                    if more and s == COPY_K_AT:
                        copy_k(j + 1)
                    if more and s == core.n - 1:
                        copy_bias(j + 1)
            core.prime_scalar(act)
            copy_bias(0)
            if has_bias:
                act.wait_ge(bias_loaded, 48)
                act.activation(bq_scaled[:, :], bq[:, :], ACT.Copy, scale=-DH ** -0.5).then_inc(bias_scaled, 1)
                act.wait_ge(bias_scaled, 1)
            copy_q(0)
            copy_k(0)
            groups(act, body)

        @block.vector
        def _(dve):
            step = Steps(dve, dve_step)
            per = core.vector_steps + 1

            def copy_v(j):
                dve.wait_ge(v_ready, j + 1)
                dve.wait_ge(core.values_done, j * HPG + core.VALUES0)
                if strided:
                    pv = psV[:, 0:HPG * (KEYS // P) * DH].rearrange("p (h c d) -> p h c d", h=HPG, d=DH)
                    for c in range(KEYS // P):
                        ins = dve.tensor_tensor(v_view[:, :, c, :], pv[:, :, c, :],
                                                bv[:, ds(j * P, P)].rearrange("p (h d) -> p h d", h=HPG), ALU.add)
                elif has_bias:
                    ins = dve.tensor_tensor(v_view, psV[:, :].rearrange("p (t n) -> p t n", t=TT),
                                            middle(bv[:, ds(j * P, P)], TT), ALU.add)
                else:
                    ins = dve.tensor_copy(v[:, :], psV[:, :])
                ins.then_inc(v_copied, 1)

            def body(j, more):
                step.n, step.k = j * per + 1, 0
                if strided:
                    dve.wait_ge(bias_copied, j + 1)
                for s in range(core.n + 1):
                    core.vector(dve, j, s, step)
                    if s == COPY_V_AT:
                        copy_v(j)
                if more:
                    dve.wait_ge(qk_copied, 2 * j + 4)
                    dve.wait_ge(core.scores_ready, (j + 1) * core.n)
                    split.vector(step)
                    assert step.k == per
            core.prime_vector(dve)
            if has_bias:
                dve.wait_ge(bias_loaded, 48)
            dve.wait_ge(qk_copied, 2)
            split.vector(step)
            groups(dve, body)



def project(pe, acc, oT, w, done, chunks):
    for t in range(TT):
        for c in range(chunks):
            ins = pe.matmul(acc[t][:, :], oT[:, c, t * P:(t + 1) * P], w[:, c, :], start=(c == 0), stop=(c == chunks - 1))
        ins.then_inc(done, 1)


def phase_project(nc, g, dram, name, w_src, last_of):
    with ExitStack() as ctx:
        m = Memory(nc, ctx, name + "_out_")
        stats = stats_tiles(m)
        w = m.sb("w", [P, KC, D])
        turn = [m.ps(f"turn{i}", [P, T]) for i in range(2)]
        acc = [m.ps(f"acc{i}", [P, D]) for i in range(TT)]
        loaded, turned, copied = m.sem("loaded"), m.sem("turned"), m.sem("copied")
        done, dve_step, normed = m.sem("done"), m.sem("dve_step"), m.sem("normed")
        rows = {}
        if last_of in ("sa", "ca"):
            rows = {k: m.sb(k, [P, D]) for k in ("bo", "gain", "shift")}
            ln = {"sa": "ln1", "ca": "ln2"}[last_of]
            row_src = {"bo": f"{name}_bo", "gain": f"{ln}_g", "shift": f"{ln}_b"}
        else:
            rows, row_src = {"gain": m.sb("gain", [P, D])}, {"gain": "g1"}
            xn = m.sb("xn", [P, TT, D])
        block = ctx.enter_context(nc.Block())

        @block.sync
        def _(sp):
            sp.dma_start(w[:, :, :], w_src.rearrange("(c p) n -> p c n", p=P)).then_inc(loaded, 16)
            for k, tile in rows.items():
                sp.dma_start(tile[:, :], row(dram[row_src[k]])).then_inc(loaded, 16)

        @block.tensor
        def _(pe):
            pe.wait_ge(loaded, 16 * (1 + len(rows)))
            project(pe, acc, g["oT"], w, done, KC)
            pe.wait_ge(normed, 1)
            turn_tokens(pe, xn if last_of == "attn" else g["a"], turn, g["ident"], turned, copied)

        @block.scalar
        def _(act):
            norm_root(act, stats, 1)
            if last_of == "attn":
                norm_root(act, stats, 2)
            copy_turned(act, g["aT"], turn, turned, copied)

        @block.vector
        def _(dve):
            step = Steps(dve, dve_step)
            dve.wait_ge(loaded, 16 * (1 + len(rows)))
            if last_of in ("sa", "ca"):
                step(dve.tensor_tensor(g["a"][:, :, :], g["a"][:, :, :], middle(rows["bo"][:, :], TT), ALU.add))
            into = g["x"] if last_of == "attn" else g["a"]
            for t in range(TT):
                dve.wait_ge(done, t + 1)
                ins = dve.tensor_tensor(into[:, t, :], into[:, t, :], acc[t][:, :], ALU.add)
            step(ins)
            if last_of in ("sa", "ca"):
                norm(step, stats, g["a"], g["a"], 1e-6, 1, gain=rows["gain"], shift=rows["shift"])
            else:
                norm(step, stats, g["a"], g["x"], 1e-5, 1)
                norm(step, stats, xn, g["a"], 1e-5, 2, gain=rows["gain"], rms=True)
            dve.sem_inc(normed, 1)



def phase_mlp(nc, g, dram):
    with ExitStack() as ctx:
        m = Memory(nc, ctx, "mlp_")
        stats = stats_tiles(m)
        PAIRS = FF // (2 * P)
        w1, w2 = m.sb("w1", [P, KC, 2 * P]), m.sb("w2", [P, 2, D])
        b1 = m.sb("b1", [P, FF // P])
        rows = {k: m.sb(k, [P, D]) for k in ("b2", "gain", "shift")}
        hT = m.sb("hT", [P, 2, T])
        zero = m.sb("zero", [P, D])
        psH = [m.ps(f"psH{i}", [P, T]) for i in range(2)]
        acc = [m.ps(f"acc{i}", [P, D]) for i in range(TT)]
        turn = [m.ps(f"turn{i}", [P, T]) for i in range(2)]
        rows_loaded, w1_loaded, w2_loaded = m.sem("rows_loaded"), m.sem("w1_loaded"), m.sem("w2_loaded")
        zeroed, h_ready, relu_done, out_done = m.sem("zeroed"), m.sem("h_ready"), m.sem("relu_done"), m.sem("out_done")
        dve_step, normed, turned, copied = m.sem("dve_step"), m.sem("normed"), m.sem("turned"), m.sem("copied")
        block = ctx.enter_context(nc.Block())

        @block.sync
        def _(sp):
            sp.dma_start(b1[:, :], dram["ffn_b1"]).then_inc(rows_loaded, 16)
            for k, name in (("b2", "ffn_b2"), ("gain", "ln3_g"), ("shift", "ln3_b")):
                sp.dma_start(rows[k][:, :], row(dram[name])).then_inc(rows_loaded, 16)
            w1_src = dram["ffn_w1"].rearrange("(c p) n -> p c n", p=P)
            w2_src = dram["ffn_w2"].rearrange("(i c p) n -> p i c n", c=2, p=P)
            with sp.Fori(0, PAIRS) as i:
                sp.wait_ge(h_ready, 2 * i + START)
                sp.dma_start(w1[:, :, :], w1_src[:, :, ds(i * (2 * P), 2 * P)]).then_inc(w1_loaded, 16)
                sp.wait_ge(out_done, 2 * i + START + 1)
                sp.dma_start(w2[:, :, :], w2_src[:, ds(i, 1), :, :].squeeze(1)).then_inc(w2_loaded, 16)

        @block.gpsimd
        def _(pool):
            pool.memset(zero[:, :], 0.0).then_inc(zeroed, 1)

        @block.tensor
        def _(pe):
            pe.wait_ge(zeroed, 1)
            for t in range(TT):
                pe.matmul(acc[t][:, :], zero[:, 0:P], zero[:, :], start=True, stop=False, skip_group_check=True)
            pe.sem_inc(h_ready, START)
            pe.sem_inc(out_done, START + 1)
            with pe.Fori(0, PAIRS) as i:
                pe.wait_ge(w1_loaded, 16 * i + 16)
                pe.wait_ge(relu_done, 2 * i + START)
                for f in range(2):
                    for c in range(KC):
                        ins = pe.matmul(psH[f][:, :], w1[:, c, f * P:(f + 1) * P], g["aT"][:, c, :],
                                        start=(c == 0), stop=(c == KC - 1))
                    ins.then_inc(h_ready, 1)
                pe.wait_ge(w2_loaded, 16 * i + 16)
                for f in range(2):
                    pe.wait_ge(relu_done, 2 * i + f + 1 + START)
                    for t in range(TT):
                        ins = pe.matmul(acc[t][:, :], hT[:, f, t * P:(t + 1) * P], w2[:, f, :],
                                        start=False, stop=False, skip_group_check=True)
                    ins.then_inc(out_done, 1)
            for t in range(TT):
                ins = pe.matmul(acc[t][:, :], zero[:, 0:P], zero[:, :], start=False, stop=True, skip_group_check=True)
            ins.then_inc(out_done, 1)
            pe.wait_ge(normed, 1)
            turn_tokens(pe, g["a"], turn, g["ident"], turned, copied)

        @block.scalar
        def _(act):
            act.wait_ge(rows_loaded, 64)
            act.sem_inc(relu_done, START)
            with act.Fori(0, PAIRS) as i:
                for f in range(2):
                    act.wait_ge(h_ready, 2 * i + f + 1 + START)
                    act.wait_ge(out_done, 2 * i + f + START)
                    act.activation(hT[:, f, :], psH[f][:, :], ACT.Relu, bias=b1[:, ds(2 * i + f, 1)]).then_inc(relu_done, 1)
            norm_root(act, stats, 1)
            norm_root(act, stats, 2)
            copy_turned(act, g["aT"], turn, turned, copied)

        @block.vector
        def _(dve):
            step = Steps(dve, dve_step)
            dve.wait_ge(rows_loaded, 64)
            step(dve.tensor_tensor(g["a"][:, :, :], g["a"][:, :, :], middle(rows["b2"][:, :], TT), ALU.add))
            dve.wait_ge(out_done, 2 * PAIRS + 1 + START + 1)
            for t in range(TT):
                ins = dve.tensor_tensor(g["a"][:, t, :], g["a"][:, t, :], acc[t][:, :], ALU.add)
            step(ins)
            norm(step, stats, g["a"], g["a"], 1e-6, 1, gain=rows["gain"], shift=rows["shift"])
            step(dve.tensor_tensor(g["x"][:, :, :], g["x"][:, :, :], g["a"][:, :, :], ALU.add))
            norm(step, stats, g["a"], g["x"], 1e-5, 2)
            dve.sem_inc(normed, 1)



def quantise(step, w, small):
    dve = step.eng
    hi, lo, scale, inv, base = (small[:, i, :] for i in range(5))
    dve.tensor_reduce(hi, w, AXX, ALU.max)
    step(dve.tensor_reduce(lo, w, AXX, ALU.min))
    step(dve.tensor_tensor(scale, hi, lo, ALU.subtract))
    step(dve.tensor_scalar(scale, scale, 1e-5, 1.0 / 15.0, ALU.max, ALU.mult))
    step(dve.reciprocal(inv, scale))
    step(dve.tensor_tensor(base, lo, inv, ALU.mult))
    step(dve.tensor_scalar(base, base, -1.0, ROUND, ALU.mult, ALU.add))
    step(dve.tensor_scalar(base, base, ROUND, 0.0, ALU.subtract, ALU.max))
    step(dve.tensor_scalar(base, base, 15.0, None, ALU.min))
    step(dve.tensor_tensor(w, w, last(inv, GS), ALU.mult))
    step(dve.tensor_scalar(w, w, ROUND, None, ALU.add))
    step(dve.scalar_tensor_tensor(w, w, ROUND, last(base, GS), ALU.subtract, ALU.add))
    step(dve.tensor_scalar(w, w, 0.0, 15.0, ALU.max, ALU.min))
    step(dve.tensor_tensor(w, w, last(base, GS), ALU.subtract))
    step(dve.tensor_tensor(w, w, last(scale, GS), ALU.mult))


QUANT_STEPS = 14


def phase_quantise_weights(nc, g, dram):
    N = 16
    BANKS = N * P // T
    with ExitStack() as ctx:
        m = Memory(nc, ctx, "quant_")
        raw, small = m.sb("raw", [P, N, GS]), m.sb("small", [P, 5, N])
        psT = [m.ps(f"psT{i}", [P, T]) for i in range(BANKS)]
        loaded, dve_step, quantised = m.sem("loaded"), m.sem("dve_step"), m.sem("quantised")
        turned, copied = m.sem("turned"), m.sem("copied")
        batches = (QKV_TILES * KC + KC * QH) // N
        block = ctx.enter_context(nc.Block())

        @block.sync
        def _(sp):
            with sp.Fori(0, batches) as i:
                sp.wait_ge(turned, BANKS * i + START)
                sp.dma_start(raw[:, :, :], dram["w_attn"][ds(i, 1), :, :].squeeze(0).rearrange("p (n k) -> p n k", n=N))\
                  .then_inc(loaded, 16)

        @block.vector
        def _(dve):
            step = Steps(dve, dve_step)
            with dve.Fori(0, batches) as i:
                step.n, step.k = i * QUANT_STEPS, 0
                dve.wait_ge(loaded, 16 * i + 16)
                quantise(step, raw[:, :, :], small)
                assert step.k == QUANT_STEPS
                dve.sem_inc(quantised, 1)

        @block.tensor
        def _(pe):
            pe.sem_inc(turned, START)
            with pe.Fori(0, batches) as i:
                pe.wait_ge(quantised, i + 1)
                pe.wait_ge(copied, BANKS * i + START)
                for b in range(BANKS):
                    for c in range(T // P):
                        ins = pe.transpose(psT[b][:, c * P:(c + 1) * P], raw[:, b * (T // P) + c, :], g["ident"][:, :])
                    ins.then_inc(turned, 1)

        @block.scalar
        def _(act):
            act.sem_inc(copied, START)
            with act.Fori(0, batches) as i:
                for b in range(BANKS):
                    act.wait_ge(turned, BANKS * i + b + 1 + START)
                    act.activation(g["wT"][:, ds(i * (N * P) + b * T, T)], psT[b][:, :], ACT.Copy).then_inc(copied, 1)



def phase_qkv(nc, g, dram):
    rows = QKV_TILES * P
    with ExitStack() as ctx:
        m = Memory(nc, ctx, "qkv_")
        q = m.sb("q", [P, TT, QH * HD])
        small = m.sb("small", [P, 5, TT * 2 * KVH])
        part = m.sb("part", [P, 2, QH * HD])
        rope = {k: m.sb(k, [P, TT, HD // 2]) for k in ("cos_q", "sin_q", "cos_k", "sin_k")}
        ps = [m.ps(f"ps{i}", [P, T]) for i in range(8)]
        loaded, ready, q_copied, kv_copied = (m.sem(n) for n in ("loaded", "ready", "q_copied", "kv_copied"))
        dve_step, rotated, turned, copied = m.sem("dve_step"), m.sem("rotated"), m.sem("turned"), m.sem("copied")
        lo_copied = m.sem("lo_copied")
        hi_of = lambda h: g["q_hi"][:, h, :] if h < QH else g["k_hi"][:, h - QH, :]
        lo_of = lambda h: g["q_lo"][:, h, :] if h < QH else g["k_lo"][:, h - QH, :]
        kv_flat = g["kv"][:, :, :, :].rearrange("p t h d -> p (t h) d")
        block = ctx.enter_context(nc.Block())

        @block.sync
        def _(sp):
            for k, tile in rope.items():
                sp.dma_start(tile[:, :, :], dram[k].rearrange("(t p) d -> p t d", p=P)).then_inc(loaded, 16)

        @block.tensor
        def _(pe):
            for n, col in enumerate((2 * T, 0, T)):
                for t in range(TT):
                    b = (n * TT + t) % 8
                    if n == 2:
                        pe.wait_ge(kv_copied, t + 1)
                    for c in range(KC):
                        ins = pe.matmul(ps[b][:, :], g["aT"][:, c, t * P:(t + 1) * P],
                                        g["wT"][:, c * rows + col:c * rows + col + T], start=(c == 0), stop=(c == KC - 1))
                    ins.then_inc(ready, 1)
            for h in range(QH + KVH):
                if h == 0:
                    pe.wait_ge(rotated, 1)
                if h == QH:
                    pe.wait_ge(rotated, 2)
                pe.wait_ge(q_copied, 8)
                wait(pe, lo_copied, h - 1)
                for t in range(TT):
                    src = q[:, t, h * HD:(h + 1) * HD] if h < QH else g["kv"][:, t, h - QH, :]
                    ins = pe.transpose(ps[h % 2][:, t * P:(t + 1) * P], src, g["ident"][:, :])
                ins.then_inc(turned, 1)

        @block.scalar
        def _(act):
            for t in range(TT):
                act.wait_ge(ready, t + 1)
                act.activation(g["kv"][:, t, :, :].rearrange("p h d -> p (h d)"), ps[t][:, :], ACT.Copy).then_inc(kv_copied, 1)
            for n in range(2):
                for t in range(TT):
                    act.wait_ge(ready, (n + 1) * TT + t + 1)
                    act.activation(q[:, t, n * T:(n + 1) * T], ps[((n + 1) * TT + t) % 8][:, :], ACT.Copy).then_inc(q_copied, 1)
            for h in range(QH + KVH):
                act.wait_ge(turned, h + 1)
                act.activation(hi_of(h), ps[h % 2][:, :], ACT.Copy).then_inc(copied, 1)

        def rotate(step, x, cos, sin, heads):
            dve = step.eng
            halves = x.rearrange("p (n d) -> p n d", d=HD // 2)
            pc, psn = (part[:, i, 0:heads * HD].rearrange("p (n d) -> p n d", d=HD // 2) for i in range(2))
            dve.tensor_tensor(pc, halves, middle(cos, 2 * heads), ALU.mult)
            step(dve.tensor_tensor(psn, halves, middle(sin, 2 * heads), ALU.mult))
            xs, cs, ss = (y.rearrange("p (h two) d -> p h two d", two=2) for y in (halves, pc, psn))
            dve.tensor_tensor(xs[:, :, 0, :], cs[:, :, 0, :], ss[:, :, 1, :], ALU.subtract)
            step(dve.tensor_tensor(xs[:, :, 1, :], cs[:, :, 1, :], ss[:, :, 0, :], ALU.add))

        @block.vector
        def _(dve):
            step = Steps(dve, dve_step)
            dve.wait_ge(loaded, 64)
            dve.wait_ge(q_copied, 8)
            for t in range(TT):
                rotate(step, q[:, t, :], rope["cos_q"][:, t, :], rope["sin_q"][:, t, :], QH)
            dve.sem_inc(rotated, 1)
            dve.wait_ge(kv_copied, 4)
            quantise(step, kv_flat, small)
            for t in range(TT):
                k = g["kv"][:, t, 0:KVH, :].rearrange("p h d -> p (h d)")
                rotate(step, k, rope["cos_k"][:, t, :], rope["sin_k"][:, t, :], KVH)
            dve.sem_inc(rotated, 1)
            for h in range(QH + KVH):
                dve.wait_ge(copied, h + 1)
                dve.tensor_tensor(lo_of(h), ps[h % 2][:, :], hi_of(h).bitcast(F32), ALU.subtract).then_inc(lo_copied, 1)


def phase_gqa_attention(nc, g):
    with ExitStack() as ctx:
        m = Memory(nc, ctx, "gqa_")
        rep = QH // KVH
        core = Core(
            m, QH, qk=lambda h: (g["q_hi"][:, h, :], g["q_lo"][:, h, :], g["k_hi"][:, h // rep, :], g["k_lo"][:, h // rep, :]),
            v=lambda h, c: g["kv"][:, c, KVH + h // rep, :],
            bias=lambda h, t, n: g["causal"][:, t, 0:n],
            keys=lambda t: (t + 1) * P, width=HD, per_out=1, out=lambda j, o: g["oT"][:, o, :], eps=0.0)
        dve_step = m.sem("dve_step")
        block = ctx.enter_context(nc.Block())

        @block.tensor
        def _(pe):
            core.prime_tensor(pe)
            for s in range(core.steps):
                core.tensor(pe, 0, s, g["ident"])

        @block.scalar
        def _(act):
            core.prime_scalar(act)
            for s in range(core.steps):
                core.scalar(act, 0, s)

        @block.vector
        def _(dve):
            core.prime_vector(dve)
            step = Steps(dve, dve_step)
            for s in range(core.n + 1):
                core.vector(dve, 0, s, step)



def phase_router(nc, g, dram):
    chunks = QH * HD // P
    with ExitStack() as ctx:
        m = Memory(nc, ctx, "router_")
        stats = stats_tiles(m)
        hn = m.sb("hn", [P, TT, D])
        gain, wg = m.sb("gain", [P, D]), m.sb("wg", [P, KC, E])
        earlier = m.sb("earlier", [P, E, E])
        logits, e, picked, rw = (m.sb(n, [P, TT, E]) for n in ("logits", "exps", "picked", "rw"))
        above, level = (m.sb(n, [P, TT, E, E]) for n in ("above", "level"))
        col = m.sb("col", [P, 3, TT])
        rwT, pick = m.sb("rwT", [E, T]), m.sb("pick", [E, E, P])
        turn = [m.ps(f"turn{i}", [P, T]) for i in range(2)]
        acc = [m.ps(f"acc{i}", [P, D]) for i in range(TT)]
        psL, psR = m.ps("psL", [P, TT, E]), m.ps("psR", [P, T])
        names = ("loaded turned copied done dve_step normed ones tri logits_ready shifted exps_ready "
                 "rw_ready rwT_ready rwT_copied spread spread_copied").split()
        (loaded, turned, copied, done, dve_step, normed, ones, tri, logits_ready, shifted, exps_ready,
         rw_ready, rwT_ready, rwT_copied, spread, spread_copied) = (m.sem(n) for n in names)
        block = ctx.enter_context(nc.Block())

        @block.sync
        def _(sp):
            sp.dma_start(gain[:, :], row(dram["g2"])).then_inc(loaded, 16)
            sp.dma_start(wg[:, :, :], dram["w_gate"]).then_inc(loaded, 16)

        @block.gpsimd
        def _(pool):
            pool.memset(earlier[:, :, :], 1.0).then_inc(ones, 1)
            pool.wait_ge(ones, 1)
            pool.affine_select(out=earlier[:, :, :], in_=earlier[:, :, :], compare_op=ALU.is_gt, fill=0.0,
                               base=0, pattern=[[1, E], [-1, E]], channel_multiplier=0).then_inc(tri, 1)

        @block.tensor
        def _(pe):
            wo = g["wT"][:, QKV_TILES * KC * P:].rearrange("p (c n) -> p c n", n=D)
            project(pe, acc, g["oT"], wo, done, chunks)
            pe.wait_ge(normed, 1)
            turn_tokens(pe, hn, turn, g["ident"], turned, copied)
            pe.wait_ge(loaded, 32)
            pe.wait_ge(copied, KC)
            for t in range(TT):
                for c in range(KC):
                    ins = pe.matmul(psL[:, t, :], g["aT"][:, c, t * P:(t + 1) * P], wg[:, c, :],
                                    start=(c == 0), stop=(c == KC - 1))
            ins.then_inc(logits_ready, 1)
            pe.wait_ge(rw_ready, 1)
            for t in range(TT):
                ins = pe.transpose(psR[0:E, t * P:(t + 1) * P], rw[:, t, :], g["ident"][:, :])
            ins.then_inc(rwT_ready, 1)
            pe.wait_ge(rwT_copied, 1)
            for x in range(E):
                wait(pe, spread_copied, x - 1)
                pe.matmul(turn[x % 2][:, :], pick[:, x, :], rwT[:, :], start=True, stop=True).then_inc(spread, 1)

        @block.scalar
        def _(act):
            norm_root(act, stats, 1)
            copy_turned(act, g["aT"], turn, turned, copied)
            act.wait_ge(shifted, 1)
            act.activation(e[:, :, :], e[:, :, :], ACT.Exp).then_inc(exps_ready, 1)
            for x in range(E):
                act.wait_ge(spread, x + 1)
                act.activation(g["rw"][:, x, :], turn[x % 2][:, :], ACT.Copy).then_inc(spread_copied, 1)

        @block.vector
        def _(dve):
            step = Steps(dve, dve_step)
            for x in range(E):
                dve.tensor_copy(pick[:, x, :], g["ident"][0:E, x:x + 1].broadcast_to([E, P]))
            for t in range(TT):
                dve.wait_ge(done, t + 1)
                ins = dve.tensor_tensor(g["a"][:, t, :], g["a"][:, t, :], acc[t][:, :], ALU.add)
            step(ins)
            dve.wait_ge(loaded, 32)
            norm(step, stats, hn, g["a"], 1e-5, 1, gain=gain, rms=True)
            dve.sem_inc(normed, 1)
            step(dve.tensor_tensor(g["x"][:, :, :], g["x"][:, :, :], g["a"][:, :, :], ALU.add))
            dve.wait_ge(copied, KC)
            step(dve.tensor_copy(g["hn_hi"][:, :, :], g["aT"][:, :, :]))
            dve.tensor_tensor(g["hn_lo"][:, :, :], g["aT"][:, :, :], g["hn_hi"][:, :, :].bitcast(F32), ALU.subtract)
            dve.wait_ge(logits_ready, 1)
            step(dve.tensor_copy(logits[:, :, :], psL[:, :, :]))
            step(dve.tensor_reduce(col[:, 0, :], logits[:, :, :], AXX, ALU.max))
            step(dve.tensor_tensor(e[:, :, :], logits[:, :, :], last(col[:, 0, :], E), ALU.subtract))
            dve.sem_inc(shifted, 1)
            mine = last(logits[:, :, :], E)
            other = logits[:, :, :].unsqueeze(2).broadcast_to([P, TT, E, E])
            dve.tensor_tensor(above[:, :, :, :], other, mine, ALU.is_gt)
            step(dve.tensor_tensor(level[:, :, :, :], other, mine, ALU.is_equal))
            dve.wait_ge(tri, 1)
            step(dve.tensor_tensor(level[:, :, :, :], level[:, :, :, :],
                                   earlier[:, :, :].unsqueeze(1).broadcast_to([P, TT, E, E]), ALU.mult))
            step(dve.tensor_tensor(above[:, :, :, :], above[:, :, :, :], level[:, :, :, :], ALU.add))
            step(dve.tensor_reduce(picked[:, :, :], above[:, :, :, :], AXX, ALU.add))
            step(dve.tensor_scalar(picked[:, :, :], picked[:, :, :], 1.5, None, ALU.is_lt))
            dve.wait_ge(exps_ready, 1)
            step(dve.tensor_tensor(picked[:, :, :], picked[:, :, :], e[:, :, :], ALU.mult))
            step(dve.tensor_reduce(col[:, 1, :], picked[:, :, :], AXX, ALU.add))
            step(dve.reciprocal(col[:, 2, :], col[:, 1, :]))
            dve.tensor_tensor(rw[:, :, :], picked[:, :, :], last(col[:, 2, :], E), ALU.mult).then_inc(rw_ready, 1)
            dve.wait_ge(rwT_ready, 1)
            dve.tensor_copy(rwT[:, :], psR[0:E, :]).then_inc(rwT_copied, 1)



def phase_experts(nc, g, dram):
    N = E * FT
    UNIT = T
    with ExitStack() as ctx:
        m = Memory(nc, ctx, "moe_")
        raw = [m.sb(f"raw{i}", [P, BLK, GS]) for i in range(4)]
        deq = [m.sb(f"deq{i}", [P, BLK, GS]) for i in range(2)]
        scales = [m.sb(f"scales{i}", [P, 6, BLK]) for i in range(4)]
        wT_hi = [m.sb(f"wT_hi{i}", [P, 3, UNIT], F32R) for i in range(2)]
        wT_lo = [m.sb(f"wT_lo{i}", [P, 3, UNIT], F32R) for i in range(2)]
        silu, gate, up = (m.sb(n, [P, 2, T]) for n in ("silu", "gate", "up"))
        up_hi, up_lo = (m.sb(n, [P, 2, T], F32R) for n in ("up_hi", "up_lo"))
        zero = m.sb("zero", [P, D])
        psH1, psH3 = m.ps("psH1", [P, T]), m.ps("psH3", [P, T])
        psT = [m.ps(f"psT{i}", [P, T]) for i in range(2)]
        acc = [m.ps(f"acc{i}", [P, D]) for i in range(TT)]
        loaded = [m.sem(f"loaded{i}") for i in range(4)]
        names = ("scales_ready scaled rounded dequantised turned hi_copied lo_copied h_ready silu_done "
                 "gate_done up_done up_hi_done up_lo_done out_done closed dve_step zeroed begun").split()
        (scales_ready, scaled, rounded, dequantised, turned, hi_copied, lo_copied, h_ready, silu_done,
         gate_done, up_done, up_hi_done, up_lo_done, out_done, closed, dve_step, zeroed, begun) = (m.sem(n) for n in names)
        HI, LO, SCALE, INV, BASE, SHIFT = range(6)
        SCALE_STEPS = 8
        block = ctx.enter_context(nc.Block())

        def live(n):
            return not isinstance(n, int) or 0 <= n < N

        def steps(eng, each):
            for n in range(-4, 4):
                each(n, n % 4)
            with eng.Fori(1, N // 4 - 1) as i:
                for j in range(4):
                    each(4 * i + j, j)
            for n in range(N - 4, N + 1):
                each(n, n % 4)

        @block.sync
        def _(sp):
            def each(n, j):
                if live(n + 4):
                    wait(sp, scaled, 3 * n + 3)
                    sp.dma_start(raw[j][:, :, :], dram["w_moe"][ds(n + 4, 1), :, :].squeeze(0)
                                 .rearrange("p (b k) -> p b k", b=BLK)).then_inc(loaded[j], 16)
            steps(sp, each)

        @block.vector
        def _(dve):
            step = Steps(dve, dve_step)

            def scales_of(n, j):
                s = scales[j]
                dve.wait_ge(loaded[j], 4 * (n - j) + 16)
                step.n, step.k = n * SCALE_STEPS, 0
                dve.tensor_reduce(s[:, HI, :], raw[j][:, :, :], AXX, ALU.max)
                step(dve.tensor_reduce(s[:, LO, :], raw[j][:, :, :], AXX, ALU.min))
                step(dve.tensor_tensor(s[:, SCALE, :], s[:, HI, :], s[:, LO, :], ALU.subtract))
                step(dve.tensor_scalar(s[:, SCALE, :], s[:, SCALE, :], 1e-5, 1.0 / 15.0, ALU.max, ALU.mult))
                step(dve.reciprocal(s[:, INV, :], s[:, SCALE, :]))
                step(dve.tensor_tensor(s[:, BASE, :], s[:, LO, :], s[:, INV, :], ALU.mult))
                step(dve.tensor_scalar(s[:, BASE, :], s[:, BASE, :], -1.0, ROUND, ALU.mult, ALU.add))
                step(dve.tensor_scalar(s[:, BASE, :], s[:, BASE, :], ROUND, 0.0, ALU.subtract, ALU.max))
                step(dve.tensor_scalar(s[:, BASE, :], s[:, BASE, :], 15.0, None, ALU.min))
                dve.tensor_scalar(s[:, SHIFT, :], s[:, BASE, :], ROUND_UP, -1.0, ALU.add, ALU.mult)\
                   .then_inc(scales_ready, 1)
                assert step.k == SCALE_STEPS

            def round_unit(n, j, r):
                dve.wait_ge(scaled, 3 * n + r + 1)
                d = deq[j % 2][:, 4 * r:4 * r + 4, :]
                dve.tensor_scalar(d, d, 15.0, ROUND_UP, ALU.min, ALU.add).then_inc(rounded, 1)

            def lo_unit(n, j, r):
                dve.wait_ge(hi_copied, 3 * n + r + 1)
                dve.tensor_tensor(wT_lo[j % 2][:, r, :], psT[(3 * j + r) % 2][:, :],
                                  wT_hi[j % 2][:, r, :].bitcast(F32), ALU.subtract).then_inc(lo_copied, 1)

            def each(n, j):
                j1, j2, j3 = (j + 1) % 4, (j + 2) % 4, (j + 3) % 4
                if live(n):
                    lo_unit(n, j, 2)
                if live(n + 3):
                    scales_of(n + 3, j3)
                if live(n + 2):
                    round_unit(n + 2, j2, 0)
                if live(n + 1):
                    lo_unit(n + 1, j1, 0)
                if live(n):
                    dve.wait_ge(h_ready, 2 * n + 2)
                    wait(dve, up_done, n - 1)
                    dve.tensor_tensor(gate[:, j % 2, :], psH3[:, :], rw_row(g, n), ALU.mult).then_inc(gate_done, 1)
                if live(n + 2):
                    round_unit(n + 2, j2, 1)
                    round_unit(n + 2, j2, 2)
                if live(n + 1):
                    lo_unit(n + 1, j1, 1)
                if live(n):
                    dve.wait_ge(up_done, n + 1)
                    wait(dve, out_done, n - 1)
                    dve.tensor_copy(up_hi[:, j % 2, :], up[:, j % 2, :]).then_inc(up_hi_done, 1)
            steps(dve, each)
            dve.wait_ge(out_done, N)
            dve.wait_ge(closed, 1)
            for t in range(TT):
                dve.tensor_tensor(g["x"][:, t, :], g["x"][:, t, :], acc[t][:, :], ALU.add)

        @block.scalar
        def _(act):
            def scale_blocks(n, j, r):
                if r == 0:
                    act.wait_ge(scales_ready, n + 1)
                wait(act, turned, 3 * (n - 2) + r + 1)
                for b in range(4 * r, 4 * r + 4):
                    ins = act.activation(deq[j % 2][:, b, :], raw[j][:, b, :], ACT.Relu,
                                         bias=scales[j][:, BASE, b:b + 1], scale=scales[j][:, INV, b:b + 1])
                ins.then_inc(scaled, 1)

            def hi_unit(n, j, r):
                act.wait_ge(turned, 3 * n + r + 1)
                act.activation(wT_hi[j % 2][:, r, :], psT[(3 * j + r) % 2][:, :], ACT.Copy).then_inc(hi_copied, 1)

            def each(n, j):
                j1, j2 = (j + 1) % 4, (j + 2) % 4
                if live(n):
                    hi_unit(n, j, 2)
                if live(n + 2):
                    scale_blocks(n + 2, j2, 0)
                if live(n):
                    act.wait_ge(h_ready, 2 * n + 1)
                    wait(act, up_done, n - 1)
                    act.activation(silu[:, j % 2, :], psH1[:, :], ACT.Silu).then_inc(silu_done, 1)
                if live(n + 1):
                    hi_unit(n + 1, j1, 0)
                if live(n + 2):
                    scale_blocks(n + 2, j2, 1)
                    scale_blocks(n + 2, j2, 2)
                if live(n + 1):
                    hi_unit(n + 1, j1, 1)
            steps(act, each)

        @block.gpsimd
        def _(pool):
            pool.memset(zero[:, :], 0.0).then_inc(zeroed, 1)

            def dequantise(n, j, r):
                pool.wait_ge(rounded, 3 * n + r + 1)
                pool.sem_inc(begun, 1)
                s = scales[j]
                for b in range(4 * r, 4 * r + 4):
                    ins = pool.tensor_scalar(deq[j % 2][:, b, :], deq[j % 2][:, b, :], s[:, SHIFT, b:b + 1],
                                             s[:, SCALE, b:b + 1], ALU.add, ALU.mult)
                ins.then_inc(dequantised, 1)

            def each(n, j):
                if live(n):
                    pool.wait_ge(silu_done, n + 1)
                    pool.wait_ge(gate_done, n + 1)
                    wait(pool, up_lo_done, n - 1)
                    pool.tensor_tensor(up[:, j % 2, :], silu[:, j % 2, :], gate[:, j % 2, :], ALU.mult)\
                        .then_inc(up_done, 1)
                if live(n + 2):
                    dequantise(n + 2, (j + 2) % 4, 0)
                if live(n):
                    pool.wait_ge(up_hi_done, n + 1)
                    pool.tensor_tensor(up_lo[:, j % 2, :], up[:, j % 2, :], up_hi[:, j % 2, :].bitcast(F32),
                                       ALU.subtract).then_inc(up_lo_done, 1)
                if live(n + 2):
                    dequantise(n + 2, (j + 2) % 4, 1)
                    dequantise(n + 2, (j + 2) % 4, 2)
            steps(pool, each)

        @block.tensor
        def _(pe):
            pe.wait_ge(zeroed, 1)
            for t in range(TT):
                pe.matmul(acc[t][:, :], zero[:, 0:P], zero[:, :], start=True, stop=False, skip_group_check=True)

            def hidden(n, j, r, ps):
                pe.wait_ge(lo_copied, 3 * n + r + 1)
                wait(pe, silu_done if r == 0 else gate_done, n)
                hi, lo = wT_hi[j % 2], wT_lo[j % 2]
                for c in range(KC):
                    col = slice(c * P, (c + 1) * P)
                    pe.matmul(ps[:, :], hi[:, r, col], g["hn_hi"][:, c, :], start=(c == 0), stop=False)
                    pe.matmul(ps[:, :], hi[:, r, col], g["hn_lo"][:, c, :], start=False, stop=False)
                    ins = pe.matmul(ps[:, :], lo[:, r, col], g["hn_hi"][:, c, :], start=False, stop=(c == KC - 1))
                ins.then_inc(h_ready, 1)

            def turn_unit(n, j, r):
                pe.wait_ge(dequantised, 3 * n + r + 1)
                wait(pe, lo_copied, 3 * n + r - 1)
                for c in range(4):
                    ins = pe.transpose(psT[(3 * j + r) % 2][:, c * P:(c + 1) * P], deq[j % 2][:, 4 * r + c, :],
                                       g["ident"][:, :])
                ins.then_inc(turned, 1)

            def output(n, j):
                pe.wait_ge(lo_copied, 3 * n + 3)
                pe.wait_ge(up_lo_done, n + 1)
                w_hi, w_lo = wT_hi[j % 2][:, 2, :], wT_lo[j % 2][:, 2, :]
                for t in range(TT):
                    hi, lo = (u[:, j % 2, t * P:(t + 1) * P] for u in (up_hi, up_lo))
                    for a, b in ((hi, w_hi), (hi, w_lo), (lo, w_hi)):
                        ins = pe.matmul(acc[t][:, :], a, b, start=False, stop=False, skip_group_check=True)
                ins.then_inc(out_done, 1)

            def each(n, j):
                j1 = (j + 1) % 4
                if live(n):
                    hidden(n, j, 0, psH1)
                if live(n + 1):
                    turn_unit(n + 1, j1, 0)
                if live(n):
                    hidden(n, j, 1, psH3)
                if live(n + 1):
                    turn_unit(n + 1, j1, 1)
                if live(n - 1):
                    output(n - 1, (j - 1) % 4)
                if live(n + 1):
                    turn_unit(n + 1, j1, 2)
            steps(pe, each)
            for t in range(TT):
                ins = pe.matmul(acc[t][:, :], zero[:, 0:P], zero[:, :], start=False, stop=True, skip_group_check=True)
            ins.then_inc(closed, 1)


def rw_row(g, n):
    e = n // FT
    return g["rw"][:, e, :] if isinstance(e, int) else g["rw"][:, ds(e, 1), :].squeeze(1)


def phase_store(nc, src, out):
    with ExitStack() as ctx:
        stored = Memory(nc, ctx).sem("stored")
        block = ctx.enter_context(nc.Block())

        @block.sync
        def _(sp):
            sp.dma_start(out.rearrange("(t p) d -> p t d", p=P), src).then_inc(stored, 16)
            sp.wait_ge(stored, 16)


def program(nc, dram, out):
    with ExitStack() as ctx:
        m = Memory(nc, ctx)
        g = {"x": m.sb("x", [P, TT, D]), "a": m.sb("a", [P, TT, D]), "aT": m.sb("aT", [P, KC, T]),
             "ident": m.sb("ident", [P, P]), "causal": m.sb("causal", [P, TT, T])}
        with ExitStack() as early:
            me = Memory(nc, early)
            g["mask"] = me.sb("mask", [P, TT, T])
            g["key_mask"] = me.sb("key_mask", [P, HEADS * KEYS])
            g["oT"] = me.sb("oT", [P, KC, T])
            phase_start(nc, g, dram)
            phase_attention(nc, g, dram, "sa", "masked")
            phase_project(nc, g, dram, "sa", dram["sa_wo"], "sa")
            phase_attention(nc, g, dram, "ca", "strided")
            phase_project(nc, g, dram, "ca", dram["ca_wo"], "ca")
            phase_mlp(nc, g, dram)
            phase_attention(nc, g, dram, "attn", "causal", eps=1e-8)
            phase_project(nc, g, dram, "attn", dram["attn_wo"], "attn")
        with ExitStack() as router:
            mr = Memory(nc, router)
            g["hn_hi"], g["hn_lo"] = mr.sb("hn_hi", [P, KC, T], F32R), mr.sb("hn_lo", [P, KC, T], F32R)
            g["rw"] = mr.sb("rw", [P, E, T])
            with ExitStack() as late:
                ml = Memory(nc, late)
                g["wT"] = ml.sb("wT", [P, (QKV_TILES * KC + KC * QH) * P])
                g["kv"] = ml.sb("kv", [P, TT, 2 * KVH, HD])
                g["q_hi"], g["q_lo"] = ml.sb("q_hi", [P, QH, T], F32R), ml.sb("q_lo", [P, QH, T], F32R)
                g["k_hi"], g["k_lo"] = ml.sb("k_hi", [P, KVH, T], F32R), ml.sb("k_lo", [P, KVH, T], F32R)
                g["oT"] = ml.sb("gqa_oT", [P, QH, T])
                phase_quantise_weights(nc, g, dram)
                phase_qkv(nc, g, dram)
                phase_gqa_attention(nc, g)
                phase_router(nc, g, dram)
            phase_experts(nc, g, dram)
            phase_store(nc, g["x"][:, :, :], out)


def lay_out(i):
    import numpy as np
    xa, at = "L0_xattn_", "L0_attn_"
    c = np.ascontiguousarray
    out = {"x": c(i["x"][0]), "mask": c(i["mask_Bx1xSxS_ik0"][0, 0])}
    out["key_mask"] = c(i["mask_Bx1x1xS2_if1"][0, 0, 0, :HEADS * KEYS].reshape(KEYS, HEADS).T).reshape(-1)
    out["enc"] = c(i["ctx_1024"][0, :HEADS * KEYS].reshape(KEYS, HEADS, D).transpose(1, 2, 0))
    for n in ("sa_wq", "sa_bq", "sa_wk", "sa_bk", "sa_wv", "sa_bv", "sa_wo", "sa_bo",
              "ca_wq", "ca_bq", "ca_wk", "ca_bk", "ca_wv", "ca_bv", "ca_wo", "ca_bo",
              "ffn_w1", "ffn_b1", "ffn_w2", "ffn_b2", "ln1_g", "ln1_b", "ln2_g", "ln2_b", "ln3_g", "ln3_b"):
        out[n] = c(i[xa + n])
    for n in ("sa_bq", "sa_bk", "ca_bq", "ca_bk", "ffn_b1"):
        out[n] = c(out[n].reshape(-1, P).T)
    out["attn_wq"], out["attn_wo"] = c(i[at + "Wq"].T), c(i[at + "Wo"].T)
    out["attn_wk"], out["attn_wv"] = c(i[at + "Wkv"][:D].T), c(i[at + "Wkv"][D:].T)
    f = "L0_ffn_"
    out["g1"], out["g2"] = c(i[f + "g1"]), c(i[f + "g2"])
    qkv = np.concatenate([i[f + "w_q"], i[f + "w_k"], i[f + "w_v"]]).reshape(QKV_TILES, P, KC, GS)
    wo = i[f + "w_o"].reshape(KC, P, QH, GS)
    blocks = np.concatenate([w.transpose(2, 0, 1, 3).reshape(-1, P, GS) for w in (qkv, wo)])
    out["w_attn"] = c(blocks.reshape(-1, 16, P, GS).transpose(0, 2, 1, 3)).reshape(-1, P, 16 * GS)
    out["w_gate"] = c(i[f + "w_gate"].T.reshape(KC, P, E).transpose(1, 0, 2))
    w1, w3 = (i[f + w].reshape(E * FT, P, KC * GS) for w in ("w1", "w3"))
    w2 = i[f + "w2"].reshape(E, KC, P, FT, GS).transpose(0, 3, 2, 1, 4).reshape(E * FT, P, KC * GS)
    out["w_moe"] = np.concatenate([w1, w3, w2], axis=2)
    inv = (1.0 / np.float32(1e6) ** (np.arange(0, HD, 2, dtype=np.float32) / np.float32(HD))).astype(np.float32)
    angle = np.arange(T, dtype=np.float32)[:, None] * inv[None, :]
    out["cos_k"], out["sin_k"] = np.cos(angle), np.sin(angle)
    scale = np.float32(-(HD ** -0.5))
    out["cos_q"], out["sin_q"] = out["cos_k"] * scale, out["sin_k"] * scale
    return out



def kernel(**inputs):
    import numpy as np
    import concourse.bacc as bacc
    from concourse.bass_utils import run_bass_kernel_spmd

    arrays = {f"{n}_dram": a for n, a in lay_out({k: np.asarray(v) for k, v in inputs.items()}).items()}
    nc = bacc.Bacc("TRN2", target_bir_lowering=False, num_devices=1)
    dram = {n[:-5]: nc.dram_tensor(n, a.shape, mybir.dt.from_np(a.dtype), kind="ExternalInput").ap()
            for n, a in arrays.items()}
    out = nc.dram_tensor("out_dram", (T, D), F32, kind="ExternalOutput").ap()
    program(nc, dram, out)
    result = run_bass_kernel_spmd(nc, [arrays], core_ids=[0])
    return result.results[0]["out_dram"].reshape(1, T, D)
```

```python
import functools
from contextlib import ExitStack

import concourse.bass as bass
from concourse import mybir

F32 = mybir.dt.float32
F32R = mybir.dt.float32r
I32 = mybir.dt.int32
ALU = mybir.AluOpType
ACT = mybir.ActivationFunctionType
AXX = mybir.AxisListType.X
ds = bass.ds

P = 128
T = 512
TT = T // P
D = 512
KC = D // P
HEADS = 16
DH = D // HEADS
HPG = P // DH
GROUPS = HEADS // HPG
START = 1
KEYS = 256
FF = 2048
QH, KVH, HD = 8, 2, 128
E, FFN = 8, 1792
FT = FFN // P
GS = 128
BLK = 12
QKV_TILES = (QH + 2 * KVH) * HD // P
ATTN_BLK = (QKV_TILES * KC + KC * QH) * P // FF
BIG = 1.0e30
HUGE = 3.0e38
ROUND = 1.5 * 2.0 ** 23
ROUND_UP = 2.0 ** 23


def wait(eng, sem, value):
    if isinstance(value, int) and value <= 0:
        return
    eng.wait_ge(sem, value)


class Steps:

    def __init__(self, eng, sem, start=0):
        self.eng, self.sem, self.n, self.k = eng, sem, start, 0

    def __call__(self, ins):
        self.n, self.k = self.n + 1, self.k + 1
        ins.then_inc(self.sem, 1)
        self.eng.wait_ge(self.sem, self.n)


class Memory:

    def __init__(self, nc, ctx, prefix=""):
        self.nc, self.ctx, self.prefix = nc, ctx, prefix

    def sb(self, name, shape, dtype=F32):
        return self.ctx.enter_context(self.nc.sbuf_tensor(self.prefix + name, shape, dtype))

    def ps(self, name, shape, dtype=F32):
        return self.ctx.enter_context(self.nc.psum_tensor(self.prefix + name, shape, dtype))

    def sem(self, name):
        sem = self.nc.alloc_semaphore(self.prefix + name)
        self.ctx.callback(self.clear, sem)
        return sem

    def clear(self, sem):
        self.nc.gpsimd.sem_clear(sem)
        self.nc.release_semaphore(sem)


def row(ap):
    return ap.rearrange("(a n) -> a n", a=1).broadcast_to([P, ap.shape[0]])


def middle(ap, n):
    return ap.unsqueeze(1).broadcast_to([ap.shape[0], n, ap.shape[1]])


def last(ap, n):
    return ap.unsqueeze(len(ap.shape)).broadcast_to([*ap.shape, n])



class Norm:

    def __init__(self, m):
        small = m.sb("norm_small", [P, 4, TT])
        self.raw, self.mv = m.sb("norm_raw", [P, TT, 6]), m.sb("norm_mv", [P, TT, 2])
        self.v, self.root, self.r, self.tmp = (small[:, i, :] for i in range(4))
        self.var_ready, self.root_ready = m.sem("var_ready"), m.sem("root_ready")
        self.vector_count = self.scalar_count = 0

    def statistics(self, step, tiles, x, eps, rms=False):
        dve, self.vector_count = step.eng, self.vector_count + 1
        some = slice(tiles[0], tiles[-1] + 1)
        mean, var = self.mv[:, some, 0], self.mv[:, some, 1]
        v, root, r, tmp = (a[:, some] for a in (self.v, self.root, self.r, self.tmp))
        for t in tiles:
            ins = dve.bn_stats(self.raw[:, t, :], x[:, t, :])
        step(ins)
        for t in tiles:
            ins = dve.bn_aggr(self.mv[:, t, :], self.raw[:, t, :])
        step(ins)
        if rms:
            step(dve.tensor_tensor(tmp, mean, mean, ALU.mult))
            ins = dve.scalar_tensor_tensor(v, var, eps, tmp, ALU.add, ALU.add)
        else:
            ins = dve.tensor_scalar(v, var, eps, None, ALU.add)
        ins.then_inc(self.var_ready, 1)
        dve.wait_ge(self.root_ready, self.vector_count)
        step(dve.reciprocal(r, root))
        step(dve.tensor_tensor(tmp, r, r, ALU.mult))
        step(dve.tensor_tensor(tmp, tmp, v, ALU.mult))
        step(dve.tensor_scalar(tmp, tmp, -0.5, 1.5, ALU.mult, ALU.add))
        step(dve.tensor_tensor(r, r, tmp, ALU.mult))

    def mean(self, t):
        return self.mv[:, t, 0:1]

    def inverse(self, t):
        return self.r[:, t:t + 1]

    def apply(self, dve, t, y, x, rms=False):
        if rms:
            return dve.tensor_scalar(y[:, t, :], x[:, t, :], self.inverse(t), None, ALU.mult)
        return dve.tensor_scalar(y[:, t, :], x[:, t, :], self.mean(t), self.inverse(t), ALU.subtract, ALU.mult)

    def vector(self, step, t, y, x, eps, rms=False):
        self.statistics(step, [t], x, eps, rms)
        return self.apply(step.eng, t, y, x, rms)

    def scalar(self, act, tiles):
        self.scalar_count += 1
        some = slice(tiles[0], tiles[-1] + 1)
        act.wait_ge(self.var_ready, self.scalar_count)
        act.activation(self.root[:, some], self.v[:, some], ACT.Sqrt).then_inc(self.root_ready, 1)


HALVES = [range(0, TT // 2), range(TT // 2, TT)]


class Turn:

    def __init__(self, m):
        self.banks = [m.ps(f"turn{i}", [P, T]) for i in range(2)]
        self.turned, self.copied = m.sem("turned"), m.sem("copied")

    def tensor(self, pe, t, src, ident):
        wait(pe, self.copied, t - 1)
        for c in range(KC):
            ins = pe.transpose(self.banks[t % 2][:, c * P:(c + 1) * P], src[:, t, c * P:(c + 1) * P], ident[:, :])
        ins.then_inc(self.turned, 1)

    def scalar(self, act, t, dst, gain=None, shift=None):
        act.wait_ge(self.turned, t + 1)
        tokens = slice(t * P, (t + 1) * P)
        if gain is None:
            ins = act.activation(dst[:, :, tokens], self.banks[t % 2][:, :].rearrange("p (c q) -> p c q", q=P), ACT.Copy)
        for c in range(KC if gain is not None else 0):
            src, out, scale = self.banks[t % 2][:, c * P:(c + 1) * P], dst[:, c, tokens], gain[:, c:c + 1]
            if shift is None:
                ins = act.activation(out, src, ACT.Copy, scale=scale)
            else:
                ins = act.activation(out, src, ACT.Identity, bias=shift[:, c:c + 1], scale=scale)
        ins.then_inc(self.copied, 1)



def phase_start(nc, g, dram):
    with ExitStack() as ctx:
        m = Memory(nc, ctx, "start_")
        norm, turn = Norm(m), Turn(m)
        mask_raw = m.sb("mask_raw", [P, TT, T], I32)
        key_raw = m.sb("key_raw", [P, HEADS * KEYS], I32)
        x_loaded, consts_loaded = [m.sem(f"x_loaded{t}") for t in range(TT)], m.sem("consts_loaded")
        dve_step, zeroed, ident_made, normed = m.sem("dve_step"), m.sem("zeroed"), m.sem("ident_made"), m.sem("normed")
        block = ctx.enter_context(nc.Block())

        @block.sync
        def _(sp):
            for t in range(TT):
                sp.dma_start(g["x"][:, t, :], dram["x"][t * P:(t + 1) * P, :]).then_inc(x_loaded[t], 16)
            load_heads(sp, g, dram, "sa", 0)
            sp.dma_start(mask_raw[:, :, :], dram["mask"].rearrange("(t p) k -> p t k", p=P)).then_inc(consts_loaded, 16)
            sp.dma_start(key_raw[:, :], row(dram["key_mask"])).then_inc(consts_loaded, 16)

        @block.gpsimd
        def _(pool):
            pool.memset(g["ident"][:, :], 0.0).then_inc(zeroed, 1)
            pool.memset(g["causal"][:, :, :], 0.0).then_inc(zeroed, 1)
            pool.wait_ge(zeroed, 2)
            pool.affine_select(out=g["ident"][:, :], in_=g["ident"][:, :], compare_op=ALU.not_equal, fill=1.0,
                               base=0, pattern=[[-1, P]], channel_multiplier=1).then_inc(ident_made, 1)
            pool.affine_select(out=g["causal"][:, :, :], in_=g["causal"][:, :, :], compare_op=ALU.is_ge, fill=BIG,
                               base=0, pattern=[[P, TT], [-1, T]], channel_multiplier=1)

        @block.vector
        def _(dve):
            step = Steps(dve, dve_step)
            for t in range(TT):
                dve.wait_ge(x_loaded[t], 16)
                norm.vector(step, t, g["a"], g["x"], 1e-5).then_inc(normed, 1)
            dve.wait_ge(consts_loaded, 32)
            dve.tensor_scalar(g["mask"][:, :, :], mask_raw[:, :, :], 0.0, BIG, ALU.is_equal, ALU.mult)
            dve.tensor_scalar(g["key_mask"][:, :], key_raw[:, :], 0.0, BIG, ALU.is_equal, ALU.mult)

        @block.tensor
        def _(pe):
            pe.wait_ge(ident_made, 1)
            for t in range(TT):
                pe.wait_ge(normed, t + 1)
                turn.tensor(pe, t, g["a"], g["ident"])

        @block.scalar
        def _(act):
            for t in range(TT):
                norm.scalar(act, [t])
                if t >= 1:
                    turn.scalar(act, t - 1, g["aT"])
            turn.scalar(act, TT - 1, g["aT"])



def load_heads(sp, g, dram, name, j, q_used=None, k_used=None):
    w, q_loaded, k_loaded = g["w_heads"], g["q_loaded"][name], g["k_loaded"][name]
    columns = lambda n: dram[f"{name}_{n}"].rearrange("(c p) n -> p c n", p=P)
    first = isinstance(j, int) and j == 0
    if not first:
        sp.wait_ge(q_used, j)
    sp.dma_start(w["q"][:, :, :], columns("wq")[:, :, ds(j * P, P)]).then_inc(q_loaded, 16)
    if not first:
        sp.wait_ge(k_used, j)
    if name == "ca":
        sp.dma_start(w["kv"], columns("wkv")[:, :, ds(j * (2 * P), 2 * P)]).then_inc(k_loaded, 16)
        enc_src = dram["enc"].rearrange("(j h) (c p) n -> p j h c n", h=HPG, p=P)
        for h in range(HPG):
            sp.dma_start(g["enc"][:, h, :, :], enc_src[:, ds(j, 1), h, :, :].squeeze(1)).then_inc(k_loaded, 16)
    else:
        sp.dma_start(w["k"][:, :, :], columns("wk")[:, :, ds(j * P, P)]).then_inc(k_loaded, 16)
    if first and name != "ca":
        sp.dma_start(w["v"][:, :, :], columns("wv")).then_inc(g["v_loaded"][name], 16)
    if first and name != "attn":
        for b, src in (("bq", dram[name + "_bq"]), ("bk", dram[name + "_bk"]), ("bv", row(dram[name + "_bv"]))):
            sp.dma_start(g[b][:, :], src).then_inc(g["bias_loaded"][name], 16)


LAYER_NORM = {"sa": "ln1", "ca": "ln2"}


def load_out(sp, g, dram, name):
    sem = g["out_loaded"][name]
    sp.dma_start(g["w_out"][:, :, :], dram[name + "_wo"].rearrange("(c p) n -> p c n", p=P)).then_inc(sem, 16)
    if name == "attn":
        sp.dma_start(g["gain_cols"][:, :], dram["g1_cols"]).then_inc(sem, 16)
    else:
        ln = LAYER_NORM[name]
        for k, vector in (("bo", name + "_bo"), ("gain", ln + "_g"), ("shift", ln + "_b")):
            sp.dma_start(g[k][:, :], row(dram[vector])).then_inc(sem, 16)
        sp.dma_start(g["gain_cols"][:, :], dram[ln + "_g_cols"]).then_inc(sem, 16)
        sp.dma_start(g["shift_cols"][:, :], dram[ln + "_b_cols"]).then_inc(sem, 16)


def out_loads(name):
    return 16 * (2 if name == "attn" else 6)



class Core:
    LEAD = HPG
    BUFFERS = 2 * HPG
    N = HPG * TT
    SHIFTED0, TURNED0, COPIED0, VALUES0, OUT0 = 4, 8, 2, 2, 2

    def __init__(self, m, qk, v, bias, keys, width, out, eps):
        self.narrow, self.width, self.eps = width < P, width, eps
        self.qk, self.v, self.bias, self.keys, self.out = qk, v, bias, keys, out
        self.banks = 1 if self.narrow else 2
        self.shifted = m.sb("shifted", [P, self.BUFFERS, T])
        self.least = m.sb("least", [P, self.N])
        self.row_sum = m.sb("row_sum", [P, self.N])
        self.row_inv = m.sb("row_inv", [P, self.N])
        self.probsT = m.sb("probsT", [P, 2, HPG, TT, P])
        self.psS = [m.ps(f"psS{i}", [P, T]) for i in range(HPG)]
        self.psT = [m.ps(f"psT{i}", [P, T]) for i in range(2)]
        self.psO = [m.ps(f"psO{i}", [P, T]) for i in range(self.banks)]
        (self.scores_ready, self.begun, self.shifted_ready, self.exps_done, self.probs_ready, self.turned,
         self.probsT_copied, self.values_done, self.out_copied) = (m.sem(n) for n in (
             "scores_ready", "begun", "shifted_ready", "exps_done", "probs_ready", "turned",
             "probsT_copied", "values_done", "out_copied"))

    def prime_vector(self, dve):
        dve.sem_inc(self.shifted_ready, self.SHIFTED0)

    def prime_scalar(self, act):
        act.sem_inc(self.probsT_copied, self.COPIED0)
        act.sem_inc(self.out_copied, self.OUT0)

    def prime_tensor(self, pe):
        pe.sem_inc(self.turned, self.TURNED0)
        pe.sem_inc(self.values_done, self.VALUES0)

    def unit_keys(self, u):
        return self.keys(u // HPG)

    def tensor_scores(self, pe, g, u, operands_ready=None):
        h, t = u % HPG, u // HPG
        n = self.keys(t)
        q_hi, q_lo, k_hi, k_lo = self.qk(g, h)
        q = slice(t * P, (t + 1) * P)
        if operands_ready is not None and u in (0, HPG // 2):
            operands_ready(pe, g, u // (HPG // 2))
        pe.wait_ge(self.shifted_ready, g * self.N + u + 1 + self.SHIFTED0 - HPG)
        ps = self.psS[h][:, 0:n]
        pe.matmul(ps, q_hi[:, q], k_hi[:, 0:n], start=True, stop=False)
        pe.matmul(ps, q_hi[:, q], k_lo[:, 0:n], start=False, stop=False)
        pe.matmul(ps, q_lo[:, q], k_hi[:, 0:n], start=False, stop=True).then_inc(self.scores_ready, 1)

    def leading(self, g, i, more):
        u = i + self.LEAD
        if u < self.N:
            return [(g, u)]
        if not more or i == self.N - 2:
            return []
        return [(g + 1, x) for x in ((u - self.N - 1, u - self.N) if i == self.N - 1 else (u - self.N,))]

    def values_at(self, i):
        return [t for t in range(TT) if min(HPG * t + HPG + 1, self.N - 1) == i]

    def tensor(self, pe, g, i, more, ident, operands_ready=None, v_ready=None):
        base = g * self.N
        h, t = i % HPG, i // HPG
        pe.wait_ge(self.probs_ready, base + i + 1)
        pe.wait_ge(self.probsT_copied, base + i - 1 + self.COPIED0)
        for c in range(self.keys(t) // P):
            ins = pe.transpose(self.psT[i % 2][:, c * P:(c + 1) * P],
                               self.shifted[:, i % self.BUFFERS, c * P:(c + 1) * P], ident[:, :])
        ins.then_inc(self.turned, 1)
        for unit in self.leading(g, i, more):
            self.tensor_scores(pe, *unit, operands_ready)
        for t in self.values_at(i):
            if t == 0 and v_ready is not None:
                pe.wait_ge(*v_ready(g))
            if t == 0 or not self.narrow:
                pe.wait_ge(self.out_copied, (g if self.narrow else g * TT + t - 1) + 1 - 1 + self.OUT0)
            pe.wait_ge(self.probsT_copied, base + HPG * t + HPG + self.COPIED0)
            chunks = self.keys(t) // P
            pairs = [(h, c) for c in range(chunks) for h in range(HPG)]
            for h, c in pairs if self.narrow else sorted(pairs):
                if self.narrow:
                    out = self.psO[0][h * self.width:(h + 1) * self.width, t * P:(t + 1) * P]
                else:
                    out = self.psO[t % 2][:, h * P:(h + 1) * P]
                ins = pe.matmul(out, self.v(g, h, c), self.probsT[:, t % 2, h, c, :], start=(c == 0), stop=(c == chunks - 1))
            ins.then_inc(self.values_done, 1)

    def vector_shift(self, dve, g, u, bias_ready=None):
        n = self.unit_keys(u)
        if bias_ready is not None and u < HPG:
            dve.wait_ge(*bias_ready(g, u))
        dve.wait_ge(self.scores_ready, g * self.N + u + 1)
        dve.wait_ge(self.turned, g * self.N + u - 7 + self.TURNED0)
        dve.sem_inc(self.begun, 1)
        dve.tensor_tensor_reduce(self.shifted[:, u % self.BUFFERS, 0:n], self.psS[u % HPG][:, 0:n],
                                 self.bias(u % HPG, u // HPG, n), 1.0, HUGE, ALU.add, ALU.min,
                                 self.least[:, u:u + 1]).then_inc(self.shifted_ready, 1)

    def vector_normalise(self, dve, g, u, step):
        n = self.unit_keys(u)
        dve.wait_ge(self.exps_done, g * self.N + u + 1)
        total, inv = self.row_sum[:, u:u + 1], self.row_inv[:, u:u + 1]
        if self.eps:
            step(dve.tensor_scalar(total, total, self.eps, None, ALU.add))
        step(dve.reciprocal(inv, total))
        p = self.shifted[:, u % self.BUFFERS, 0:n]
        dve.tensor_scalar(p, p, inv, None, ALU.mult).then_inc(self.probs_ready, 1)

    FIRST = 2

    def vector_first(self, dve, step, bias_ready=None):
        for u in range(self.LEAD):
            self.vector_shift(dve, 0, u, bias_ready)
            if 1 <= u <= self.FIRST:
                self.vector_normalise(dve, 0, u - 1, step)

    def vector(self, dve, g, i, more, step, bias_ready=None, between=None):
        for unit in self.leading(g, i, more):
            self.vector_shift(dve, *unit, bias_ready)
        if between is not None:
            between()
        for unit in self.leading(g, i - 1, more) if i > 0 else [(g, u) for u in range(self.FIRST, self.LEAD)]:
            self.vector_normalise(dve, *unit, step)

    @property
    def first_steps(self):
        return self.FIRST * (2 if self.eps else 1)

    @property
    def vector_steps(self):
        return self.N * (2 if self.eps else 1)

    def scalar_exp(self, act, g, u):
        n = self.unit_keys(u)
        act.wait_ge(self.shifted_ready, g * self.N + u + 1 + self.SHIFTED0)
        act.activation(self.shifted[:, u % self.BUFFERS, 0:n], self.shifted[:, u % self.BUFFERS, 0:n], ACT.Exp,
                       bias=self.least[:, u:u + 1], scale=-1.0,
                       accum_out=self.row_sum[:, u:u + 1]).then_inc(self.exps_done, 1)

    def scalar(self, act, g, i, more):
        h, t = i % HPG, i // HPG
        chunks = self.keys(t) // P
        act.wait_ge(self.turned, g * self.N + i + 1 + self.TURNED0)
        act.wait_ge(self.values_done, g * TT + t - 1 + self.VALUES0)
        act.activation(self.probsT[:, t % 2, h, 0:chunks, :],
                       self.psT[i % 2][:, 0:chunks * P].rearrange("p (c q) -> p c q", q=P), ACT.Copy)\
           .then_inc(self.probsT_copied, 1)
        for unit in self.leading(g, i, more):
            self.scalar_exp(act, *unit)
        for t in range(TT):
            if (t == TT - 1 or not self.narrow) and min(HPG * t + HPG + 2, self.N - 1) == i:
                act.wait_ge(self.values_done, g * TT + t + 1 + self.VALUES0)
                src = self.psO[t % self.banks][:, :]
                if not self.narrow:
                    src = src.rearrange("p (h q) -> p h q", h=HPG)
                act.activation(self.out(g, t), src, ACT.Copy).then_inc(self.out_copied, 1)


class Split:

    def __init__(self, m, keys):
        self.q, self.k = m.sb("q", [P, T]), m.sb("k", [P, keys])
        self.q_hi, self.q_lo = m.sb("q_hi", [P, T], F32R), m.sb("q_lo", [P, T], F32R)
        self.k_hi, self.k_lo = m.sb("k_hi", [P, keys], F32R), m.sb("k_lo", [P, keys], F32R)
        self.hi_ready, self.q_ready, self.k_ready = m.sem("hi_ready"), m.sem("q_split"), m.sem("k_split")
        self.begun = m.sem("split_begun")

    def head(self, g, h):
        rows = slice(h * DH, (h + 1) * DH)
        return self.q_hi[rows, :], self.q_lo[rows, :], self.k_hi[rows, :], self.k_lo[rows, :]

    def vector(self, dve, half, count):
        rows = slice(half * P // 2, (half + 1) * P // 2)
        dve.tensor_copy(self.q_hi[rows, :], self.q[rows, :])
        dve.tensor_copy(self.k_hi[rows, :], self.k[rows, :]).then_inc(self.hi_ready, 1)
        dve.wait_ge(self.hi_ready, count)
        dve.tensor_tensor(self.k_lo[rows, :], self.k[rows, :], self.k_hi[rows, :].bitcast(F32), ALU.subtract)\
           .then_inc(self.k_ready, 1)

    def gpsimd(self, pool, half, count):
        rows = slice(half * P // 2, (half + 1) * P // 2)
        pool.wait_ge(self.hi_ready, count)
        pool.sem_inc(self.begun, 1)
        pool.tensor_tensor(self.q_lo[rows, :], self.q[rows, :], self.q_hi[rows, :].bitcast(F32), ALU.subtract)\
            .then_inc(self.q_ready, 1)
        pool.wait_ge(self.q_ready, count)

    def wait(self, eng, count):
        wait(eng, self.k_ready, count)
        wait(eng, self.q_ready, count)



def phase_attention(nc, g, dram, name, kind, eps=0.0):
    strided = kind == "strided"
    keys = KEYS if strided else T
    VC = KEYS // P
    with ExitStack() as ctx:
        m = Memory(nc, ctx, name + "_")
        has_bias = name + "_bq" in dram
        w, enc = g["w_heads"], g.get("enc")
        split = Split(m, keys)
        if strided:
            kv = m.sb("kv", [P, 2, KEYS])
            v = m.sb("v", [P, HPG, VC, DH])
            group_bias = m.sb("group_bias", [P, HPG, KEYS])
            v_of = lambda g, h, c: v[:, h, c, :]
            bias = lambda h, t, n: group_bias[:, h, :]
        else:
            v_all = m.sb("v_all", [P, TT, D])
            v = m.sb("v", [P, TT, P])
            v_of = lambda g, h, c: v[:, c, h * DH:(h + 1) * DH]
            bias = lambda h, t, n: g["causal" if kind == "causal" else "mask"][:, t, 0:n]
        if has_bias:
            bq, bk, bv, bq_scaled = g["bq"], g["bk"], g["bv"], m.sb("bq_scaled", [P, GROUPS])
        core = Core(m, qk=split.head, v=v_of, bias=bias,
                    keys=(lambda t: (t + 1) * P) if kind == "causal" else (lambda t: keys),
                    width=DH, out=lambda j, t: g["oT"][:, ds(j, 1), :].squeeze(1), eps=eps)
        psP = m.ps("psP", [P, T])
        first_q, first_k, first_v = core.psT[1], core.psT[0], psP
        all_v = (core.psO[0], psP)
        q_loaded, k_loaded, bias_loaded, v_loaded = (g[n][name] for n in ("q_loaded", "k_loaded", "bias_loaded", "v_loaded"))
        (bias_scaled, q_ready, k_ready, v_ready, qk_copied, kv_copied, v_copied, v_all_copied, bias_copied,
         dve_step, begun) = (m.sem(n) for n in ("bias_scaled", "q_ready", "k_ready", "v_ready", "qk_copied", "kv_copied",
                                      "v_copied", "v_all_copied", "bias_copied", "dve_step", "pool_begun"))
        k_loads = 1 + (HPG if strided else 0)
        copies = 5 if strided else 2
        Q_AT, COPY_Q_AT, K_AT, COPY_K_AT, TURN_V_AT, V_AT = (1, 2, 3, 4), 4, (5, 6, 7, 8), 8, 10, 0
        SPLIT_AT = {9: 0, 12: 1}
        head_rows = lambda h: slice(h * DH, (h + 1) * DH)
        split_ready = lambda pe, j, half: split.wait(pe, 2 * j + half + 1)
        v_here = lambda j: (v_copied, j + 1)
        block = ctx.enter_context(nc.Block())

        def groups(eng, body):
            with eng.Fori(0, GROUPS - 1) as j:
                body(j, True)
            body(GROUPS - 1, False)

        @block.sync
        def _(sp):
            load_out(sp, g, dram, name)
            with sp.Fori(1, GROUPS) as j:
                load_heads(sp, g, dram, name, j, q_ready, k_ready)

        @block.tensor
        def _(pe):
            def project_q(j, part, bank=psP):
                if part == 0:
                    pe.wait_ge(q_loaded, 16 * j + 16)
                    wait(pe, v_copied, j if strided else 0)
                ins = pe.matmul(bank[:, :], w["q"][:, part, :], g["aT"][:, part, :], start=(part == 0), stop=(part == KC - 1))
                if part == KC - 1:
                    ins.then_inc(q_ready, 1)

            def project_k(j, part, bank=psP):
                if part == 0:
                    pe.wait_ge(k_loaded, 16 * k_loads * j + 16 * k_loads)
                    if bank is psP:
                        pe.wait_ge(qk_copied, copies * j + 1)
                if strided:
                    h, rows = part, slice(part // 2 * 2 * DH, (part // 2 * 2 + 2) * DH)
                    for i in range(KC):
                        ins = pe.matmul(bank[rows, (h % 2) * KEYS:(h % 2 + 1) * KEYS], w["kv"][:, i, h * 2 * DH:(h + 1) * 2 * DH],
                                        enc[:, h, i, :], start=(i == 0), stop=(i == KC - 1))
                else:
                    ins = pe.matmul(bank[:, :], w["k"][:, part, :], g["aT"][:, part, :], start=(part == 0), stop=(part == KC - 1))
                if part == HPG - 1:
                    ins.then_inc(k_ready, 1)

            def turn_values(j):
                pe.wait_ge(kv_copied, j + 1)
                pe.wait_ge(qk_copied, copies * j + copies)
                for half in range(2):
                    for c in range(VC):
                        ins = pe.transpose(psP[:, (half * VC + c) * P:(half * VC + c + 1) * P],
                                           kv[:, half, c * P:(c + 1) * P], g["ident"][:, :])
                ins.then_inc(v_ready, 1)

            def body(j, more):
                for i in range(core.N):
                    core.tensor(pe, j, i, more, g["ident"], operands_ready=split_ready, v_ready=v_here)
                    if more and i in Q_AT:
                        project_q(j + 1, Q_AT.index(i))
                    if more and i in K_AT:
                        project_k(j + 1, K_AT.index(i))
                    if more and strided and i == TURN_V_AT:
                        turn_values(j + 1)
            core.prime_tensor(pe)
            for part in range(KC):
                project_q(0, part, first_q)
            for part in range(KC):
                project_k(0, part, first_k)
            if strided:
                turn_values(0)
            else:
                pe.wait_ge(v_loaded, 16)
                for t in range(TT):
                    bank = all_v[t % 2]
                    wait(pe, v_all_copied, t - 1)
                    for i in range(KC):
                        ins = pe.matmul(bank[:, :], g["aT"][:, i, t * P:(t + 1) * P], w["v"][:, i, :],
                                        start=(i == 0), stop=(i == KC - 1))
                    ins.then_inc(v_ready, 1)
            for u in range(core.LEAD):
                core.tensor_scores(pe, 0, u, split_ready)
            groups(pe, body)

        @block.scalar
        def _(act):
            def copy_q(j, bank=psP):
                act.wait_ge(q_ready, j + 1)
                split.wait(act, 2 * j)
                if has_bias:
                    act.activation(split.q[:, :], bank[:, :], ACT.Identity, bias=bq_scaled[:, ds(j, 1)],
                                   scale=-DH ** -0.5).then_inc(qk_copied, 1)
                else:
                    act.activation(split.q[:, :], bank[:, :], ACT.Copy, scale=-DH ** -0.5).then_inc(qk_copied, 1)

            def copy_k(j, bank=psP):
                act.wait_ge(k_ready, j + 1)
                if strided:
                    wait(act, v_ready, j)
                    act.activation(kv[:, :, :].rearrange("p a k -> p (a k)"), bank[:, :], ACT.Copy).then_inc(kv_copied, 1)
                    for h in range(HPG):
                        rows = head_rows(h)
                        act.activation(split.k[rows, :], bank[rows, (h % 2) * KEYS:(h % 2 + 1) * KEYS], ACT.Identity,
                                       bias=bk[rows, ds(j, 1)]).then_inc(qk_copied, 1)
                elif has_bias:
                    act.activation(split.k[:, :], bank[:, 0:keys], ACT.Identity, bias=bk[:, ds(j, 1)]).then_inc(qk_copied, 1)
                else:
                    act.activation(split.k[:, :], bank[:, 0:keys], ACT.Copy).then_inc(qk_copied, 1)

            def body(j, more):
                for i in range(core.N):
                    core.scalar(act, j, i, more)
                    if more and i == COPY_Q_AT:
                        copy_q(j + 1)
                    if more and i == COPY_K_AT:
                        copy_k(j + 1)
            core.prime_scalar(act)
            if has_bias:
                act.wait_ge(bias_loaded, 48)
                act.activation(bq_scaled[:, :], bq[:, :], ACT.Copy, scale=-DH ** -0.5).then_inc(bias_scaled, 1)
                act.wait_ge(bias_scaled, 1)
            copy_q(0, first_q)
            copy_k(0, first_k)
            for u in range(core.LEAD):
                core.scalar_exp(act, 0, u)
            groups(act, body)

        @block.gpsimd
        def _(pool):
            def copy_bias(j, h):
                src = g["key_mask"][:, ds(j * (HPG * KEYS) + h * KEYS, KEYS)]
                pool.tensor_copy(group_bias[:, h, :], src).then_inc(bias_copied, 1)

            def body(j, more):
                if not strided:
                    wait(pool, v_all_copied, TT)
                    pool.wait_ge(core.values_done, j * TT + core.VALUES0)
                    pool.sem_inc(begun, 1)
                    pool.tensor_copy(v[:, :, :], v_all[:, :, ds(j * P, P)]).then_inc(v_copied, 1)
                    pool.wait_ge(v_copied, j + 1)
                for half in range(2 if more else 0):
                    split.gpsimd(pool, half, 2 * j + 2 + half + 1)
                    for h in (2 * half, 2 * half + 1) if strided else ():
                        pool.wait_ge(core.shifted_ready, j * core.N + core.N - HPG + h + 1 + core.SHIFTED0)
                        pool.sem_inc(begun, 1)
                        copy_bias(j + 1, h)
                    if strided:
                        pool.wait_ge(bias_copied, HPG * (j + 1) + 2 * half + 2)
            if strided:
                for h in range(HPG):
                    copy_bias(0, h)
                pool.wait_ge(bias_copied, HPG)
            split.gpsimd(pool, 0, 1)
            split.gpsimd(pool, 1, 2)
            groups(pool, body)

        @block.vector
        def _(dve):
            step = Steps(dve, dve_step)
            per = core.vector_steps
            bias_ready = (lambda j, h: (bias_copied, j * HPG + h + 1)) if strided else None

            def copy_v(j):
                if strided:
                    dve.wait_ge(v_ready, j + 1)
                    dve.wait_ge(core.values_done, j * TT + core.VALUES0)
                    turned = psP[:, :].rearrange("p (half c a two d) -> p half a c two d", half=2, c=VC, a=2, two=2)
                    bv_group = bv[:, ds(j * P, P)].rearrange("p (a half d) -> p half a d", half=2, a=2)
                    for half in range(2):
                        for c in range(VC):
                            ins = dve.tensor_tensor(v[:, half::2, c, :], turned[:, half, :, c, 1 - half, :],
                                                    bv_group[:, half, :, :], ALU.add)
                    ins.then_inc(v_copied, 1)

            def split_group(j, half):
                dve.wait_ge(qk_copied, copies * j + 2 * copies)
                split.vector(dve, half, 2 * j + 2 + half + 1)

            def body(j, more):
                step.n, step.k = core.first_steps + j * per, 0
                for i in range(core.N):
                    core.vector(dve, j, i, more, step, bias_ready, between=functools.partial(
                        split_group, j, SPLIT_AT[i]) if more and i in SPLIT_AT else None)
                    if i == V_AT:
                        copy_v(j)
                assert step.k == per or not more
            core.prime_vector(dve)
            if has_bias:
                dve.wait_ge(bias_loaded, 48)
            dve.wait_ge(qk_copied, copies)
            split.vector(dve, 0, 1)
            split.vector(dve, 1, 2)
            if not strided:
                for t in range(TT):
                    dve.wait_ge(v_ready, t + 1)
                    bank = all_v[t % 2]
                    if has_bias:
                        ins = dve.tensor_tensor(v_all[:, t, :], bank[:, :], bv[:, :], ALU.add)
                    else:
                        ins = dve.tensor_copy(v_all[:, t, :], bank[:, :])
                    ins.then_inc(v_all_copied, 1)
            core.vector_first(dve, step, bias_ready)
            groups(dve, body)



def project(pe, acc, oT, w, done, chunks):
    for t in range(TT):
        for c in range(chunks):
            ins = pe.matmul(acc[t][:, :], oT[:, c, t * P:(t + 1) * P], w[:, c, :], start=(c == 0), stop=(c == chunks - 1))
        ins.then_inc(done, 1)


def phase_project(nc, g, dram, name, prefetch):
    decoder = name != "attn"
    with ExitStack() as ctx:
        m = Memory(nc, ctx, name + "_out_")
        norm, turn = Norm(m), Turn(m)
        acc = [m.ps(f"acc{i}", [P, D]) for i in range(TT)]
        normed_x = m.sb("normed_x", [P, TT, D])
        names = "done dve_step pool_step normed begun".split()
        done, dve_step, pool_step, normed, begun = (m.sem(n) for n in names)
        w, loaded = g["w_out"], g["out_loaded"][name]
        block = ctx.enter_context(nc.Block())

        @block.sync
        def _(sp):
            prefetch(sp)

        @block.tensor
        def _(pe):
            pe.wait_ge(loaded, out_loads(name))
            lag = 3 if decoder else TT
            for t in range(TT + lag):
                if t < TT:
                    for c in range(KC):
                        ins = pe.matmul(acc[t][:, :], g["oT"][:, c, t * P:(t + 1) * P], w[:, c, :],
                                        start=(c == 0), stop=(c == KC - 1))
                    ins.then_inc(done, 1)
                if t >= lag:
                    pe.wait_ge(normed, t - lag + 1)
                    turn.tensor(pe, t - lag, normed_x, g["ident"])

        @block.scalar
        def _(act):
            act.wait_ge(loaded, out_loads(name))
            for t in range(TT + 1):
                if t < TT and decoder:
                    norm.scalar(act, [t])
                if t in (0, 2) and not decoder:
                    norm.scalar(act, HALVES[t // 2])
                    norm.scalar(act, HALVES[t // 2])
                if t >= 1:
                    turn.scalar(act, t - 1, g["aT"], g["gain_cols"], g["shift_cols"] if decoder else None)

        @block.vector
        def _(dve):
            step = Steps(dve, dve_step)
            into = g["a"] if decoder else g["x"]
            if decoder:
                dve.wait_ge(loaded, out_loads(name))
                step(dve.tensor_tensor(into[:, :, :], into[:, :, :], middle(g["bo"][:, :], TT), ALU.add))
            for tiles in [[t] for t in range(TT)] if decoder else HALVES:
                for t in tiles:
                    dve.wait_ge(done, t + 1)
                    ins = dve.tensor_tensor(into[:, t, :], into[:, t, :], acc[t][:, :], ALU.add)
                step(ins)
                norm.statistics(step, tiles, into, 1e-6 if decoder else 1e-5)
                if decoder:
                    for t in tiles:
                        norm.apply(dve, t, normed_x, into).then_inc(normed, 1)
                else:
                    for t in tiles:
                        ins = norm.apply(dve, t, g["a"], into)
                    step(ins)
                    norm.statistics(step, tiles, g["a"], 1e-5, rms=True)
                    for t in tiles:
                        norm.apply(dve, t, normed_x, g["a"], rms=True).then_inc(normed, 1)

        @block.gpsimd
        def _(pool):
            step = Steps(pool, pool_step)
            for t in range(TT if decoder else 0):
                pool.wait_ge(normed, t + 1)
                pool.sem_inc(begun, 1)
                step(pool.tensor_tensor(g["a"][:, t, :], normed_x[:, t, :], g["gain"][:, :], ALU.mult))
                step(pool.tensor_tensor(g["a"][:, t, :], g["a"][:, t, :], g["shift"][:, :], ALU.add))



HI, LO, SCALE, INV, BASE, SHIFT = range(6)
SCALE_STEPS = 8


def quantisation_extremes(dve, w, s):
    dve.tensor_reduce(s[:, HI, :], w, AXX, ALU.max)
    return dve.tensor_reduce(s[:, LO, :], w, AXX, ALU.min)


def quantisation_scales(step, s):
    dve = step.eng
    step(dve.tensor_tensor(s[:, SCALE, :], s[:, HI, :], s[:, LO, :], ALU.subtract))
    step(dve.tensor_scalar(s[:, SCALE, :], s[:, SCALE, :], 1e-5, 1.0 / 15.0, ALU.max, ALU.mult))
    step(dve.reciprocal(s[:, INV, :], s[:, SCALE, :]))
    step(dve.tensor_tensor(s[:, BASE, :], s[:, LO, :], s[:, INV, :], ALU.mult))
    step(dve.tensor_scalar(s[:, BASE, :], s[:, BASE, :], -1.0, ROUND, ALU.mult, ALU.add))
    step(dve.tensor_scalar(s[:, BASE, :], s[:, BASE, :], ROUND, 0.0, ALU.subtract, ALU.max))
    step(dve.tensor_scalar(s[:, BASE, :], s[:, BASE, :], 15.0, None, ALU.min))
    return dve.tensor_scalar(s[:, SHIFT, :], s[:, BASE, :], ROUND_UP, -1.0, ALU.add, ALU.mult)


def scale_groups(act, out, w, s, groups):
    for b in groups:
        ins = act.activation(out[:, b, :], w[:, b, :], ACT.Relu, bias=s[:, BASE, b:b + 1], scale=s[:, INV, b:b + 1])
    return ins


def round_groups(dve, w):
    return dve.tensor_scalar(w, w, 15.0, ROUND_UP, ALU.min, ALU.add)


def dequantise_groups(pool, w, s, groups):
    for b in groups:
        ins = pool.tensor_scalar(w[:, b, :], w[:, b, :], s[:, SHIFT, b:b + 1], s[:, SCALE, b:b + 1], ALU.add, ALU.mult)
    return ins



def load_mlp_tile(sp, g, dram, n, f, part):
    sp.dma_start(g["mlp_raw"][:, part, f, :], dram["w_mlp"][ds(n, 1), part, :, :].squeeze(0))\
      .then_inc(g["mlp_loaded"][2 * part + f], 16)


def load_attn_blocks(sp, g, dram, n, f):
    sp.dma_start(g["blocks"][:, f, :, :], dram["w_attn"][ds(n, 1), :, :].squeeze(0)
                 .rearrange("p (b k) -> p b k", b=ATTN_BLK)).then_inc(g["blocks_loaded"][f], 16)


def load_mlp(sp, g, dram):
    for n in range(2):
        load_mlp_tile(sp, g, dram, n, n, 0)
        load_mlp_tile(sp, g, dram, n, n, 1)
        load_attn_blocks(sp, g, dram, n, n)


def phase_mlp(nc, g, dram):
    N = FF // P
    UNITS = [range(i, min(i + T // P, ATTN_BLK)) for i in range(0, ATTN_BLK, T // P)]
    U = len(UNITS)
    with ExitStack() as ctx:
        m = Memory(nc, ctx, "mlp_")
        norm = Norm(m)
        b1 = m.sb("b1", [P, FF // P])
        rows = {k: m.sb(k, [P, D]) for k in ("b2", "gain", "shift")}
        aT_hi, aT_lo = (m.sb(n, [P, KC, T], F32R) for n in ("aT_hi", "aT_lo"))
        w_hi, w_lo = (m.sb(n, [P, 2, 2, T], F32R) for n in ("w_hi", "w_lo"))
        hT = m.sb("hT", [P, 2, T])
        hT_hi, hT_lo = (m.sb(n, [P, 2, T], F32R) for n in ("hT_hi", "hT_lo"))
        quantised = m.sb("quantised", [P, 2, ATTN_BLK, GS])
        scales = [m.sb(f"scales{i}", [P, 6, ATTN_BLK]) for i in range(2)]
        zero = m.sb("zero", [P, D])
        psH = [m.ps(f"psH{i}", [P, T]) for i in range(2)]
        acc = [m.ps(f"acc{i}", [P, D]) for i in range(TT)]
        turn = Turn(m)
        names = ("rows_loaded zeroed a_rounded a_split w1_hi_done w1_lo_done w2_hi_done w2_lo_done h_ready relu_done h_split "
                 "out_done closed scales_ready scaled rounded dequantised blocks_turned blocks_copied "
                 "dve_step begun finished").split()
        (rows_loaded, zeroed, a_rounded, a_split, w1_hi_done, w1_lo_done, w2_hi_done, w2_lo_done, h_ready, relu_done, h_split,
         out_done, closed, scales_ready, scaled, rounded, dequantised, blocks_turned, blocks_copied,
         dve_step, begun, finished) = (m.sem(n) for n in names)
        raw, blocks = g["mlp_raw"], g["blocks"]
        normed_x = raw[:, :, :, :].rearrange("p a b k -> p (a b) k")
        block = ctx.enter_context(nc.Block())

        def live(n):
            return not isinstance(n, int) or 0 <= n < N

        def steps(eng, each):
            for n in range(-1, 4):
                each(n, n % 2)
            with eng.Fori(2, N // 2 - 1) as i:
                for f in range(2):
                    each(2 * i + f, f)
            for n in range(N - 2, N + 3):
                each(n, n % 2)

        @block.sync
        def _(sp):
            sp.dma_start(b1[:, :], dram["ffn_b1"]).then_inc(rows_loaded, 16)
            for k, name in (("b2", "ffn_b2"), ("gain", "ln3_g"), ("shift", "ln3_b")):
                sp.dma_start(rows[k][:, :], row(dram[name])).then_inc(rows_loaded, 16)
            load_heads(sp, g, dram, "attn", 0)

            def each(n, f):
                if live(n - 1) and live(n + 1):
                    wait(sp, w2_lo_done, n)
                    load_mlp_tile(sp, g, dram, n + 1, 1 - f, 1)
                if live(n) and live(n + 2):
                    wait(sp, w1_lo_done, n + 1)
                    load_mlp_tile(sp, g, dram, n + 2, f, 0)
                if live(n - 1) and live(n + 1):
                    wait(sp, scaled, n)
                    load_attn_blocks(sp, g, dram, n + 1, 1 - f)
            steps(sp, each)

        @block.gpsimd
        def _(pool):
            pool.memset(zero[:, :], 0.0).then_inc(zeroed, 1)

            def each(n, f):
                if live(n - 2):
                    pool.wait_ge(rounded, n - 1)
                    pool.sem_inc(begun, 1)
                    dequantise_groups(pool, quantised[:, f, :, :], scales[f], range(ATTN_BLK)).then_inc(dequantised, 1)
                if live(n):
                    pool.wait_ge(relu_done, n + 1)
                    wait(pool, out_done, n - 1)
                    pool.sem_inc(begun, 1)
                    pool.tensor_tensor(hT_lo[:, f, :], hT[:, f, :], hT_hi[:, f, :].bitcast(F32), ALU.subtract)\
                        .then_inc(h_split, 1)
            steps(pool, each)

        @block.tensor
        def _(pe):
            pe.wait_ge(zeroed, 1)
            for t in range(TT):
                pe.matmul(acc[t][:, :], zero[:, 0:P], zero[:, :], start=True, stop=False, skip_group_check=True)

            def each(n, f):
                if live(n - 3):
                    pe.wait_ge(dequantised, n - 2)
                    wait(pe, blocks_copied, U * (n - 3))
                    for u, unit in enumerate(UNITS):
                        for c, b in enumerate(unit):
                            ins = pe.transpose(turn.banks[u][:, c * P:(c + 1) * P], quantised[:, 1 - f, b, :],
                                               g["ident"][:, :])
                        ins.then_inc(blocks_turned, 1)
                if live(n):
                    pe.wait_ge(w1_lo_done, n + 1)
                    wait(pe, relu_done, n - 1)
                    for c in range(KC):
                        if isinstance(n, int) and n == 0:
                            pe.wait_ge(a_split, c + 1)
                        hi, lo = (w[:, 0, f, c * P:(c + 1) * P] for w in (w_hi, w_lo))
                        pe.matmul(psH[f][:, :], hi, aT_hi[:, c, :], start=(c == 0), stop=False)
                        pe.matmul(psH[f][:, :], hi, aT_lo[:, c, :], start=False, stop=False)
                        ins = pe.matmul(psH[f][:, :], lo, aT_hi[:, c, :], start=False, stop=(c == KC - 1))
                    ins.then_inc(h_ready, 1)
                if live(n - 1):
                    pe.wait_ge(h_split, n)
                    pe.wait_ge(w2_lo_done, n)
                    b_hi, b_lo = w_hi[:, 1, 1 - f, :], w_lo[:, 1, 1 - f, :]
                    for t in range(TT):
                        hi, lo = (h[:, 1 - f, t * P:(t + 1) * P] for h in (hT_hi, hT_lo))
                        for a, b in ((hi, b_hi), (hi, b_lo), (lo, b_hi)):
                            ins = pe.matmul(acc[t][:, :], a, b, start=False, stop=False, skip_group_check=True)
                    ins.then_inc(out_done, 1)
                    if isinstance(n, int) and n == N:
                        for t in range(TT):
                            ins = pe.matmul(acc[t][:, :], zero[:, 0:P], zero[:, :], start=False, stop=True,
                                            skip_group_check=True)
                        ins.then_inc(closed, 1)
            steps(pe, each)
            pe.wait_ge(blocks_copied, U * N)
            for t in range(TT):
                pe.wait_ge(finished, t + 1)
                turn.tensor(pe, t, g["a"], g["ident"])

        @block.scalar
        def _(act):
            def split_hi(n, f, part, done):
                act.wait_ge(g["mlp_loaded"][2 * part + f], 8 * (n - f) + 16)
                act.activation(w_hi[:, part, f, :], raw[:, part, f, :], ACT.Copy).then_inc(done, 1)

            def each(n, f):
                if live(n - 3):
                    for u, unit in enumerate(UNITS):
                        act.wait_ge(blocks_turned, U * (n - 3) + u + 1)
                        act.activation(g["wT"][:, ds((n - 3) * (ATTN_BLK * P) + unit[0] * P, len(unit) * P)],
                                       turn.banks[u][:, 0:len(unit) * P], ACT.Copy).then_inc(blocks_copied, 1)
                if live(n + 1):
                    wait(act, h_ready, n)
                    split_hi(n + 1, 1 - f, 0, w1_hi_done)
                if live(n):
                    wait(act, out_done, n - 1)
                    split_hi(n, f, 1, w2_hi_done)
                if live(n - 1):
                    act.wait_ge(scales_ready, n)
                    scale_groups(act, quantised[:, 1 - f, :, :], blocks[:, 1 - f, :, :], scales[1 - f], range(ATTN_BLK))\
                        .then_inc(scaled, 1)
                if live(n):
                    if isinstance(n, int) and n == 0:
                        act.wait_ge(rows_loaded, 64)
                    act.wait_ge(h_ready, n + 1)
                    wait(act, h_split, n - 1)
                    wait(act, out_done, n - 1)
                    bias = b1[:, ds(n, 1)]
                    act.activation(hT_hi[:, f, :], psH[f][:, :], ACT.Relu, bias=bias)
                    act.activation(hT[:, f, :], psH[f][:, :], ACT.Relu, bias=bias).then_inc(relu_done, 1)
            steps(act, each)
            for tiles in HALVES:
                norm.scalar(act, tiles)
                norm.scalar(act, tiles)
            for t in range(TT):
                turn.scalar(act, t, g["aT"])

        @block.vector
        def _(dve):
            step = Steps(dve, dve_step)
            for c in range(KC):
                dve.tensor_copy(aT_hi[:, c, :], g["aT"][:, c, :]).then_inc(a_rounded, 1)
            for c in range(KC):
                dve.wait_ge(a_rounded, c + 1)
                dve.tensor_tensor(aT_lo[:, c, :], g["aT"][:, c, :], aT_hi[:, c, :].bitcast(F32), ALU.subtract)\
                   .then_inc(a_split, 1)
            first_scales = step.n

            def split_lo(n, f, part, hi_done, done):
                dve.wait_ge(hi_done, n + 1)
                dve.tensor_tensor(w_lo[:, part, f, :], raw[:, part, f, :], w_hi[:, part, f, :].bitcast(F32),
                                  ALU.subtract).then_inc(done, 1)

            def each(n, f):
                if live(n - 2):
                    dve.wait_ge(scaled, n - 1)
                    round_groups(dve, quantised[:, f, :, :]).then_inc(rounded, 1)
                if live(n + 1):
                    split_lo(n + 1, 1 - f, 0, w1_hi_done, w1_lo_done)
                if live(n):
                    split_lo(n, f, 1, w2_hi_done, w2_lo_done)
                    dve.wait_ge(g["blocks_loaded"][f], 8 * (n - f) + 16)
                    step.n, step.k = first_scales + n * SCALE_STEPS, 0
                    step(quantisation_extremes(dve, blocks[:, f, :, :], scales[f]))
                    wait(dve, dequantised, n - 1)
                    quantisation_scales(step, scales[f]).then_inc(scales_ready, 1)
                    assert step.k == SCALE_STEPS
                if isinstance(n, int) and 0 <= n < TT:
                    dve.wait_ge(rows_loaded, 64)
                    dve.tensor_tensor(g["a"][:, n, :], g["a"][:, n, :], rows["b2"][:, :], ALU.add)
                    dve.tensor_tensor(g["x"][:, n, :], g["x"][:, n, :], rows["shift"][:, :], ALU.add)
            steps(dve, each)
            step.n = first_scales + N * SCALE_STEPS
            dve.wait_ge(closed, 1)
            for tiles in HALVES:
                for t in tiles:
                    ins = dve.tensor_tensor(g["a"][:, t, :], g["a"][:, t, :], acc[t][:, :], ALU.add)
                step(ins)
                norm.statistics(step, tiles, g["a"], 1e-6)
                for t in tiles:
                    ins = dve.scalar_tensor_tensor(normed_x[:, t, :], g["a"][:, t, :], norm.mean(t), rows["gain"][:, :],
                                                   ALU.subtract, ALU.mult)
                step(ins)
                for t in tiles:
                    ins = dve.scalar_tensor_tensor(g["x"][:, t, :], normed_x[:, t, :], norm.inverse(t), g["x"][:, t, :],
                                                   ALU.mult, ALU.add)
                step(ins)
                norm.statistics(step, tiles, g["x"], 1e-5)
                for t in tiles:
                    norm.apply(dve, t, g["a"], g["x"]).then_inc(finished, 1)



def quantise(step, w, small):
    dve = step.eng
    hi, lo, scale, inv, base = (small[:, i, :] for i in range(5))
    dve.tensor_reduce(hi, w, AXX, ALU.max)
    step(dve.tensor_reduce(lo, w, AXX, ALU.min))
    step(dve.tensor_tensor(scale, hi, lo, ALU.subtract))
    step(dve.tensor_scalar(scale, scale, 1e-5, 1.0 / 15.0, ALU.max, ALU.mult))
    step(dve.reciprocal(inv, scale))
    step(dve.tensor_tensor(base, lo, inv, ALU.mult))
    step(dve.tensor_scalar(base, base, -1.0, ROUND, ALU.mult, ALU.add))
    step(dve.tensor_scalar(base, base, ROUND, 0.0, ALU.subtract, ALU.max))
    step(dve.tensor_scalar(base, base, 15.0, None, ALU.min))
    step(dve.tensor_tensor(w, w, last(inv, GS), ALU.mult))
    step(dve.tensor_scalar(w, w, ROUND, None, ALU.add))
    step(dve.scalar_tensor_tensor(w, w, ROUND, last(base, GS), ALU.subtract, ALU.add))
    step(dve.tensor_scalar(w, w, 0.0, 15.0, ALU.max, ALU.min))
    step(dve.tensor_tensor(w, w, last(base, GS), ALU.subtract))
    step(dve.tensor_tensor(w, w, last(scale, GS), ALU.mult))


def quantise(step, w, small):
    dve = step.eng
    hi, lo, scale, inv, base = (small[:, i, :] for i in range(5))
    dve.tensor_reduce(hi, w, AXX, ALU.max)
    step(dve.tensor_reduce(lo, w, AXX, ALU.min))
    step(dve.tensor_tensor(scale, hi, lo, ALU.subtract))
    step(dve.tensor_scalar(scale, scale, 1e-5, 1.0 / 15.0, ALU.max, ALU.mult))
    step(dve.reciprocal(inv, scale))
    step(dve.tensor_tensor(base, lo, inv, ALU.mult))
    step(dve.tensor_scalar(base, base, -1.0, ROUND, ALU.mult, ALU.add))
    step(dve.tensor_scalar(base, base, ROUND, 0.0, ALU.subtract, ALU.max))
    step(dve.tensor_scalar(base, base, 15.0, None, ALU.min))
    step(dve.tensor_tensor(w, w, last(inv, GS), ALU.mult))
    step(dve.tensor_scalar(w, w, ROUND, None, ALU.add))
    step(dve.scalar_tensor_tensor(w, w, ROUND, last(base, GS), ALU.subtract, ALU.add))
    step(dve.tensor_scalar(w, w, 0.0, 15.0, ALU.max, ALU.min))
    step(dve.tensor_tensor(w, w, last(base, GS), ALU.subtract))
    step(dve.tensor_tensor(w, w, last(scale, GS), ALU.mult))



def phase_qkv(nc, g, dram):
    rows = QKV_TILES * P
    with ExitStack() as ctx:
        m = Memory(nc, ctx, "qkv_")
        q = m.sb("q", [P, TT, QH * HD])
        small = m.sb("small", [P, 5, TT * 2 * KVH])
        part = m.sb("part", [P, 2, QH * HD])
        rope = {k: m.sb(k, [P, TT, HD // 2]) for k in ("cos_q", "sin_q", "cos_k", "sin_k")}
        ps = [m.ps(f"ps{i}", [P, T]) for i in range(8)]
        loaded, ready, q_copied, kv_copied = (m.sem(n) for n in ("loaded", "ready", "q_copied", "kv_copied"))
        dve_step, rotated, turned, copied = m.sem("dve_step"), m.sem("rotated"), m.sem("turned"), m.sem("copied")
        lo_copied = m.sem("lo_copied")
        hi_of = lambda h: g["q_hi"][:, h, :] if h < QH else g["k_hi"][:, h - QH, :]
        lo_of = lambda h: g["q_lo"][:, h, :] if h < QH else g["k_lo"][:, h - QH, :]
        HEAD_ORDER = [*range(QH, QH + KVH), *range(QH)]
        kv_flat = g["kv"][:, :, :, :].rearrange("p t h d -> p (t h) d")
        block = ctx.enter_context(nc.Block())

        @block.sync
        def _(sp):
            for k, tile in rope.items():
                sp.dma_start(tile[:, :, :], dram[k].rearrange("(t p) d -> p t d", p=P)).then_inc(loaded, 16)

        @block.tensor
        def _(pe):
            for n in range(3 * TT):
                t, col = (n, 2 * T) if n < TT else ((n - TT) // 2, (n - TT) % 2 * T)
                if n >= 8:
                    pe.wait_ge(kv_copied, n - 7)
                for c in range(KC):
                    ins = pe.matmul(ps[n % 8][:, :], g["aT"][:, c, t * P:(t + 1) * P],
                                    g["wT"][:, c * rows + col:c * rows + col + T], start=(c == 0), stop=(c == KC - 1))
                ins.then_inc(ready, 1)
            for i, h in enumerate(HEAD_ORDER):
                pe.wait_ge(rotated, 1 if h >= QH else 2)
                pe.wait_ge(q_copied, 2 * TT)
                wait(pe, lo_copied, i - 1)
                for t in range(TT):
                    src = q[:, t, h * HD:(h + 1) * HD] if h < QH else g["kv"][:, t, h - QH, :]
                    ins = pe.transpose(ps[i % 2][:, t * P:(t + 1) * P], src, g["ident"][:, :])
                ins.then_inc(turned, 1)

        @block.scalar
        def _(act):
            for n in range(3 * TT):
                act.wait_ge(ready, n + 1)
                if n < TT:
                    act.activation(g["kv"][:, n, :, :].rearrange("p h d -> p (h d)"), ps[n][:, :], ACT.Copy).then_inc(kv_copied, 1)
                else:
                    t, half = (n - TT) // 2, (n - TT) % 2
                    act.activation(q[:, t, half * T:(half + 1) * T], ps[n % 8][:, :], ACT.Copy).then_inc(q_copied, 1)
            for i, h in enumerate(HEAD_ORDER):
                act.wait_ge(turned, i + 1)
                act.activation(hi_of(h), ps[i % 2][:, :], ACT.Copy).then_inc(copied, 1)

        def rotate(step, x, cos, sin, heads):
            dve = step.eng
            halves = x.rearrange("p (n d) -> p n d", d=HD // 2)
            pc, psn = (part[:, i, 0:heads * HD].rearrange("p (n d) -> p n d", d=HD // 2) for i in range(2))
            dve.tensor_tensor(pc, halves, middle(cos, 2 * heads), ALU.mult)
            step(dve.tensor_tensor(psn, halves, middle(sin, 2 * heads), ALU.mult))
            xs, cs, ss = (y.rearrange("p (h two) d -> p h two d", two=2) for y in (halves, pc, psn))
            dve.tensor_tensor(xs[:, :, 0, :], cs[:, :, 0, :], ss[:, :, 1, :], ALU.subtract)
            step(dve.tensor_tensor(xs[:, :, 1, :], cs[:, :, 1, :], ss[:, :, 0, :], ALU.add))

        @block.vector
        def _(dve):
            step = Steps(dve, dve_step)
            dve.wait_ge(loaded, 64)
            dve.wait_ge(kv_copied, 4)
            quantise(step, kv_flat, small)
            for t in range(TT):
                k = g["kv"][:, t, 0:KVH, :].rearrange("p h d -> p (h d)")
                rotate(step, k, rope["cos_k"][:, t, :], rope["sin_k"][:, t, :], KVH)
            dve.sem_inc(rotated, 1)
            for t in range(TT):
                dve.wait_ge(q_copied, 2 * t + 2)
                rotate(step, q[:, t, :], rope["cos_q"][:, t, :], rope["sin_q"][:, t, :], QH)
            dve.sem_inc(rotated, 1)
            for i, h in enumerate(HEAD_ORDER):
                dve.wait_ge(copied, i + 1)
                dve.tensor_tensor(lo_of(h), ps[i % 2][:, :], hi_of(h).bitcast(F32), ALU.subtract).then_inc(lo_copied, 1)


def phase_gqa_attention(nc, g):
    with ExitStack() as ctx:
        m = Memory(nc, ctx, "gqa_")
        shared = lambda j, h: (HPG * j + h) // (QH // KVH)
        core = Core(
            m, qk=lambda j, h: (g["q_hi"][:, HPG * j + h, :], g["q_lo"][:, HPG * j + h, :],
                                g["k_hi"][:, shared(j, h), :], g["k_lo"][:, shared(j, h), :]),
            v=lambda j, h, c: g["kv"][:, c, KVH + shared(j, h), :],
            bias=lambda h, t, n: g["causal"][:, t, 0:n],
            keys=lambda t: (t + 1) * P, width=HD,
            out=lambda j, t: g["oT"][:, HPG * j:HPG * (j + 1), t * P:(t + 1) * P], eps=0.0)
        dve_step = m.sem("dve_step")
        block = ctx.enter_context(nc.Block())
        groups = [(j, j < QH // HPG - 1) for j in range(QH // HPG)]

        @block.tensor
        def _(pe):
            core.prime_tensor(pe)
            for u in range(core.LEAD):
                core.tensor_scores(pe, 0, u)
            for j, more in groups:
                for i in range(core.N):
                    core.tensor(pe, j, i, more, g["ident"])

        @block.scalar
        def _(act):
            core.prime_scalar(act)
            for u in range(core.LEAD):
                core.scalar_exp(act, 0, u)
            for j, more in groups:
                for i in range(core.N):
                    core.scalar(act, j, i, more)

        @block.vector
        def _(dve):
            core.prime_vector(dve)
            step = Steps(dve, dve_step)
            core.vector_first(dve, step)
            for j, more in groups:
                for i in range(core.N):
                    core.vector(dve, j, i, more, step)



def phase_router(nc, g, dram):
    chunks = QH * HD // P
    with ExitStack() as ctx:
        m = Memory(nc, ctx, "router_")
        norm, turn = Norm(m), Turn(m)
        hn = m.sb("hn", [P, TT, D])
        gain_cols, wg = m.sb("gain_cols", [P, KC]), m.sb("wg", [P, KC, E])
        earlier = m.sb("earlier", [P, E, E])
        logits, e, picked, rw = (m.sb(n, [P, TT, E]) for n in ("logits", "exps", "picked", "rw"))
        above, level = (m.sb(n, [P, TT, E, E]) for n in ("above", "level"))
        col = m.sb("col", [P, 3, TT])
        rwT_hi, rwT_lo = m.sb("rwT_hi", [E, T], F32R), m.sb("rwT_lo", [E, T], F32R)
        pick = m.sb("pick", [E, E, P], F32R)
        acc = [m.ps(f"acc{i}", [P, D]) for i in range(TT)]
        psL, psR = m.ps("psL", [P, TT, E]), m.ps("psR", [P, T])
        names = ("loaded done dve_step pool_step begun normed ones tri logits_ready shifted exps_ready "
                 "rw_ready rwT_ready rwT_copied spread spread_copied").split()
        (loaded, done, dve_step, pool_step, begun, normed, ones, tri, logits_ready, shifted, exps_ready,
         rw_ready, rwT_ready, rwT_copied, spread, spread_copied) = (m.sem(n) for n in names)
        block = ctx.enter_context(nc.Block())

        @block.sync
        def _(sp):
            sp.dma_start(gain_cols[:, :], dram["g2_cols"]).then_inc(loaded, 16)
            sp.dma_start(wg[:, :, :], dram["w_gate"]).then_inc(loaded, 16)

        @block.gpsimd
        def _(pool):
            pool.memset(earlier[:, :, :], 1.0).then_inc(ones, 1)
            pool.wait_ge(ones, 1)
            pool.affine_select(out=earlier[:, :, :], in_=earlier[:, :, :], compare_op=ALU.is_gt, fill=0.0,
                               base=0, pattern=[[1, E], [-1, E]], channel_multiplier=0).then_inc(tri, 1)
            for t in range(TT):
                pool.wait_ge(normed, t + 1)
                pool.sem_inc(begun, 1)
                pool.tensor_tensor(g["x"][:, t, :], g["x"][:, t, :], g["a"][:, t, :], ALU.add)

        @block.tensor
        def _(pe):
            wo = g["wT"][:, QKV_TILES * KC * P:].rearrange("p (c n) -> p c n", n=D)
            for t in range(TT + 1):
                if t < TT:
                    for c in range(chunks):
                        ins = pe.matmul(acc[t][:, :], g["oT"][:, c, t * P:(t + 1) * P], wo[:, c, :],
                                        start=(c == 0), stop=(c == chunks - 1))
                    ins.then_inc(done, 1)
                if t >= 1:
                    pe.wait_ge(normed, t)
                    turn.tensor(pe, t - 1, hn, g["ident"])
            pe.wait_ge(loaded, 32)
            pe.wait_ge(turn.copied, TT)
            for t in range(TT):
                for c in range(KC):
                    ins = pe.matmul(psL[:, t, :], g["aT"][:, c, t * P:(t + 1) * P], wg[:, c, :],
                                    start=(c == 0), stop=(c == KC - 1))
            ins.then_inc(logits_ready, 1)
            pe.wait_ge(rw_ready, 1)
            for t in range(TT):
                ins = pe.transpose(psR[0:E, t * P:(t + 1) * P], rw[:, t, :], g["ident"][:, :])
            ins.then_inc(rwT_ready, 1)
            pe.wait_ge(rwT_copied, 1)
            for x in range(E):
                wait(pe, spread_copied, x - 1)
                pe.matmul(turn.banks[x % 2][:, :], pick[:, x, :], rwT_hi[:, :], start=True, stop=False)
                pe.matmul(turn.banks[x % 2][:, :], pick[:, x, :], rwT_lo[:, :], start=False, stop=True).then_inc(spread, 1)

        @block.scalar
        def _(act):
            act.wait_ge(loaded, 32)
            for t in range(TT + 1):
                if t < TT:
                    norm.scalar(act, [t])
                if t >= 1:
                    turn.scalar(act, t - 1, g["aT"], gain_cols)
            act.wait_ge(shifted, 1)
            act.activation(e[:, :, :], e[:, :, :], ACT.Exp).then_inc(exps_ready, 1)
            for x in range(E):
                act.wait_ge(spread, x + 1)
                act.activation(g["rw"][:, x, :], turn.banks[x % 2][:, :], ACT.Copy).then_inc(spread_copied, 1)

        @block.vector
        def _(dve):
            step = Steps(dve, dve_step)
            for x in range(E):
                dve.tensor_copy(pick[:, x, :], g["ident"][0:E, x:x + 1].broadcast_to([E, P]))
            for t in range(TT):
                dve.wait_ge(done, t + 1)
                step(dve.tensor_tensor(g["a"][:, t, :], g["a"][:, t, :], acc[t][:, :], ALU.add))
                norm.vector(step, t, hn, g["a"], 1e-5, rms=True).then_inc(normed, 1)
            dve.wait_ge(turn.copied, TT)
            step(dve.tensor_copy(g["hn_hi"][:, :, :], g["aT"][:, :, :]))
            dve.tensor_tensor(g["hn_lo"][:, :, :], g["aT"][:, :, :], g["hn_hi"][:, :, :].bitcast(F32), ALU.subtract)
            dve.wait_ge(logits_ready, 1)
            step(dve.tensor_copy(logits[:, :, :], psL[:, :, :]))
            step(dve.tensor_reduce(col[:, 0, :], logits[:, :, :], AXX, ALU.max))
            step(dve.tensor_tensor(e[:, :, :], logits[:, :, :], last(col[:, 0, :], E), ALU.subtract))
            dve.sem_inc(shifted, 1)
            mine = last(logits[:, :, :], E)
            other = logits[:, :, :].unsqueeze(2).broadcast_to([P, TT, E, E])
            dve.tensor_tensor(above[:, :, :, :], other, mine, ALU.is_gt)
            step(dve.tensor_tensor(level[:, :, :, :], other, mine, ALU.is_equal))
            dve.wait_ge(tri, 1)
            step(dve.tensor_tensor(level[:, :, :, :], level[:, :, :, :],
                                   earlier[:, :, :].unsqueeze(1).broadcast_to([P, TT, E, E]), ALU.mult))
            step(dve.tensor_tensor(above[:, :, :, :], above[:, :, :, :], level[:, :, :, :], ALU.add))
            step(dve.tensor_reduce(picked[:, :, :], above[:, :, :, :], AXX, ALU.add))
            step(dve.tensor_scalar(picked[:, :, :], picked[:, :, :], 1.5, None, ALU.is_lt))
            dve.wait_ge(exps_ready, 1)
            step(dve.tensor_tensor(picked[:, :, :], picked[:, :, :], e[:, :, :], ALU.mult))
            step(dve.tensor_reduce(col[:, 1, :], picked[:, :, :], AXX, ALU.add))
            step(dve.reciprocal(col[:, 2, :], col[:, 1, :]))
            dve.tensor_tensor(rw[:, :, :], picked[:, :, :], last(col[:, 2, :], E), ALU.mult).then_inc(rw_ready, 1)
            dve.wait_ge(rwT_ready, 1)
            step(dve.tensor_copy(rwT_hi[:, :], psR[0:E, :]))
            dve.tensor_tensor(rwT_lo[:, :], psR[0:E, :], rwT_hi[:, :].bitcast(F32), ALU.subtract).then_inc(rwT_copied, 1)



def phase_experts(nc, g, dram, out):
    N = E * FT
    UNIT = T
    with ExitStack() as ctx:
        m = Memory(nc, ctx, "moe_")
        raw = [m.sb(f"raw{i}", [P, BLK, GS]) for i in range(4)]
        deq = [m.sb(f"deq{i}", [P, BLK, GS]) for i in range(2)]
        scales = [m.sb(f"scales{i}", [P, 6, BLK]) for i in range(4)]
        wT_hi = [m.sb(f"wT_hi{i}", [P, 3, UNIT], F32R) for i in range(2)]
        wT_lo = [m.sb(f"wT_lo{i}", [P, 3, UNIT], F32R) for i in range(2)]
        silu, gate, up = (m.sb(n, [P, 2, T]) for n in ("silu", "gate", "up"))
        up_hi, up_lo = (m.sb(n, [P, 2, T], F32R) for n in ("up_hi", "up_lo"))
        zero = m.sb("zero", [P, D])
        psH1, psH3 = m.ps("psH1", [P, T]), m.ps("psH3", [P, T])
        psT = [m.ps(f"psT{i}", [P, T]) for i in range(2)]
        acc = [m.ps(f"acc{i}", [P, D]) for i in range(TT)]
        loaded = [m.sem(f"loaded{i}") for i in range(4)]
        names = ("scales_ready scaled rounded dequantised turned hi_copied lo_copied h_ready silu_done "
                 "gate_done up_done up_hi_done up_lo_done out_done closed added stored dve_step zeroed begun").split()
        (scales_ready, scaled, rounded, dequantised, turned, hi_copied, lo_copied, h_ready, silu_done,
         gate_done, up_done, up_hi_done, up_lo_done, out_done, closed, added, stored, dve_step, zeroed, begun) = (m.sem(n) for n in names)
        block = ctx.enter_context(nc.Block())

        def live(n):
            return not isinstance(n, int) or 0 <= n < N

        def steps(eng, each):
            for n in range(-4, 4):
                each(n, n % 4)
            with eng.Fori(1, N // 4 - 1) as i:
                for j in range(4):
                    each(4 * i + j, j)
            for n in range(N - 4, N + 1):
                each(n, n % 4)

        @block.sync
        def _(sp):
            def each(n, j):
                if live(n + 4):
                    wait(sp, scaled, 3 * n + 3)
                    sp.dma_start(raw[j][:, :, :], dram["w_moe"][ds(n + 4, 1), :, :].squeeze(0)
                                 .rearrange("p (b k) -> p b k", b=BLK)).then_inc(loaded[j], 16)
            steps(sp, each)
            for t in range(TT):
                sp.wait_ge(added, t + 1)
                sp.dma_start(out[t * P:(t + 1) * P, :], g["x"][:, t, :]).then_inc(stored, 16)
            sp.wait_ge(stored, 16 * TT)

        @block.vector
        def _(dve):
            step = Steps(dve, dve_step)

            def scales_of(n, j):
                s = scales[j]
                dve.wait_ge(loaded[j], 4 * (n - j) + 16)
                step.n, step.k = n * SCALE_STEPS, 0
                step(quantisation_extremes(dve, raw[j][:, :, :], s))
                quantisation_scales(step, s).then_inc(scales_ready, 1)
                assert step.k == SCALE_STEPS

            def round_unit(n, j, r):
                dve.wait_ge(scaled, 3 * n + r + 1)
                round_groups(dve, deq[j % 2][:, 4 * r:4 * r + 4, :]).then_inc(rounded, 1)

            def lo_unit(n, j, r):
                dve.wait_ge(hi_copied, 3 * n + r + 1)
                dve.tensor_tensor(wT_lo[j % 2][:, r, :], psT[(3 * j + r) % 2][:, :],
                                  wT_hi[j % 2][:, r, :].bitcast(F32), ALU.subtract).then_inc(lo_copied, 1)

            def each(n, j):
                j1, j2, j3 = (j + 1) % 4, (j + 2) % 4, (j + 3) % 4
                if live(n):
                    lo_unit(n, j, 2)
                if live(n + 3):
                    scales_of(n + 3, j3)
                if live(n + 2):
                    round_unit(n + 2, j2, 0)
                if live(n + 1):
                    lo_unit(n + 1, j1, 0)
                if live(n):
                    dve.wait_ge(h_ready, 2 * n + 2)
                    wait(dve, up_done, n - 1)
                    dve.tensor_tensor(gate[:, j % 2, :], psH3[:, :], rw_row(g, n), ALU.mult).then_inc(gate_done, 1)
                if live(n + 2):
                    round_unit(n + 2, j2, 1)
                    round_unit(n + 2, j2, 2)
                if live(n + 1):
                    lo_unit(n + 1, j1, 1)
                if live(n):
                    dve.wait_ge(up_done, n + 1)
                    wait(dve, out_done, n - 1)
                    dve.tensor_copy(up_hi[:, j % 2, :], up[:, j % 2, :]).then_inc(up_hi_done, 1)
            steps(dve, each)
            for t in range(TT):
                dve.wait_ge(closed, t + 1)
                dve.tensor_tensor(g["x"][:, t, :], g["x"][:, t, :], acc[t][:, :], ALU.add).then_inc(added, 1)

        @block.scalar
        def _(act):
            def scale_blocks(n, j, r):
                if r == 0:
                    act.wait_ge(scales_ready, n + 1)
                wait(act, turned, 3 * (n - 2) + r + 1)
                scale_groups(act, deq[j % 2], raw[j], scales[j], range(4 * r, 4 * r + 4)).then_inc(scaled, 1)

            def hi_unit(n, j, r):
                act.wait_ge(turned, 3 * n + r + 1)
                act.activation(wT_hi[j % 2][:, r, :], psT[(3 * j + r) % 2][:, :], ACT.Copy).then_inc(hi_copied, 1)

            def each(n, j):
                j1, j2 = (j + 1) % 4, (j + 2) % 4
                if live(n):
                    hi_unit(n, j, 2)
                if live(n + 2):
                    scale_blocks(n + 2, j2, 0)
                if live(n):
                    act.wait_ge(h_ready, 2 * n + 1)
                    wait(act, up_done, n - 1)
                    act.activation(silu[:, j % 2, :], psH1[:, :], ACT.Silu).then_inc(silu_done, 1)
                if live(n + 1):
                    hi_unit(n + 1, j1, 0)
                if live(n + 2):
                    scale_blocks(n + 2, j2, 1)
                    scale_blocks(n + 2, j2, 2)
                if live(n + 1):
                    hi_unit(n + 1, j1, 1)
            steps(act, each)

        @block.gpsimd
        def _(pool):
            pool.memset(zero[:, :], 0.0).then_inc(zeroed, 1)

            def dequantise(n, j, r):
                pool.wait_ge(rounded, 3 * n + r + 1)
                pool.sem_inc(begun, 1)
                dequantise_groups(pool, deq[j % 2], scales[j], range(4 * r, 4 * r + 4)).then_inc(dequantised, 1)

            def each(n, j):
                if live(n):
                    pool.wait_ge(silu_done, n + 1)
                    pool.wait_ge(gate_done, n + 1)
                    wait(pool, up_lo_done, n - 1)
                    pool.tensor_tensor(up[:, j % 2, :], silu[:, j % 2, :], gate[:, j % 2, :], ALU.mult)\
                        .then_inc(up_done, 1)
                if live(n + 2):
                    dequantise(n + 2, (j + 2) % 4, 0)
                if live(n):
                    pool.wait_ge(up_hi_done, n + 1)
                    pool.tensor_tensor(up_lo[:, j % 2, :], up[:, j % 2, :], up_hi[:, j % 2, :].bitcast(F32),
                                       ALU.subtract).then_inc(up_lo_done, 1)
                if live(n + 2):
                    dequantise(n + 2, (j + 2) % 4, 1)
                    dequantise(n + 2, (j + 2) % 4, 2)
            steps(pool, each)

        @block.tensor
        def _(pe):
            pe.wait_ge(zeroed, 1)
            for t in range(TT):
                pe.matmul(acc[t][:, :], zero[:, 0:P], zero[:, :], start=True, stop=False, skip_group_check=True)

            def hidden(n, j, r, ps):
                pe.wait_ge(lo_copied, 3 * n + r + 1)
                wait(pe, silu_done if r == 0 else gate_done, n)
                hi, lo = wT_hi[j % 2], wT_lo[j % 2]
                for c in range(KC):
                    col = slice(c * P, (c + 1) * P)
                    pe.matmul(ps[:, :], hi[:, r, col], g["hn_hi"][:, c, :], start=(c == 0), stop=False)
                    pe.matmul(ps[:, :], hi[:, r, col], g["hn_lo"][:, c, :], start=False, stop=False)
                    ins = pe.matmul(ps[:, :], lo[:, r, col], g["hn_hi"][:, c, :], start=False, stop=(c == KC - 1))
                ins.then_inc(h_ready, 1)

            def turn_unit(n, j, r):
                pe.wait_ge(dequantised, 3 * n + r + 1)
                wait(pe, lo_copied, 3 * n + r - 1)
                for c in range(4):
                    ins = pe.transpose(psT[(3 * j + r) % 2][:, c * P:(c + 1) * P], deq[j % 2][:, 4 * r + c, :],
                                       g["ident"][:, :])
                ins.then_inc(turned, 1)

            def output(n, j):
                pe.wait_ge(lo_copied, 3 * n + 3)
                pe.wait_ge(up_lo_done, n + 1)
                w_hi, w_lo = wT_hi[j % 2][:, 2, :], wT_lo[j % 2][:, 2, :]
                for t in range(TT):
                    hi, lo = (u[:, j % 2, t * P:(t + 1) * P] for u in (up_hi, up_lo))
                    for a, b in ((hi, w_hi), (hi, w_lo), (lo, w_hi)):
                        ins = pe.matmul(acc[t][:, :], a, b, start=False, stop=False, skip_group_check=True)
                ins.then_inc(out_done, 1)

            def each(n, j):
                j1 = (j + 1) % 4
                if live(n):
                    hidden(n, j, 0, psH1)
                if live(n + 1):
                    turn_unit(n + 1, j1, 0)
                if live(n):
                    hidden(n, j, 1, psH3)
                if live(n + 1):
                    turn_unit(n + 1, j1, 1)
                if live(n - 1):
                    output(n - 1, (j - 1) % 4)
                if live(n + 1):
                    turn_unit(n + 1, j1, 2)
            steps(pe, each)
            for t in range(TT):
                ins = pe.matmul(acc[t][:, :], zero[:, 0:P], zero[:, :], start=False, stop=True, skip_group_check=True)
                ins.then_inc(closed, 1)


def rw_row(g, n):
    e = n // FT
    return g["rw"][:, e, :] if isinstance(e, int) else g["rw"][:, ds(e, 1), :].squeeze(1)


def program(nc, dram, out):
    with ExitStack() as ctx:
        m = Memory(nc, ctx)
        g = {"x": m.sb("x", [P, TT, D]), "a": m.sb("a", [P, TT, D]), "aT": m.sb("aT", [P, KC, T]),
             "ident": m.sb("ident", [P, P]), "causal": m.sb("causal", [P, TT, T])}
        g["hn_hi"], g["hn_lo"] = m.sb("hn_hi", [P, KC, T], F32R), m.sb("hn_lo", [P, KC, T], F32R)
        g["rw"] = m.sb("rw", [P, E, T])
        g["oT"] = g["rw"][:, 0:KC, :]
        with ExitStack() as late:
            ml = Memory(nc, late)
            g["wT"] = ml.sb("wT", [P, (QKV_TILES * KC + KC * QH) * P])
            g["enc"] = g["wT"][:, 0:HPG * KC * KEYS].rearrange("p (h c n) -> p h c n", h=HPG, c=KC)
            g["key_mask"] = g["wT"][:, HPG * KC * KEYS:][:, 0:HEADS * KEYS]
            g["mask"] = g["wT"][:, (HPG * KC + HEADS) * KEYS:].rearrange("p (t k) -> p t k", k=T)
            with ExitStack() as early:
                me = Memory(nc, early)
                g["w_heads"] = {"q": me.sb("w_q", [P, KC, P]), "k": me.sb("w_k", [P, KC, P]), "v": me.sb("w_v", [P, KC, D])}
                g["w_heads"]["kv"] = g["w_heads"]["v"][:, :, 0:2 * P]
                g["bq"], g["bk"], g["bv"] = me.sb("bq", [P, GROUPS]), me.sb("bk", [P, GROUPS]), me.sb("bv", [P, D])
                g["w_out"] = me.sb("w_out", [P, KC, D])
                for n in ("bo", "gain", "shift"):
                    g[n] = me.sb(n, [P, D])
                g["gain_cols"], g["shift_cols"] = me.sb("gain_cols", [P, KC]), me.sb("shift_cols", [P, KC])
                g["mlp_raw"], g["blocks"] = me.sb("mlp_raw", [P, 2, 2, T]), me.sb("blocks", [P, 2, ATTN_BLK, GS])
                for kind in ("q_loaded", "k_loaded", "v_loaded", "bias_loaded", "out_loaded"):
                    g[kind] = {n: me.sem(f"{n}_{kind}") for n in ("sa", "ca", "attn")}
                g["mlp_loaded"] = [me.sem(f"mlp_loaded{i}") for i in range(4)]
                g["blocks_loaded"] = [me.sem(f"blocks_loaded{i}") for i in range(2)]
                phase_start(nc, g, dram)
                phase_attention(nc, g, dram, "sa", "masked")
                phase_project(nc, g, dram, "sa", lambda sp: load_heads(sp, g, dram, "ca", 0))
                phase_attention(nc, g, dram, "ca", "strided")
                phase_project(nc, g, dram, "ca", lambda sp: load_mlp(sp, g, dram))
                phase_mlp(nc, g, dram)
                phase_attention(nc, g, dram, "attn", "causal", eps=1e-8)
                phase_project(nc, g, dram, "attn", lambda sp: None)
            g["kv"] = ml.sb("kv", [P, TT, 2 * KVH, HD])
            g["q_hi"], g["q_lo"] = ml.sb("q_hi", [P, QH, T], F32R), ml.sb("q_lo", [P, QH, T], F32R)
            g["k_hi"], g["k_lo"] = ml.sb("k_hi", [P, KVH, T], F32R), ml.sb("k_lo", [P, KVH, T], F32R)
            g["oT"] = ml.sb("gqa_oT", [P, QH, T])
            phase_qkv(nc, g, dram)
            phase_gqa_attention(nc, g)
            phase_router(nc, g, dram)
        phase_experts(nc, g, dram, out)


def lay_out(i):
    import numpy as np
    xa, at = "L0_xattn_", "L0_attn_"
    c = np.ascontiguousarray
    out = {"x": c(i["x"][0]), "mask": c(i["mask_Bx1xSxS_ik0"][0, 0])}
    out["key_mask"] = c(i["mask_Bx1x1xS2_if1"][0, 0, 0, :HEADS * KEYS].reshape(KEYS, HEADS).T).reshape(-1)
    out["enc"] = c(i["ctx_1024"][0, :HEADS * KEYS].reshape(KEYS, HEADS, D).transpose(1, 2, 0))
    for n in ("sa_wq", "sa_bq", "sa_wk", "sa_bk", "sa_wv", "sa_bv", "sa_wo", "sa_bo",
              "ca_wq", "ca_bq", "ca_bk", "ca_bv", "ca_wo", "ca_bo",
              "ffn_b1", "ffn_b2", "ln1_g", "ln1_b", "ln2_g", "ln2_b", "ln3_g", "ln3_b"):
        out[n] = c(i[xa + n])
    for n in ("sa_bq", "sa_bk", "ca_bq", "ca_bk", "ffn_b1"):
        out[n] = c(out[n].reshape(-1, P).T)
    wk, wv = (i[xa + n].reshape(D, HEADS, DH) for n in ("ca_wk", "ca_wv"))
    out["ca_wkv"] = np.concatenate([part[:, h] for h in range(HEADS) for part in ((wk, wv), (wv, wk))[h % 2]], axis=1)
    for n in ("ln1_g", "ln1_b", "ln2_g", "ln2_b"):
        out[n + "_cols"] = c(out[n].reshape(-1, P).T)
    w1 = i[xa + "ffn_w1"].reshape(KC, P, FF // P, P).transpose(2, 1, 0, 3).reshape(-1, 1, P, KC * P)
    out["w_mlp"] = np.concatenate([w1, i[xa + "ffn_w2"].reshape(-1, 1, P, D)], axis=1)
    out["attn_wq"], out["attn_wo"] = c(i[at + "Wq"].T), c(i[at + "Wo"].T)
    out["attn_wk"], out["attn_wv"] = c(i[at + "Wkv"][:D].T), c(i[at + "Wkv"][D:].T)
    f = "L0_ffn_"
    out["g1_cols"], out["g2_cols"] = (c(i[f + n].reshape(-1, P).T) for n in ("g1", "g2"))
    qkv = np.concatenate([i[f + "w_q"], i[f + "w_k"], i[f + "w_v"]]).reshape(QKV_TILES, P, KC, GS)
    wo = i[f + "w_o"].reshape(KC, P, QH, GS)
    blocks = np.concatenate([w.transpose(2, 0, 1, 3).reshape(-1, P, GS) for w in (qkv, wo)])
    out["w_attn"] = c(blocks.reshape(-1, ATTN_BLK, P, GS).transpose(0, 2, 1, 3)).reshape(-1, P, ATTN_BLK * GS)
    out["w_gate"] = c(i[f + "w_gate"].T.reshape(KC, P, E).transpose(1, 0, 2))
    w1, w3 = (i[f + w].reshape(E * FT, P, KC * GS) for w in ("w1", "w3"))
    w2 = i[f + "w2"].reshape(E, KC, P, FT, GS).transpose(0, 3, 2, 1, 4).reshape(E * FT, P, KC * GS)
    out["w_moe"] = np.concatenate([w1, w3, w2], axis=2)
    inv = (1.0 / np.float32(1e6) ** (np.arange(0, HD, 2, dtype=np.float32) / np.float32(HD))).astype(np.float32)
    angle = np.arange(T, dtype=np.float32)[:, None] * inv[None, :]
    out["cos_k"], out["sin_k"] = np.cos(angle), np.sin(angle)
    scale = np.float32(-(HD ** -0.5))
    out["cos_q"], out["sin_q"] = out["cos_k"] * scale, out["sin_k"] * scale
    return out



def kernel(**inputs):
    import numpy as np
    import concourse.bacc as bacc
    from concourse.bass_utils import run_bass_kernel_spmd

    arrays = {f"{n}_dram": a for n, a in lay_out({k: np.asarray(v) for k, v in inputs.items()}).items()}
    nc = bacc.Bacc("TRN2", target_bir_lowering=False, num_devices=1)
    dram = {n[:-5]: nc.dram_tensor(n, a.shape, mybir.dt.from_np(a.dtype), kind="ExternalInput").ap()
            for n, a in arrays.items()}
    out = nc.dram_tensor("out_dram", (T, D), F32, kind="ExternalOutput").ap()
    program(nc, dram, out)
    result = run_bass_kernel_spmd(nc, [arrays], core_ids=[0])
    return result.results[0]["out_dram"].reshape(1, T, D)
```
